# Optimizing a Trainium2 kernel written in Bass

```python
import numpy as np
import jax
import jax.numpy as jnp

def _softmax(x, axis=-1):
    return jax.nn.softmax(x, axis=axis)

def _gelu(x):
    return jax.nn.gelu(x, approximate=True)

def _silu(x):
    return jax.nn.silu(x)

def _sigmoid(x):
    return jax.nn.sigmoid(x)

def _layernorm(x, axis=-1, eps=1e-05):
    m = jnp.mean(x, axis=axis, keepdims=True)
    v = jnp.var(x, axis=axis, keepdims=True)
    return (x - m) / jnp.sqrt(v + eps)

def _scatter_add(tgt, idx, src, axis=0):
    return tgt.at[idx].add(src)

def _segment_sum(src, seg, n):
    return jax.ops.segment_sum(src, seg, n)
kernel_name = 'mk_recurrent_d1_jaxref_r8_cecce7'

def setup_inputs(seed: int=0):
    np.random.seed(seed)
    _w = jnp.asarray

    def _L0_attn_setup():
        import jax, jax.numpy as jnp
        import numpy as np
        HIDDEN = 128
        EXPAND = 2
        D_REC = HIDDEN * EXPAND
        INTER = 512
        B, T = (4, 512)

        def _rmsnorm(x, w, eps=1e-06):
            var = jnp.mean(x * x, axis=-1, keepdims=True)
            return x * jax.lax.rsqrt(var + eps) * w

        def _hawk_scan(x_in, a):
            xs = jnp.moveaxis(x_in, 1, 0)
            As = jnp.moveaxis(a, 1, 0)

            def step(state, inp):
                a_t, x_t = inp
                new = a_t * state + jnp.sqrt(1.0 - a_t * a_t + 1e-08) * x_t
                return (new, new)
            init = jnp.zeros(x_in.shape[::2], dtype=x_in.dtype)
            _, ys = jax.lax.scan(step, init, (As, xs))
            return jnp.moveaxis(ys, 0, 1)
        key = jax.random.key(seed)
        ks = jax.random.split(key, 11)
        s = lambda fan: 1.0 / np.sqrt(fan)
        return {'x': jax.random.normal(ks[0], (B, T, HIDDEN), dtype=jnp.float32), 'ln1_w': jnp.ones((HIDDEN,), dtype=jnp.float32), 'ln2_w': jnp.ones((HIDDEN,), dtype=jnp.float32), 'w_in': jax.random.normal(ks[1], (D_REC, HIDDEN), dtype=jnp.float32) * s(HIDDEN), 'w_gate': jax.random.normal(ks[2], (D_REC, HIDDEN), dtype=jnp.float32) * s(HIDDEN), 'a_param': jax.random.normal(ks[3], (D_REC,), dtype=jnp.float32) * 0.1, 'w_a': jax.random.normal(ks[4], (D_REC, D_REC), dtype=jnp.float32) * s(D_REC), 'w_out': jax.random.normal(ks[5], (HIDDEN, D_REC), dtype=jnp.float32) * s(D_REC), 'w_mlp_gate': jax.random.normal(ks[6], (INTER, HIDDEN), dtype=jnp.float32) * s(HIDDEN), 'w_mlp_up': jax.random.normal(ks[7], (INTER, HIDDEN), dtype=jnp.float32) * s(HIDDEN), 'w_mlp_down': jax.random.normal(ks[8], (HIDDEN, INTER), dtype=jnp.float32) * s(INTER)}
    _L0_attn_in = _L0_attn_setup()

    def _L0_ffn_setup():
        import jax, jax.numpy as jnp
        import numpy as np
        B, S = (4, 64)
        H = 128
        I = 352
        E = 8
        K = 2
        IS = 176
        key = jax.random.key(seed)
        ks = jax.random.split(key, 8)

        def init(k, shape, fan_in):
            return (jax.random.normal(k, shape, jnp.float32) / np.sqrt(fan_in)).astype(jnp.float32)
        return {'hidden_states': jax.random.normal(ks[0], (B, S, H), jnp.float32), 'gate_w': init(ks[1], (H, E), H), 'Wg': init(ks[2], (E, H, I), H), 'Wu': init(ks[3], (E, H, I), H), 'Wd': init(ks[4], (E, I, H), I), 'Sg': init(ks[5], (H, IS), H), 'Su': init(ks[6], (H, IS), H), 'Sd': init(ks[7], (IS, H), IS)}
    _L0_ffn_in = _L0_ffn_setup()
    _d = {'L0_attn_x': _L0_attn_in['x'], 'L0_attn_ln1_w': _L0_attn_in['ln1_w'], 'L0_attn_ln2_w': _L0_attn_in['ln2_w'], 'L0_attn_w_in': _L0_attn_in['w_in'], 'L0_attn_w_gate': _L0_attn_in['w_gate'], 'L0_attn_a_param': _L0_attn_in['a_param'], 'L0_attn_w_a': _L0_attn_in['w_a'], 'L0_attn_w_out': _L0_attn_in['w_out'], 'L0_attn_w_mlp_gate': _L0_attn_in['w_mlp_gate'], 'L0_attn_w_mlp_up': _L0_attn_in['w_mlp_up'], 'L0_attn_w_mlp_down': _L0_attn_in['w_mlp_down'], 'L0_ffn_gate_w': _L0_ffn_in['gate_w'], 'L0_ffn_Wg': _L0_ffn_in['Wg'], 'L0_ffn_Wu': _L0_ffn_in['Wu'], 'L0_ffn_Wd': _L0_ffn_in['Wd'], 'L0_ffn_Sg': _L0_ffn_in['Sg'], 'L0_ffn_Su': _L0_ffn_in['Su'], 'L0_ffn_Sd': _L0_ffn_in['Sd']}
    _x0 = _d['L0_attn_x']
    _d['L0_attn_x'] = jax.random.normal(jax.random.fold_in(jax.random.key(seed), 1), (4, 1024, 128), dtype=_x0.dtype)
    del _x0
    return _d

def reference(L0_attn_x, L0_attn_ln1_w, L0_attn_ln2_w, L0_attn_w_in, L0_attn_w_gate, L0_attn_a_param, L0_attn_w_a, L0_attn_w_out, L0_attn_w_mlp_gate, L0_attn_w_mlp_up, L0_attn_w_mlp_down, L0_ffn_gate_w, L0_ffn_Wg, L0_ffn_Wu, L0_ffn_Wd, L0_ffn_Sg, L0_ffn_Su, L0_ffn_Sd):

    def _L0_attn_ref(x, ln1_w, ln2_w, w_in, w_gate, a_param, w_a, w_out, w_mlp_gate, w_mlp_up, w_mlp_down):
        import jax, jax.numpy as jnp
        import numpy as np
        HIDDEN = 128
        EXPAND = 2
        D_REC = HIDDEN * EXPAND
        INTER = 512
        B, T = (4, 512)

        def _rmsnorm(x, w, eps=1e-06):
            var = jnp.mean(x * x, axis=-1, keepdims=True)
            return x * jax.lax.rsqrt(var + eps) * w

        def _hawk_scan(x_in, a):
            xs = jnp.moveaxis(x_in, 1, 0)
            As = jnp.moveaxis(a, 1, 0)

            def step(state, inp):
                a_t, x_t = inp
                new = a_t * state + jnp.sqrt(1.0 - a_t * a_t + 1e-08) * x_t
                return (new, new)
            init = jnp.zeros(x_in.shape[::2], dtype=x_in.dtype)
            _, ys = jax.lax.scan(step, init, (As, xs))
            return jnp.moveaxis(ys, 0, 1)
        h = _rmsnorm(x, ln1_w)
        x_in = h @ w_in.T
        gate = jax.nn.sigmoid(h @ w_gate.T)
        a = jax.nn.sigmoid(a_param + x_in @ w_a.T)
        y = gate * _hawk_scan(x_in, a)
        x = x + y @ w_out.T
        h2 = _rmsnorm(x, ln2_w)
        mlp = jax.nn.silu(h2 @ w_mlp_gate.T) * (h2 @ w_mlp_up.T) @ w_mlp_down.T
        return x + mlp

    def _L0_ffn_ref(hidden_states, gate_w, Wg, Wu, Wd, Sg, Su, Sd):
        import jax, jax.numpy as jnp
        import numpy as np
        B, S = (4, 64)
        H = 128
        I = 352
        E = 8
        K = 2
        IS = 176
        b, s, h = hidden_states.shape
        x = hidden_states.reshape(-1, h)
        T = x.shape[0]
        logits = x @ gate_w
        top_v, top_i = jax.lax.top_k(logits, K)
        top_p = jax.nn.softmax(top_v, axis=-1)
        combine = jnp.zeros((T, E), x.dtype).at[jnp.arange(T)[:, None], top_i].add(top_p)
        g = jnp.einsum('th,ehi->tei', x, Wg)
        u = jnp.einsum('th,ehi->tei', x, Wu)
        d = jnp.einsum('tei,eih->teh', jax.nn.silu(g) * u, Wd)
        expert_out = jnp.einsum('te,teh->th', combine, d)
        shared = jax.nn.silu(x @ Sg) * (x @ Su) @ Sd
        return (expert_out + shared).reshape(b, s, h)
    x = L0_attn_x
    xn = _layernorm(x, axis=-1)
    s = _L0_attn_ref(xn, L0_attn_ln1_w, L0_attn_ln2_w, L0_attn_w_in, L0_attn_w_gate, L0_attn_a_param, L0_attn_w_a, L0_attn_w_out, L0_attn_w_mlp_gate, L0_attn_w_mlp_up, L0_attn_w_mlp_down)
    g = _silu(_L0_ffn_ref(xn, L0_ffn_gate_w, L0_ffn_Wg, L0_ffn_Wu, L0_ffn_Wd, L0_ffn_Sg, L0_ffn_Su, L0_ffn_Sd))
    x = x + s * g
    return x

_drawn_inputs = setup_inputs


def setup_inputs(seed=0):
    import zlib

    import numpy as np

    out = dict(_drawn_inputs(seed))
    spreads = {'L0_attn_ln1_w': (1.0, 0.2), 'L0_attn_ln2_w': (1.0, 0.2)}
    factors = {'L0_attn_a_param': 8.0}
    for name, (base, spread) in spreads.items():
        noise = np.random.default_rng([zlib.crc32(name.encode()), seed]).standard_normal(out[name].shape)
        drawn = base * np.exp(spread * noise) if base else spread * noise
        out[name] = jnp.asarray(drawn.astype(out[name].dtype))
    for name, factor in factors.items():
        out[name] = (out[name] * factor).astype(out[name].dtype)
    return out
```

```python
from contextlib import ExitStack

import concourse.bass as bass
from concourse import mybir

F32 = mybir.dt.float32
F32R = mybir.dt.float32r
I32 = mybir.dt.int32
ALU = mybir.AluOpType
ACT = mybir.ActivationFunctionType
AX = mybir.AxisListType

P = 128


def gated_recurrent_moe_kernel(
    nc: bass.Bass,
    x: bass.AP,
    ln1_w: bass.AP,
    ln2_w: bass.AP,
    w_in: bass.AP,
    w_gate: bass.AP,
    a_param: bass.AP,
    w_a: bass.AP,
    w_out: bass.AP,
    w_mlp_gate: bass.AP,
    w_mlp_up: bass.AP,
    w_mlp_down: bass.AP,
    gate_w: bass.AP,
    Wg: bass.AP,
    Wu: bass.AP,
    Wd: bass.AP,
    Sg: bass.AP,
    Su: bass.AP,
    Sd: bass.AP,
    out: bass.AP,
):
    BATCH, T, H = x.shape
    REC = w_in.shape[0]
    INTER = w_mlp_gate.shape[0]
    E, _, I = Wg.shape
    IS = Sg.shape[1]
    TOK = BATCH * T
    NT = TOK // P
    BT = 4
    BLK = BT * P
    NB = TOK // BLK
    RC = REC // P
    IC = INTER // P
    EC = -(-I // P)
    SC = -(-IS // P)
    TILES = 2 * TOK // P + E - 1
    TILES += TILES % 2
    SLOTS = TILES * P
    HALF = NB // 2
    BIG = 3.0e38
    ZW = RC * BLK
    assert SLOTS % ZW == 0
    ROOM = 2 * NT * E + TILES * E + NT * (P + 6)
    assert H == P and T % BLK == 0 and T // BLK == 2 and IC == 4 and RC == 2 and SC == 2

    xt = x.rearrange("b (t p) d -> p (b t) d", p=P)
    ot = out.rearrange("b (t p) d -> p (b t) d", p=P)
    slots = nc.dram_tensor("slots", (SLOTS, P), F32, kind="Internal").ap()
    moved = nc.dram_tensor("moved", (SLOTS, P), F32, kind="Internal").ap()

    with ExitStack() as ctx:

        def sb(name, shape, dt=F32):
            return ctx.enter_context(nc.sbuf_tensor(name, shape, dt))

        def sem(name):
            return ctx.enter_context(nc.semaphore(name))

        pair = [ctx.enter_context(nc.psum_tensor(f"pair{i}", [P, 2, 512], F32)) for i in range(3)]
        turned = ctx.enter_context(nc.psum_tensor("turned", [P, 512], F32))
        bytok = ctx.enter_context(nc.psum_tensor("bytok", [P, 512], F32))

        xn = sb("xn", [P, NT, P])
        ident = sb("ident", [P, P])
        below = sb("below", [P, P])
        ones = sb("ones", [P, P])
        keep = sb("keep", [P, NB + 1])
        tiny = sb("tiny", [P, 3])

        raw_router = sb("raw_router", [P, E])
        ln1 = sb("ln1", [P, 1])
        ln2 = sb("ln2", [P, 1])
        ap_sb = sb("ap_sb", [P, RC])
        ap_half = sb("ap_half", [P, RC])
        NREC = 3 * RC
        w_hi = sb("w_hi", [P, NREC + 2 * IC, P], F32R)
        w_lo = sb("w_lo", [P, NREC + 2 * IC, P], F32R)
        wout_t = sb("wout_t", [P, RC, P])
        wdown_t = sb("wdown_t", [P, IC, P])
        sh_hi = sb("sh_hi", [P, 2, SC * P], F32R)
        sh_lo = sb("sh_lo", [P, 2, SC * P], F32R)
        sd_sb = sb("sd_sb", [P, SC, P])
        rt_w = sb("rt_w", [P, 2 * E], F32R)
        up_hi = sb("up_hi", [P, E, 2 * I], F32R)
        up_lo = sb("up_lo", [P, E, 2 * I], F32R)
        wd_sb = sb("wd_sb", [P, E, EC * P])

        mv = sb("mv", [P, NT, 2])
        std = sb("std", [P, NT])
        rstd = sb("rstd", [P, NT])
        msq = sb("msq", [P, NT])
        rms1 = sb("rms1", [P, NT])
        r1 = sb("r1", [P, NT])
        part_hi = sb("part_hi", [P, BLK], F32R)
        part_lo = sb("part_lo", [P, BLK], F32R)

        m1 = sb("m1", [P, NT])
        m2 = sb("m2", [P, NT])
        best = sb("best", [P, NT])
        gap = sb("gap", [P, NT])
        egap = sb("egap", [P, NT])
        esum = sb("esum", [P, NT])
        p1 = sb("p1", [P, NT])
        p2 = sb("p2", [P, NT])
        total = sb("total", [P, E])
        total_i = sb("total_i", [P, E], I32)
        tiles_i = sb("tiles_i", [P, E], I32)
        tiles = sb("tiles", [P, E])
        tiles_to = sb("tiles_to", [P, E])
        tiles_from = sb("tiles_from", [P, E])
        slot_f = sb("slot_f", [P, 2, NT])
        slot_i = sb("slot_i", [P, 2, NT], I32)
        expert_f = sb("expert_f", [P, TILES])
        expert_i = sb("expert_i", [P, TILES], I32)

        h_tok = sb("h_tok", [P, BT, P])
        hT_hi = sb("hT_hi", [P, BLK], F32R)
        hT_lo = sb("hT_lo", [P, BLK], F32R)
        rec_room = sb("rec_room", [P, 3 * RC * BLK])
        x_in, t_gate, t_decay = (
            rec_room[:, n * RC * BLK : (n + 1) * RC * BLK].rearrange("p (c t) -> p c t", c=RC) for n in range(3)
        )
        act_room = sb("act_room", [P, (2 + IC + SC) * BLK])
        silu_b, mlp_act, sh_act = (
            act_room[:, a * BLK : b * BLK].rearrange("p (c t) -> p c t", t=BLK)
            for a, b in ((0, 2), (2, 2 + IC), (2 + IC, 2 + IC + SC))
        )
        decay = sb("decay", [P, RC, BLK])
        state = sb("state", [P, RC, BLK])
        square = rest = root = t_decay
        feed = x_in
        y = t_gate
        zeros = state[:, :, :].rearrange("p a b -> p (a b)")
        carry = sb("carry", [P, RC])
        results = sb("results", [P, 2 * NT * P])
        s_tok = results[:, 0 : NT * P].rearrange("p (t d) -> p t d", d=P)
        shared = results[:, NT * P :].rearrange("p (t d) -> p t d", d=P)
        raw_up = results[:, 0 : E * 2 * I].rearrange("p (e i) -> p e i", e=E)
        ssq = sb("ssq", [P, BT])
        rms2 = sb("rms2", [P, BT])
        r2 = sb("r2", [P, BT])
        h2_tok = sb("h2_tok", [P, BT, P])
        squares = h2_tok
        h2_hi = sb("h2_hi", [P, BLK], F32R)
        h2_lo = sb("h2_lo", [P, BLK], F32R)

        x_tile = sh_act[:, :, :].rearrange("p a b -> p (a b)")[:, 0 : 4 * P].rearrange("p (k d) -> p k d", d=P)
        xe_hi = h2_hi[:, 0 : 2 * P].rearrange("p (k d) -> p k d", d=P)
        xe_lo = h2_lo[:, 0 : 2 * P].rearrange("p (k d) -> p k d", d=P)
        mlp_flat = mlp_act[:, :, :].rearrange("p a b -> p (a b)")
        silu_e = mlp_flat[:, 0 : 2 * I].rearrange("p (k d) -> p k d", k=2)
        actT = mlp_flat[:, 2 * I : 2 * I + 2 * EC * P].rearrange("p (k d) -> p k d", k=2)
        y_tile = mlp_flat[:, 2 * I + 2 * EC * P : 2 * I + (2 * EC + 4) * P].rearrange("p (k d) -> p k d", d=P)
        act_e = sb("act_e", [P, 2, EC * P])

        def carve(base, at, shape):
            size = 1
            for n in shape[1:]:
                size *= n
            flat = base[:, at[0] : at[0] + size]
            at[0] += size
            assert at[0] <= base.shape[1]
            if len(shape) == 2:
                return flat
            if len(shape) == 3:
                return flat.rearrange("p (a b) -> p a b", b=shape[2])
            assert len(shape) == 5
            return flat.rearrange("p (a b c d) -> p a b c d", b=shape[2], c=shape[3], d=shape[4])

        rec_raw = [0]
        raw_rec = carve(rec_room, rec_raw, [P, 2 * RC, P])
        raw_a = carve(rec_room, rec_raw, [P, RC, REC])
        raw_out = carve(rec_room, rec_raw, [P, REC])
        raw_down = carve(rec_room, rec_raw, [P, INTER])
        wa_t = carve(rec_room, rec_raw, [P, RC, REC])
        act_raw = [0]
        raw_mlp = carve(act_room, act_raw, [P, 2 * IC, P])
        raw_shared = carve(act_room, act_raw, [P, 2, SC * P])
        scaled = carve(act_room, act_raw, [P, NREC + 2 * IC, P])

        room = sb("room", [P, ROOM])
        early = [0]
        rank_of = carve(room, early, [P, NT, E])
        tile_no = carve(room, early, [P, TILES, E])
        restart = carve(room, early, [P, E, NT])
        st6 = carve(room, early, [P, NT, 6])
        routing = [early[0]]
        x_sb = carve(room, early, [P, NT, P])
        lg = carve(room, routing, [P, NT, 2 * E])
        logit = carve(room, routing, [P, NT, E])
        first = carve(room, routing, [P, NT, E])
        second = carve(room, routing, [P, NT, E])
        scratch = carve(room, routing, [P, NT, E])
        chosen = carve(room, routing, [P, E, NT])
        count = carve(room, routing, [P, E, NT])
        steps = carve(room, routing, [P, E, NT])
        offset = carve(room, routing, [P, E, NT])
        slot = carve(room, routing, [P, E, NT])
        passed = carve(room, routing, [P, TILES, E])
        late = [0]
        got = carve(room, late, [P, 2, 2, BT, P])
        half_sum = carve(room, late, [P, 2, BLK])
        fin = carve(room, late, [P, 2, BLK])
        x_back = carve(room, late, [P, 2, BLK])
        silu_f = fin
        gated = half_sum

        x_loaded = sem("x_loaded")
        rec_loaded = sem("rec_loaded")
        small_loaded = sem("small_loaded")
        mlp_loaded = sem("mlp_loaded")
        shared_loaded = sem("shared_loaded")
        up_loaded = sem("up_loaded")
        down_loaded = sem("down_loaded")
        zeroed = sem("zeroed")
        pads_ready = sem("pads_ready")
        zeros_ready = sem("zeros_ready")
        consts_ready = sem("consts_ready")
        const_step = sem("const_step")
        stats_done = sem("stats_done")
        std_done = sem("std_done")
        msq_done = sem("msq_done")
        rms1_done = sem("rms1_done")
        xn_done = sem("xn_done")
        normal_done = sem("normal_done")
        x_tok_done = sem("x_tok_done")
        rstd_done = sem("rstd_done")
        wT_done = sem("wT_done")
        wT_taken = sem("wT_taken")
        waT_done = sem("waT_done")
        scaled_done = sem("scaled_done")
        w_hi_done = sem("w_hi_done")
        w_lo_done = sem("w_lo_done")
        shared_split = sem("shared_split")
        router_split = sem("router_split")
        waT_taken = sem("waT_taken")
        tiny_ready = sem("tiny_ready")
        stats_step = sem("stats_step")
        feed_done = sem("feed_done")
        scan_done = sem("scan_done")
        carry_done = sem("carry_done")
        r2_done = sem("r2_done")
        half_done = sem("half_done")
        product_done = sem("product_done")
        up_hi_done = sem("up_hi_done")
        up_lo_done = sem("up_lo_done")
        xT_done = sem("xT_done")
        xT_hi_done = sem("xT_hi_done")
        xT_lo_done = sem("xT_lo_done")
        logits_done = sem("logits_done")
        route_step = sem("route_step")
        gap_done = sem("gap_done")
        egap_done = sem("egap_done")
        chosen_done = sem("chosen_done")
        ranks_done = sem("ranks_done")
        slots_known = sem("slots_known")
        experts_known = sem("experts_known")
        scattered = sem("scattered")

        h_done = sem("h_done")
        hT_done = sem("hT_done")
        hT_hi_done = sem("hT_hi_done")
        hT_lo_done = sem("hT_lo_done")
        pair_done = sem("pair_done")
        t_decay_done = sem("t_decay_done")
        decay_done = sem("decay_done")
        square_done = sem("square_done")
        rest_done = sem("rest_done")
        x_in_done = sem("x_in_done")
        t_gate_done = sem("t_gate_done")
        root_done = sem("root_done")
        y_done = sem("y_done")
        proj_done = sem("proj_done")
        mid_done = sem("mid_done")
        ssq_done = sem("ssq_done")
        rms2_done = sem("rms2_done")
        h2_done = sem("h2_done")
        h2T_done = sem("h2T_done")
        h2_hi_done = sem("h2_hi_done")
        h2_lo_done = sem("h2_lo_done")
        silu_done = sem("silu_done")
        sh_act_done = sem("sh_act_done")
        mlp_act_done = sem("mlp_act_done")
        sh_out_done = sem("sh_out_done")
        shared_done = sem("shared_done")
        mlp_out_done = sem("mlp_out_done")
        s_done = sem("s_done")

        tile_loaded = [sem(f"tile_loaded{i}") for i in range(4)]
        eT_done = sem("eT_done")
        e_hi_done = sem("e_hi_done")
        e_lo_done = sem("e_lo_done")
        e_up_done = sem("e_up_done")
        e_silu_done = sem("e_silu_done")
        e_act_done = sem("e_act_done")
        e_actT_done = sem("e_actT_done")
        e_copy_done = sem("e_copy_done")
        e_down_done = sem("e_down_done")
        e_out_done = sem("e_out_done")
        tile_stored = [sem(f"tile_stored{i}") for i in range(4)]
        gathered = [sem(f"gathered{i}") for i in range(2)]
        x_again = [sem(f"x_again{i}") for i in range(2)]
        summed = sem("summed")
        silu_f_done = sem("silu_f_done")
        gated_done = sem("gated_done")
        out_stored = [sem(f"out_stored{i}") for i in range(2)]

        GROUPS = [(0, 2 * RC), (2 * RC, NREC), (NREC, NREC + IC), (NREC + IC, NREC + 2 * IC)]
        ranks_ps = pair[2][:, 0, 0 : E * NT]
        counts_ps = pair[2][:, 1, 0 : E * NT]
        PAIRS = 3 + SC + IC
        assert PAIRS % 3 == 0

        block = ctx.enter_context(nc.Block())

        @block.sync
        def _(sp):
            sp.dma_start(x_sb[:, :, :], xt).then_inc(x_loaded, 16)
            sp.dma_start(raw_rec[:, 0:RC, :], w_in.rearrange("(c p) h -> p c h", p=P)).then_inc(rec_loaded, 16)
            sp.dma_start(raw_rec[:, RC:, :], w_gate.rearrange("(c p) h -> p c h", p=P)).then_inc(rec_loaded, 16)
            sp.dma_start(raw_a[:, :, :], w_a.rearrange("(c p) h -> p c h", p=P)).then_inc(rec_loaded, 16)
            sp.dma_start(raw_out[:, :], w_out).then_inc(rec_loaded, 16)
            sp.dma_start(raw_down[:, :], w_mlp_down).then_inc(rec_loaded, 16)
            sp.dma_start(raw_mlp[:, 0:IC, :], w_mlp_gate.rearrange("(c p) h -> p c h", p=P)).then_inc(mlp_loaded, 16)
            sp.dma_start(raw_mlp[:, IC:, :], w_mlp_up.rearrange("(c p) h -> p c h", p=P)).then_inc(mlp_loaded, 16)
            sp.dma_start(raw_router[:, :], gate_w).then_inc(small_loaded, 16)
            sp.dma_start(ln1[:, :], ln1_w.rearrange("(p o) -> p o", o=1)).then_inc(small_loaded, 16)
            sp.dma_start(ln2[:, :], ln2_w.rearrange("(p o) -> p o", o=1)).then_inc(small_loaded, 16)
            for c in range(RC):
                sp.dma_start(ap_sb[:, c : c + 1], a_param[c * P : (c + 1) * P].rearrange("(p o) -> p o", o=1)).then_inc(
                    small_loaded, 16
                )
            sp.wait_ge(pads_ready, 4)
            sp.dma_start(raw_shared[:, 0, 0:IS], Sg).then_inc(shared_loaded, 16)
            sp.dma_start(raw_shared[:, 1, 0:IS], Su).then_inc(shared_loaded, 16)
            sp.dma_start(sd_sb[:, 0, :], Sd[0:P, :]).then_inc(shared_loaded, 16)
            sp.dma_start(sd_sb[0 : IS - P, 1, :], Sd[P:IS, :]).then_inc(shared_loaded, 16)
            sp.wait_ge(zeros_ready, 1)
            flat = slots.rearrange("(p n) d -> p (n d)", p=P)
            for c in range(SLOTS // ZW):
                sp.dma_start(flat[:, c * ZW : (c + 1) * ZW], zeros[:, :]).then_inc(zeroed, 16)
            sp.dma_start(raw_up[:, :, 0:I], Wg.rearrange("e h i -> h e i")).then_inc(up_loaded, 16)
            sp.dma_start(raw_up[:, :, I:], Wu.rearrange("e h i -> h e i")).then_inc(up_loaded, 16)
            for c in range(EC):
                n = min(P, I - c * P)
                sp.dma_start(
                    wd_sb[0:n, :, c * P : (c + 1) * P], Wd[:, c * P : c * P + n, :].rearrange("e i h -> i e h")
                ).then_inc(down_loaded, 16)

            def load_tile(i, j):
                sp.dma_start(x_tile[:, j % 4, :], slots[bass.ds((i * 4 + j) * P, P), :]).then_inc(
                    tile_loaded[j % 4], 16
                )

            def store_tile(i, j):
                sp.wait_ge(e_out_done, i * 4 + (j + 2))
                sp.dma_start(moved[bass.ds((i * 4 + j) * P, P), :], y_tile[:, j % 4, :]).then_inc(
                    tile_stored[j % 4], 16
                )

            sp.wait_ge(scattered, 16 * 2 * NT)
            sp.wait_ge(s_done, HALF + 1)
            for j in range(4):
                load_tile(0, j)
            for j in range(3):
                sp.wait_ge(eT_done, j + 1)
                load_tile(0, j + 4)
            with sp.Fori(0, TILES // 4 - 2) as i:
                for j in range(4):
                    sp.wait_ge(eT_done, i * 4 + (j + 4))
                    load_tile(i, j + 7)
                    store_tile(i, j)
            sp.wait_ge(eT_done, TILES - 4)
            load_tile(0, TILES - 1)
            for t in range(TILES - 8, TILES):
                store_tile(0, t)
            def load_x(i, k):
                sp.dma_start(x_back[:, k, :].rearrange("p (t d) -> p t d", d=P),
                             xt[:, bass.ds((i * 2 + k) * BT, BT), :]).then_inc(x_again[k], 16)

            def store(i, k):
                sp.wait_ge(gated_done, i * 2 + (k + 1))
                sp.dma_start(ot[:, bass.ds((i * 2 + k) * BT, BT), :],
                             gated[:, k, :].rearrange("p (t d) -> p t d", d=P)).then_inc(out_stored[k], 16)

            load_x(0, 0)
            load_x(0, 1)
            with sp.Fori(0, NB // 2 - 1) as i:
                for k in range(2):
                    store(i, k)
                    load_x(i + 1, k)
            for k in range(2):
                store(NB // 2 - 1, k)
            for k in range(2):
                sp.wait_ge(out_stored[k], 16 * (NB // 2))

        @block.gpsimd
        def _(pool):
            pool.memset(zeros[:, :], 0.0).then_inc(zeros_ready, 1)
            pool.memset(ident[:, :], 0.0).then_inc(const_step, 1)
            pool.memset(ones[:, :], 1.0).then_inc(const_step, 1)
            pool.memset(below[:, :], 1.0).then_inc(const_step, 1)
            pool.memset(rank_of[:, :, :], 0.0).then_inc(const_step, 1)
            pool.memset(raw_shared[:, :, IS:], 0.0).then_inc(pads_ready, 1)
            pool.memset(sd_sb[:, 1, :], 0.0).then_inc(pads_ready, 1)
            pool.memset(wd_sb[:, :, (EC - 1) * P :], 0.0).then_inc(pads_ready, 1)
            pool.memset(act_e[:, :, I:], 0.0).then_inc(pads_ready, 1)
            pool.wait_ge(const_step, 4)
            pool.affine_select(
                out=ident[:, :], in_=ident[:, :], compare_op=ALU.not_equal, fill=1.0, base=0,
                pattern=[[-1, P]], channel_multiplier=1,
            ).then_inc(consts_ready, 1)
            pool.affine_select(
                out=below[:, :], in_=below[:, :], compare_op=ALU.is_gt, fill=0.0, base=0,
                pattern=[[1, P]], channel_multiplier=-1,
            ).then_inc(consts_ready, 1)
            pool.iota(rank_of[:, :, :], pattern=[[0, NT], [-1, E]], base=E, channel_multiplier=0,
                      allow_small_or_imprecise_dtypes=True).then_inc(consts_ready, 1)
            pool.iota(tile_no[:, :, :], pattern=[[1, TILES], [0, E]], base=0, channel_multiplier=0,
                      allow_small_or_imprecise_dtypes=True).then_inc(consts_ready, 1)
            pool.memset(restart[:, :, :], 1.0).then_inc(const_step, 1)
            pool.memset(keep[:, :], 0.0).then_inc(const_step, 1)
            pool.wait_ge(const_step, 6)
            pool.memset(restart[:, :, 0:1], 0.0).then_inc(consts_ready, 1)
            pool.memset(keep[:, 1 : NB : 2], 1.0).then_inc(consts_ready, 1)
            for e in range(E):
                pool.wait_ge(up_hi_done, e + 1)
                pool.tensor_tensor(up_lo[:, e, :], raw_up[:, e, :], up_hi[:, e, :].bitcast(F32),
                                   ALU.subtract).then_inc(up_lo_done, 1)
            pool.wait_ge(zeroed, 16 * (SLOTS // ZW))
            pool.wait_ge(slots_known, 1)
            pool.wait_ge(xn_done, NB)
            for t in range(NT):
                for c in range(2):
                    pool.indirect_dma_start(
                        slots, bass.IndirectOffsetOnAxis(ap=slot_i[:, c, t : t + 1], axis=0), xn[:, t, :], None
                    ).then_inc(scattered, 16)
            for k in range(4):
                pool.wait_ge(tile_stored[k], 16 * (TILES // 4))
            for f in range(NB):
                k = f % 2
                if f >= 2:
                    pool.wait_ge(summed, f - 1)
                for t in range(BT):
                    for c in range(2):
                        pool.indirect_dma_start(
                            got[:, k, c, t, :], None, moved,
                            bass.IndirectOffsetOnAxis(ap=slot_i[:, c, f * BT + t : f * BT + t + 1], axis=0),
                        ).then_inc(gathered[k], 16)

        @block.tensor
        def _(pe):
            def split_product(dst, c_hi, c_lo, m_hi, m_lo):
                pe.matmul(dst, c_hi, m_hi, start=True, stop=False)
                pe.matmul(dst, c_lo, m_hi, start=False, stop=False)
                return pe.matmul(dst, c_hi, m_lo, start=False, stop=True)

            pe.wait_ge(consts_ready, 1)
            pe.wait_ge(rec_loaded, 16 * 5)
            banks = [pair[0][:, 0, :], pair[0][:, 1, :], pair[1][:, 0, :], pair[1][:, 1, :]]
            for c in range(RC):
                for j in range(RC):
                    last = pe.transpose(pair[2][:, 0, (j * RC + c) * P : (j * RC + c + 1) * P],
                                        raw_a[:, c, j * P : (j + 1) * P], ident[:, :])
            last.then_inc(waT_done, 1)
            for c in range(2 * RC):
                last = pe.transpose(banks[0][:, c * P : (c + 1) * P], raw_rec[:, c, :], ident[:, :])
            last.then_inc(wT_done, 1)
            for c in range(RC):
                last = pe.transpose(banks[1][:, c * P : (c + 1) * P], raw_out[:, c * P : (c + 1) * P], ident[:, :])
            last.then_inc(wT_done, 1)
            for c in range(IC):
                last = pe.transpose(banks[2][:, c * P : (c + 1) * P], raw_down[:, c * P : (c + 1) * P], ident[:, :])
            last.then_inc(wT_done, 1)
            pe.wait_ge(waT_taken, 1)
            for j in range(RC):
                last = pe.matmul(banks[3][:, 0:REC], raw_rec[:, j, :], wa_t[:, j, :], start=(j == 0), stop=(j == RC - 1))
            last.then_inc(wT_done, 1)
            pe.wait_ge(mlp_loaded, 32)
            pe.wait_ge(scaled_done, 1)
            for half in range(2):
                for c in range(IC):
                    last = pe.transpose(banks[half][:, c * P : (c + 1) * P], raw_mlp[:, half * IC + c, :], ident[:, :])
                last.then_inc(wT_done, 1)

            def turn_x(i, j):
                pe.wait_ge(normal_done, i * 2 + (j + 1))
                for k in range(BT):
                    last = pe.transpose(turned[:, k * P : (k + 1) * P], (h_tok, h2_tok)[j % 2][:, k, :], ident[:, :])
                last.then_inc(xT_done, 1)

            logits_ps = pair[2][:, 1, :].rearrange("p (t e) -> p t e", e=2 * E)

            def logits(b):
                pe.wait_ge(xT_lo_done, b + 1)
                for k in range(BT):
                    dst = logits_ps[:, b * BT + k, :]
                    pe.matmul(dst, part_hi[:, k * P : (k + 1) * P], rt_w[:, :], start=True, stop=False)
                    last = pe.matmul(dst, part_lo[:, k * P : (k + 1) * P], rt_w[:, :], start=False, stop=True)
                last.then_inc(logits_done, 1)

            pe.wait_ge(router_split, 2)
            turn_x(0, 0)
            with pe.Fori(0, NB // 2 - 1) as i:
                for j in range(2):
                    logits(i * 2 + j)
                    turn_x(i, j + 1)
            logits(NB - 2)
            turn_x(0, NB - 1)
            logits(NB - 1)

            def turn_h(b):
                pe.wait_ge(h_done, b + 1)
                for k in range(BT):
                    last = pe.transpose(turned[:, k * P : (k + 1) * P], h_tok[:, k, :], ident[:, :])
                last.then_inc(hT_done, 1)

            def rec_pair(n):
                first_chunk = (2 * RC, 0, RC)[n]
                for c in range(RC):
                    w = first_chunk + c
                    last = split_product(pair[n][:, c, :], w_hi[:, w, :], w_lo[:, w, :], hT_hi[:, :], hT_lo[:, :])
                last.then_inc(pair_done, 1)

            def project(b):
                pe.wait_ge(y_done, b + 1)
                pe.wait_ge(s_done, b + 1)
                for c in range(RC):
                    for k in range(BT):
                        last = pe.matmul(bytok[:, k * P : (k + 1) * P], y[:, c, k * P : (k + 1) * P], wout_t[:, c, :],
                                         start=(c == 0 and k == 0), stop=(c == RC - 1), skip_group_check=True)
                last.then_inc(proj_done, 1)

            def turn_block_x(b):
                pe.wait_ge(x_tok_done, b + 1)
                for k in range(BT):
                    last = pe.transpose(turned[:, k * P : (k + 1) * P], h_tok[:, k, :], ident[:, :])
                last.then_inc(xT_done, 1)

            def shared_up(b, ahead):
                pe.wait_ge(xT_lo_done, b + (NB + 1))
                for c in range(SC):
                    pe.wait_ge((t_decay_done, x_in_done)[c], b + 1 + ahead)
                    for g in range(2):
                        last = split_product(pair[c][:, g, :], sh_hi[:, g, c * P : (c + 1) * P],
                                             sh_lo[:, g, c * P : (c + 1) * P], part_hi[:, :], part_lo[:, :])
                    last.then_inc(pair_done, 1)

            def turn_h2(b):
                pe.wait_ge(h2_done, b + 1)
                for k in range(BT):
                    last = pe.transpose(turned[:, k * P : (k + 1) * P], h2_tok[:, k, :], ident[:, :])
                last.then_inc(h2T_done, 1)

            def shared_down(b):
                pe.wait_ge(sh_act_done, b * SC + SC)
                for c in range(SC):
                    for k in range(BT):
                        last = pe.matmul(bytok[:, k * P : (k + 1) * P], sh_act[:, c, k * P : (k + 1) * P],
                                         sd_sb[:, c, :], start=(c == 0 and k == 0), stop=(c == SC - 1),
                                         skip_group_check=True)
                last.then_inc(sh_out_done, 1)

            def mlp_up(b, ahead):
                pe.wait_ge(h2_lo_done, b + 1)
                for j in range(IC):
                    if j == 0:
                        pe.wait_ge(t_gate_done, b + 1 + ahead)
                    if j == IC - 1:
                        pe.wait_ge(mlp_act_done, b * IC + 1)
                    for g in range(2):
                        w = NREC + g * IC + j
                        last = split_product(pair[(SC + j) % 3][:, g, :], w_hi[:, w, :], w_lo[:, w, :],
                                             h2_hi[:, :], h2_lo[:, :])
                    last.then_inc(pair_done, 1)

            def mlp_down(b):
                pe.wait_ge(shared_done, b + 1)
                for j in range(IC):
                    pe.wait_ge(mlp_act_done, b * IC + (j + 1))
                    for k in range(BT):
                        last = pe.matmul(bytok[:, k * P : (k + 1) * P], mlp_act[:, j, k * P : (k + 1) * P],
                                         wdown_t[:, j, :], start=(j == 0 and k == 0), stop=(j == IC - 1),
                                         skip_group_check=True)
                last.then_inc(mlp_out_done, 1)

            def run_block(b, ahead=1):
                if ahead:
                    turn_h(b + 1)
                project(b)
                if ahead:
                    pe.wait_ge(hT_lo_done, b + 2)
                    rec_pair(0)
                    rec_pair(1)
                turn_block_x(b)
                if ahead:
                    rec_pair(2)
                shared_up(b, ahead)
                turn_h2(b)
                shared_down(b)
                mlp_up(b, ahead)
                mlp_down(b)

            pe.wait_ge(w_lo_done, 4)
            turn_h(0)
            pe.wait_ge(hT_lo_done, 1)
            rec_pair(0)
            rec_pair(1)
            every = chosen[:, :, :].rearrange("p e t -> p (e t)")
            pe.wait_ge(chosen_done, 1)
            pe.matmul(ranks_ps, below[:, :], every, start=True, stop=True)
            pe.matmul(counts_ps, ones[:, :], every, start=True, stop=True).then_inc(ranks_done, 1)
            pe.wait_ge(slots_known, 1)
            rec_pair(2)
            pe.wait_ge(shared_split, 2)
            with pe.Fori(0, HALF) as b:
                run_block(b)

            def e_turn(i, j):
                pe.wait_ge(tile_loaded[j % 4], i * 16 + (j // 4 + 1) * 16)
                pe.transpose(turned[:, 0:P], x_tile[:, j % 4, :], ident[:, :]).then_inc(eT_done, 1)

            def expert_of(i, j):
                return pe.value_load(expert_i[0:1, bass.ds(i * 4 + j, 1)], min_val=0, max_val=E - 1)

            hi_flat = up_hi[:, :, :].rearrange("p e i -> p (e i)")
            lo_flat = up_lo[:, :, :].rearrange("p e i -> p (e i)")
            wd_flat = wd_sb[:, :, :].rearrange("p e i -> p (e i)")

            def e_up(i, j):
                e = expert_of(i, j)
                pe.wait_ge(e_lo_done, i * 4 + (j + 1))
                for g in range(2):
                    dst = pair[j % 2][:, g, 0:I]
                    hi = hi_flat[:, bass.ds(e * (2 * I) + g * I, I)]
                    lo = lo_flat[:, bass.ds(e * (2 * I) + g * I, I)]
                    pe.matmul(dst, xe_hi[:, j % 2, :], hi, start=True, stop=False)
                    pe.matmul(dst, xe_hi[:, j % 2, :], lo, start=False, stop=False)
                    last = pe.matmul(dst, xe_lo[:, j % 2, :], hi, start=False, stop=True)
                last.then_inc(e_up_done, 1)

            def e_turn_act(i, j):
                pe.wait_ge(e_act_done, i * 4 + (j + 1))
                for c in range(EC):
                    last = pe.transpose(pair[2][:, 0, c * P : (c + 1) * P], act_e[:, j % 2, c * P : (c + 1) * P],
                                        ident[:, :])
                last.then_inc(e_actT_done, 1)

            def e_down(i, j):
                e = expert_of(i, j)
                pe.wait_ge(e_copy_done, i * 4 + (j + 1))
                pe.wait_ge(e_out_done, i * 4 + (j + 1))
                for c in range(EC):
                    last = pe.matmul(pair[2][:, 1, 0:P], actT[:, j % 2, c * P : (c + 1) * P],
                                     wd_flat[:, bass.ds(e * (EC * P) + c * P, P)], start=(c == 0), stop=(c == EC - 1))
                last.then_inc(e_down_done, 1)

            pe.wait_ge(s_done, HALF + 1)
            pe.wait_ge(experts_known, 1)
            pe.wait_ge(up_lo_done, E)
            pe.wait_ge(down_loaded, 16 * EC)
            e_turn(0, 0)
            e_up(0, 0)
            e_turn(0, 1)
            e_up(0, 1)
            e_turn(0, 2)
            e_turn_act(0, 0)
            with pe.Fori(0, (TILES - 4) // 4) as i:
                for j in range(1, 5):
                    e_up(i, j + 1)
                    e_turn(i, j + 2)
                    e_down(i, j - 1)
                    e_turn_act(i, j)
            for t in range(TILES - 3, TILES):
                if t + 1 < TILES:
                    e_up(0, t + 1)
                if t + 2 < TILES:
                    e_turn(0, t + 2)
                e_down(0, t - 1)
                e_turn_act(0, t)
            e_down(0, TILES - 1)

            pe.wait_ge(e_out_done, TILES + 1)
            with pe.Fori(HALF, NB - 1) as b:
                run_block(b)
            run_block(NB - 1, ahead=0)

        @block.scalar
        def _(act):
            act.wait_ge(tiny_ready, 3)
            act.wait_ge(stats_done, 1)
            act.activation(std[:, :], mv[:, :, 1], ACT.Sqrt, bias=tiny[:, 0:1]).then_inc(std_done, 1)
            act.wait_ge(msq_done, 1)
            act.activation(rms1[:, :], msq[:, :], ACT.Sqrt, bias=tiny[:, 1:2]).then_inc(rms1_done, 1)

            def x_hi(b):
                act.wait_ge(xT_done, b + 1)
                if not (isinstance(b, int) and b == 0):
                    act.wait_ge(logits_done, b)
                act.activation(part_hi[:, :], turned[:, :], ACT.Copy).then_inc(xT_hi_done, 1)

            def keep_x(i, j):
                act.wait_ge(normal_done, i * 2 + (j + 1))
                act.activation(xn[:, bass.ds((i * 2 + j) * BT, BT), :], (h_tok, h2_tok)[j % 2][:, :, :],
                               ACT.Copy).then_inc(xn_done, 1)

            keep_x(0, 0)
            x_hi(0)
            with act.Fori(0, NB // 2 - 1) as i:
                for j in range(1, 3):
                    keep_x(i, j)
                    x_hi(i * 2 + j)
            keep_x(0, NB - 1)
            x_hi(NB - 1)
            act.wait_ge(gap_done, 1)
            act.activation(egap[:, :], gap[:, :], ACT.Exp).then_inc(egap_done, 1)
            for n, (c0, c1) in enumerate(GROUPS):
                act.wait_ge(scaled_done, n + 1)
                act.activation(w_hi[:, c0:c1, :], scaled[:, c0:c1, :], ACT.Copy).then_inc(w_hi_done, 1)
            act.wait_ge(shared_loaded, 64)
            act.activation(sh_hi[:, :, :], raw_shared[:, :, :], ACT.Copy).then_inc(shared_split, 1)

            def h_hi(b):
                act.wait_ge(hT_done, b + 1)
                act.activation(hT_hi[:, :], turned[:, :], ACT.Copy).then_inc(hT_hi_done, 1)

            def rec_decay(b, q):
                act.wait_ge(pair_done, q + 1)
                for c in range(RC):
                    last = act.activation(t_decay[:, c, :], pair[0][:, c, :], ACT.Tanh, bias=ap_half[:, c : c + 1],
                                          scale=0.5)
                last.then_inc(t_decay_done, 1)
                act.wait_ge(decay_done, b + 1)
                act.activation(square[:, :, :], decay[:, :, :], ACT.Square).then_inc(square_done, 1)

            def rec_x_in(q):
                act.wait_ge(pair_done, q + 2)
                act.activation(x_in[:, :, :], pair[1][:, :, :], ACT.Copy).then_inc(x_in_done, 1)

            def rec_gate(q):
                act.wait_ge(pair_done, q + 3)
                act.activation(t_gate[:, :, :], pair[2][:, :, :], ACT.Tanh, scale=0.5).then_inc(t_gate_done, 1)

            def rec_root(b):
                act.wait_ge(rest_done, b + 1)
                act.activation(root[:, :, :], rest[:, :, :], ACT.Sqrt, bias=tiny[:, 2:3]).then_inc(root_done, 1)

            def mid_squares(b):
                act.wait_ge(mid_done, b + 1)
                for k in range(BT):
                    act.activation(squares[:, k, :], s_tok[:, b * BT + k, :], ACT.Square,
                                   accum_out=ssq[:, k : k + 1]).then_inc(ssq_done, 1)

            def mid_root(b):
                act.wait_ge(ssq_done, b * BT + BT)
                act.activation(rms2[:, :], ssq[:, :], ACT.Sqrt, bias=tiny[:, 1:2], scale=1.0 / H).then_inc(rms2_done, 1)

            def block_x_hi(b):
                act.wait_ge(xT_done, b + (NB + 1))
                act.activation(part_hi[:, :], turned[:, :], ACT.Copy).then_inc(xT_hi_done, 1)

            def take_silu(b, n, q):
                act.wait_ge(pair_done, q + 1)
                if n >= 2 + SC:
                    act.wait_ge(mlp_act_done, b * IC + (n - 2 - SC + 1))
                elif n >= 2:
                    act.wait_ge(sh_act_done, b * SC + (n - 2 + 1))
                act.activation(silu_b[:, n % 2, :], pair[n % 3][:, 0, :], ACT.Silu).then_inc(silu_done, 1)

            def run_block(b, ahead=1):
                q = b * PAIRS + 3
                if ahead:
                    h_hi(b + 1)
                mid_squares(b)
                if ahead:
                    rec_decay(b + 1, q)
                    rec_x_in(q)
                block_x_hi(b)
                if ahead:
                    rec_gate(q)
                mid_root(b)
                if ahead:
                    rec_root(b + 1)
                for n in range(SC):
                    take_silu(b, n, q + 3 * ahead + n)
                act.wait_ge(h2T_done, b + 1)
                act.activation(h2_hi[:, :], turned[:, :], ACT.Copy).then_inc(h2_hi_done, 1)
                act.wait_ge(sh_out_done, b + 1)
                act.activation(shared[:, bass.ds(b * BT, BT), :].rearrange("p t d -> p (t d)"), bytok[:, :],
                               ACT.Copy).then_inc(shared_done, 1)
                for n in range(SC, SC + IC):
                    take_silu(b, n, q + 3 * ahead + n)

            def silu_final(f, k):
                act.wait_ge(summed, f + 1)
                act.activation(silu_f[:, k, :], fin[:, k, :], ACT.Silu).then_inc(silu_f_done, 1)

            h_hi(0)
            rec_decay(0, 0)
            rec_x_in(0)
            act.wait_ge(up_loaded, 32)
            for e in range(E):
                act.activation(up_hi[:, e, :], raw_up[:, e, :], ACT.Copy).then_inc(up_hi_done, 1)
            rec_gate(0)
            rec_root(0)
            with act.Fori(0, HALF) as b:
                run_block(b)

            def e_hi(i, j):
                act.wait_ge(eT_done, i * 4 + (j + 1))
                act.activation(xe_hi[:, j % 2, :], turned[:, 0:P], ACT.Copy).then_inc(e_hi_done, 1)

            def e_silu(i, j):
                act.wait_ge(e_up_done, i * 4 + (j + 1))
                if not (isinstance(i, int) and i * 4 + j < 2):
                    act.wait_ge(e_act_done, i * 4 + (j - 1))
                act.activation(silu_e[:, j % 2, :], pair[j % 2][:, 0, 0:I], ACT.Silu).then_inc(e_silu_done, 1)

            def e_copy(i, j):
                act.wait_ge(e_actT_done, i * 4 + (j + 1))
                act.activation(actT[:, j % 2, :], pair[2][:, 0, 0 : EC * P], ACT.Copy).then_inc(e_copy_done, 1)

            e_hi(0, 0)
            e_silu(0, 0)
            e_hi(0, 1)
            e_silu(0, 1)
            e_hi(0, 2)
            e_copy(0, 0)
            with act.Fori(0, (TILES - 4) // 4) as i:
                for j in range(1, 5):
                    e_silu(i, j + 1)
                    e_hi(i, j + 2)
                    e_copy(i, j)
            for t in range(TILES - 3, TILES):
                if t + 1 < TILES:
                    e_silu(0, t + 1)
                if t + 2 < TILES:
                    e_hi(0, t + 2)
                e_copy(0, t)

            with act.Fori(HALF, NB - 1) as b:
                run_block(b)
                for k in range(2):
                    silu_final(b * 2 + (k - 2 * HALF), k)
            run_block(NB - 1, ahead=0)
            silu_final(NB - 2, 0)
            silu_final(NB - 1, 1)

        @block.vector
        def _(dve):
            def flat(ap):
                return ap.rearrange("p a b -> p (a b)")

            def each(ap):
                return ap.unsqueeze(2).to_broadcast([P, NT, E])

            dve.memset(tiny[:, 0:1], 1e-5).then_inc(tiny_ready, 1)
            dve.memset(tiny[:, 1:2], 1e-6).then_inc(tiny_ready, 1)
            dve.memset(tiny[:, 2:3], 1e-8).then_inc(tiny_ready, 1)
            dve.wait_ge(x_loaded, 16)
            with dve.Fori(0, NT) as t:
                dve.bn_stats(st6[:, t, :], x_sb[:, t, :]).then_inc(stats_step, 1)
            dve.wait_ge(stats_step, NT)
            for t in range(NT):
                last = dve.bn_aggr(mv[:, t, :], st6[:, t, :])
            last.then_inc(stats_done, 1)
            dve.wait_ge(rec_loaded, 16 * 5)
            dve.wait_ge(small_loaded, 16 * (3 + RC))
            dve.tensor_scalar(ap_half[:, :], ap_sb[:, :], 0.5, None, ALU.mult)
            dve.wait_ge(waT_done, 1)
            dve.tensor_copy(flat(wa_t[:, :, :]), pair[2][:, 0, 0 : RC * REC]).then_inc(waT_taken, 1)
            dve.wait_ge(wT_done, 2)
            dve.tensor_scalar(flat(wout_t[:, :, :]), pair[0][:, 1, 0:REC], 0.5, None, ALU.mult).then_inc(wT_taken, 1)
            dve.tensor_scalar(flat(scaled[:, 0 : 2 * RC, :]), pair[0][:, 0, :], ln1[:, 0:1], None,
                              ALU.mult).then_inc(scaled_done, 1)
            dve.wait_ge(wT_done, 3)
            dve.tensor_copy(flat(wdown_t[:, :, :]), pair[1][:, 0, :]).then_inc(wT_taken, 1)
            dve.wait_ge(std_done, 1)
            dve.reciprocal(rstd[:, :], std[:, :]).then_inc(rstd_done, 1)
            dve.wait_ge(rstd_done, 1)
            dve.tensor_tensor(msq[:, :], mv[:, :, 1], rstd[:, :], ALU.mult).then_inc(rstd_done, 1)
            dve.wait_ge(rstd_done, 2)
            dve.tensor_tensor(msq[:, :], msq[:, :], rstd[:, :], ALU.mult).then_inc(msq_done, 1)
            dve.tensor_copy(rt_w[:, 0:E], raw_router[:, :]).then_inc(router_split, 1)
            dve.wait_ge(router_split, 1)
            dve.tensor_tensor(rt_w[:, E:], raw_router[:, :], rt_w[:, 0:E].bitcast(F32), ALU.subtract).then_inc(
                router_split, 1
            )

            def normalise(i, j):
                if not (isinstance(i, int) and i * 2 + j < 2):
                    dve.wait_ge(xn_done, i * 2 + (j - 1))
                for k in range(BT):
                    t = (i * 2 + j) * BT + k
                    last = dve.tensor_scalar((h_tok, h2_tok)[j % 2][:, k, :], x_sb[:, t, :], mv[:, t, 0:1],
                                             rstd[:, bass.ds(t, 1)], ALU.subtract, ALU.mult)
                last.then_inc(normal_done, 1)

            def x_lo(n):
                dve.wait_ge(xT_hi_done, n + 1)
                dve.tensor_tensor(part_lo[:, :], turned[:, :], part_hi[:, :].bitcast(F32), ALU.subtract).then_inc(
                    xT_lo_done, 1
                )

            normalise(0, 0)
            normalise(0, 1)
            with dve.Fori(0, NB // 2 - 1) as i:
                for j in range(2):
                    x_lo(i * 2 + j)
                    normalise(i, j + 2)
            x_lo(NB - 2)
            x_lo(NB - 1)
            dve.wait_ge(rms1_done, 1)
            dve.reciprocal(r1[:, :], rms1[:, :]).then_inc(rstd_done, 1)

            step = [0]

            def done(ins):
                step[0] += 1
                ins.then_inc(route_step, 1)
                dve.wait_ge(route_step, step[0])

            dve.wait_ge(consts_ready, 6)
            dve.wait_ge(logits_done, NB)
            done(dve.tensor_copy(flat(lg[:, :, :]), pair[2][:, 1, :]))
            done(dve.tensor_tensor(logit[:, :, :], lg[:, :, 0:E], lg[:, :, E:], ALU.add))

            def best_of(values, top, one_hot):
                done(dve.tensor_reduce(top, values, AX.X, ALU.max))
                done(dve.tensor_tensor(scratch[:, :, :], values, each(top), ALU.is_equal))
                done(dve.tensor_tensor(scratch[:, :, :], scratch[:, :, :], rank_of[:, :, :], ALU.mult))
                done(dve.tensor_reduce(best[:, :], scratch[:, :, :], AX.X, ALU.max))
                done(dve.tensor_tensor(one_hot, scratch[:, :, :], each(best[:, :]), ALU.is_equal))

            best_of(logit[:, :, :], m1[:, :], first[:, :, :])
            done(dve.scalar_tensor_tensor(out=logit[:, :, :], in0=first[:, :, :], scalar=-BIG, in1=logit[:, :, :],
                                          op0=ALU.mult, op1=ALU.add))
            best_of(logit[:, :, :], m2[:, :], second[:, :, :])
            dve.tensor_tensor(gap[:, :], m2[:, :], m1[:, :], ALU.subtract).then_inc(gap_done, 1)
            dve.tensor_tensor(chosen[:, :, :].rearrange("p e t -> p t e"), first[:, :, :], second[:, :, :],
                              ALU.add).then_inc(chosen_done, 1)
            dve.wait_ge(egap_done, 1)
            done(dve.tensor_scalar(esum[:, :], egap[:, :], 1.0, None, ALU.add))
            done(dve.reciprocal(p1[:, :], esum[:, :]))
            done(dve.tensor_tensor(p2[:, :], egap[:, :], p1[:, :], ALU.mult))

            def make_h(b):
                for k in range(BT):
                    t = b * BT + k
                    last = dve.tensor_scalar(h_tok[:, k, :], xn[:, t, :], r1[:, bass.ds(t, 1)], None, ALU.mult)
                last.then_inc(h_done, 1)

            def h_lo(b):
                dve.wait_ge(hT_hi_done, b + 1)
                dve.tensor_tensor(hT_lo[:, :], turned[:, :], hT_hi[:, :].bitcast(F32), ALU.subtract).then_inc(
                    hT_lo_done, 1
                )

            def make_decay(b):
                dve.wait_ge(t_decay_done, b + 1)
                dve.tensor_scalar(decay[:, :, :], t_decay[:, :, :], 0.5, 0.5, ALU.mult, ALU.add).then_inc(decay_done, 1)
                dve.wait_ge(square_done, b + 1)
                dve.tensor_scalar(rest[:, :, :], square[:, :, :], -1.0, 1.0, ALU.mult, ALU.add).then_inc(rest_done, 1)

            def make_feed(b):
                dve.wait_ge(x_in_done, b + 1)
                dve.wait_ge(root_done, b + 1)
                dve.tensor_tensor(feed[:, :, :], root[:, :, :], x_in[:, :, :], ALU.mult).then_inc(feed_done, 1)

            def scan(b):
                dve.wait_ge(feed_done, b + 1)
                dve.wait_ge(carry_done, b + 1)
                for c in range(RC):
                    dve.tensor_tensor_scan(state[:, c, :], decay[:, c, :], feed[:, c, :], carry[:, c : c + 1],
                                           ALU.mult, ALU.add).then_inc(scan_done, 1)

            def make_y(b):
                dve.wait_ge(t_gate_done, b + 1)
                dve.wait_ge(scan_done, b * RC + RC)
                dve.tensor_scalar(carry[:, :], state[:, :, BLK - 1], keep[:, bass.ds(b + 1, 1)], None,
                                  ALU.mult).then_inc(carry_done, 1)
                dve.scalar_tensor_tensor(out=flat(y[:, :, :]), in0=flat(t_gate[:, :, :]), scalar=1.0,
                                         in1=flat(state[:, :, :]), op0=ALU.add, op1=ALU.mult).then_inc(y_done, 1)

            def tokens(ap, b):
                return ap[:, bass.ds(b * BT, BT), :].rearrange("p t d -> p (t d)")

            def middle(b):
                dve.wait_ge(proj_done, b + 1)
                dve.tensor_tensor(tokens(s_tok, b), bytok[:, :], tokens(xn, b), ALU.add).then_inc(mid_done, 1)

            def make_h2(b):
                dve.wait_ge(rms2_done, b + 1)
                dve.reciprocal(r2[:, :], rms2[:, :]).then_inc(r2_done, 1)
                dve.wait_ge(r2_done, b + 1)
                for k in range(BT):
                    last = dve.tensor_scalar(h2_tok[:, k, :], s_tok[:, b * BT + k, :], r2[:, k : k + 1], None, ALU.mult)
                last.then_inc(h2_done, 1)

            def make_h2_lo(b):
                dve.wait_ge(h2_hi_done, b + 1)
                dve.tensor_tensor(h2_lo[:, :], turned[:, :], h2_hi[:, :].bitcast(F32), ALU.subtract).then_inc(
                    h2_lo_done, 1
                )

            def shared_act(b, c):
                dve.wait_ge(silu_done, b * (SC + IC) + (c + 1))
                dve.tensor_tensor(sh_act[:, c, :], silu_b[:, c % 2, :], pair[c][:, 1, :], ALU.mult).then_inc(
                    sh_act_done, 1
                )

            def mlp_product(b, j):
                n = SC + j
                dve.wait_ge(silu_done, b * (SC + IC) + (n + 1))
                dve.tensor_tensor(mlp_act[:, j, :], silu_b[:, n % 2, :], pair[n % 3][:, 1, :], ALU.mult).then_inc(
                    mlp_act_done, 1
                )

            def make_s(b):
                dve.wait_ge(mlp_out_done, b + 1)
                dve.tensor_tensor(tokens(s_tok, b), bytok[:, :], tokens(s_tok, b), ALU.add).then_inc(s_done, 1)

            def run_block(b, ahead=2):
                if ahead:
                    h_lo(b + 1)
                dve.tensor_copy(h_tok[:, :, :], xn[:, bass.ds(b * BT, BT), :]).then_inc(x_tok_done, 1)
                middle(b)
                if ahead:
                    make_decay(b + 1)
                x_lo(b + NB)
                make_h2(b)
                if ahead:
                    make_feed(b + 1)
                for c in range(SC):
                    shared_act(b, c)
                if ahead:
                    scan(b + 1)
                make_h2_lo(b)
                if ahead:
                    make_y(b + 1)
                for j in range(IC):
                    mlp_product(b, j)
                if ahead > 1:
                    make_h(b + 2)
                make_s(b)

            dve.memset(carry[:, :], 0.0).then_inc(carry_done, 1)
            dve.engine_nop().then_inc(s_done, 1)
            dve.engine_nop().then_inc(e_out_done, 1)
            dve.wait_ge(rstd_done, 3)
            make_h(0)
            dve.wait_ge(wT_done, 4)
            dve.tensor_scalar(flat(scaled[:, 2 * RC : NREC, :]), pair[1][:, 1, 0:REC], ln1[:, 0:1], None,
                              ALU.mult).then_inc(scaled_done, 1)
            for half in range(2):
                dve.wait_ge(wT_done, 5 + half)
                dve.tensor_scalar(flat(scaled[:, NREC + half * IC : NREC + (half + 1) * IC, :]), pair[0][:, half, :],
                                  ln2[:, 0:1], None, ALU.mult).then_inc(scaled_done, 1)
            for n, (c0, c1) in enumerate(GROUPS):
                dve.wait_ge(w_hi_done, n + 1)
                dve.tensor_tensor(w_lo[:, c0:c1, :], scaled[:, c0:c1, :], w_hi[:, c0:c1, :].bitcast(F32),
                                  ALU.subtract).then_inc(w_lo_done, 1)
            dve.wait_ge(shared_split, 1)
            dve.tensor_tensor(sh_lo[:, :, :], raw_shared[:, :, :], sh_hi[:, :, :].bitcast(F32),
                              ALU.subtract).then_inc(shared_split, 1)
            h_lo(0)

            dve.wait_ge(ranks_done, 1)
            done(dve.tensor_copy(flat(count[:, :, :]), counts_ps))
            done(dve.tensor_reduce(total[:, :], count[:, :, :], AX.X, ALU.add))
            done(dve.tensor_scalar(total_i[:, :], total[:, :], float(P - 1), None, ALU.add))
            done(dve.tensor_scalar(tiles_i[:, :], total_i[:, :], 7, None, ALU.logical_shift_right))
            done(dve.tensor_copy(tiles[:, :], tiles_i[:, :]))
            done(dve.tensor_tensor_scan(tiles_to[:, :], ones[:, 0:E], tiles[:, :], 0.0, ALU.mult, ALU.add))
            done(dve.tensor_tensor(tiles_from[:, :], tiles_to[:, :], tiles[:, :], ALU.subtract))
            done(dve.tensor_scalar(steps[:, :, 0], tiles_from[:, :], float(P), None, ALU.mult))
            done(dve.tensor_copy(steps[:, :, 1:], count[:, :, 0 : NT - 1]))
            done(dve.tensor_tensor_scan(flat(offset[:, :, :]), flat(restart[:, :, :]), flat(steps[:, :, :]), 0.0,
                                        ALU.mult, ALU.add))
            done(dve.tensor_tensor(flat(slot[:, :, :]), flat(offset[:, :, :]), ranks_ps, ALU.add))
            for c, one_hot in enumerate((first, second)):
                done(dve.tensor_tensor(scratch[:, :, :], one_hot[:, :, :], slot[:, :, :].rearrange("p e t -> p t e"),
                                       ALU.mult))
                done(dve.tensor_reduce(slot_f[:, c, :], scratch[:, :, :], AX.X, ALU.add))
            dve.tensor_copy(slot_i[:, :, :], slot_f[:, :, :]).then_inc(slots_known, 1)
            done(dve.tensor_tensor(passed[:, :, :], tile_no[:, :, :],
                                   tiles_to[:, :].unsqueeze(1).to_broadcast([P, TILES, E]), ALU.is_ge))
            done(dve.tensor_reduce(expert_f[:, :], passed[:, :, :], AX.X, ALU.add))
            dve.tensor_scalar(expert_i[:, :], expert_f[:, :], float(E - 1), None, ALU.min).then_inc(experts_known, 1)

            make_decay(0)
            make_feed(0)
            dve.wait_ge(zeroed, 16 * (SLOTS // ZW))
            scan(0)
            make_y(0)
            make_h(1)
            dve.wait_ge(up_lo_done, E)
            with dve.Fori(0, HALF) as b:
                run_block(b)

            def e_lo(i, j):
                dve.wait_ge(e_hi_done, i * 4 + (j + 1))
                dve.tensor_tensor(xe_lo[:, j % 2, :], turned[:, 0:P], xe_hi[:, j % 2, :].bitcast(F32),
                                  ALU.subtract).then_inc(e_lo_done, 1)

            def e_act(i, j):
                dve.wait_ge(e_silu_done, i * 4 + (j + 1))
                if not (isinstance(i, int) and i * 4 + j < 2):
                    dve.wait_ge(e_actT_done, i * 4 + (j - 1))
                dve.tensor_tensor(act_e[:, j % 2, 0:I], silu_e[:, j % 2, :], pair[j % 2][:, 1, 0:I],
                                  ALU.mult).then_inc(e_act_done, 1)

            def e_out(i, j):
                dve.wait_ge(e_down_done, i * 4 + (j + 1))
                if not (isinstance(i, int) and i * 4 + j < 4):
                    dve.wait_ge(tile_stored[j % 4], i * 16 + (j // 4) * 16)
                dve.tensor_copy(y_tile[:, j % 4, :], pair[2][:, 1, 0:P]).then_inc(e_out_done, 1)

            dve.wait_ge(pads_ready, 4)
            e_lo(0, 0)
            e_act(0, 0)
            e_lo(0, 1)
            e_act(0, 1)
            e_lo(0, 2)

            def e_step(i, j):
                e_act(i, j + 1)
                e_lo(i, j + 2)
                e_out(i, j - 1)

            for j in range(1, 5):
                e_step(0, j)
            with dve.Fori(1, (TILES - 4) // 4) as i:
                for j in range(1, 5):
                    e_step(i, j)
            for t in range(TILES - 3, TILES):
                if t + 1 < TILES:
                    e_act(0, t + 1)
                if t + 2 < TILES:
                    e_lo(0, t + 2)
                e_out(0, t - 1)
            e_out(0, TILES - 1)

            def add_experts(f, k, n):
                dve.wait_ge(gathered[k], n * (16 * 2 * BT))
                if not (isinstance(n, int) and n == 1):
                    dve.wait_ge(out_stored[k], n * 16 - 16)
                for t in range(BT):
                    cols = slice(t * P, (t + 1) * P)
                    dve.scalar_tensor_tensor(out=half_sum[:, k, cols], in0=got[:, k, 0, t, :],
                                             scalar=p1[:, bass.ds(f * BT + t, 1)], in1=shared[:, f * BT + t, :],
                                             op0=ALU.mult, op1=ALU.add).then_inc(half_done, 1)
                for t in range(BT):
                    cols = slice(t * P, (t + 1) * P)
                    dve.wait_ge(half_done, f * BT + (t + 1))
                    last = dve.scalar_tensor_tensor(out=fin[:, k, cols], in0=got[:, k, 1, t, :],
                                                    scalar=p2[:, bass.ds(f * BT + t, 1)], in1=half_sum[:, k, cols],
                                                    op0=ALU.mult, op1=ALU.add)
                last.then_inc(summed, 1)

            def finish(f, k, n):
                dve.wait_ge(silu_f_done, f + 1)
                dve.tensor_tensor(gated[:, k, :], silu_f[:, k, :], tokens(s_tok, f), ALU.mult).then_inc(product_done, 1)
                dve.wait_ge(product_done, f + 1)
                dve.wait_ge(x_again[k], n * 16)
                dve.tensor_tensor(gated[:, k, :], gated[:, k, :], x_back[:, k, :], ALU.add).then_inc(gated_done, 1)

            def finals(b):
                f, n = b * 2 - 2 * HALF, b - (HALF - 1)
                for k in range(2):
                    add_experts(f + k, k, n)
                for k in range(2):
                    finish(f + k, k, n)

            for k in range(4):
                dve.wait_ge(tile_stored[k], 16 * (TILES // 4))
            run_block(HALF)
            finals(HALF)
            with dve.Fori(HALF + 1, NB - 2) as b:
                run_block(b)
                finals(b)
            run_block(NB - 2, ahead=1)
            finals(NB - 2)
            run_block(NB - 1, ahead=0)
            finals(NB - 1)

    return nc


_INS = [
    "L0_attn_x", "L0_attn_ln1_w", "L0_attn_ln2_w", "L0_attn_w_in", "L0_attn_w_gate", "L0_attn_a_param", "L0_attn_w_a",
    "L0_attn_w_out", "L0_attn_w_mlp_gate", "L0_attn_w_mlp_up", "L0_attn_w_mlp_down", "L0_ffn_gate_w", "L0_ffn_Wg",
    "L0_ffn_Wu", "L0_ffn_Wd", "L0_ffn_Sg", "L0_ffn_Su", "L0_ffn_Sd",
]
_OUTS = [((4, 1024, 128), "float32")]


def kernel(**inputs):
    import numpy as _np
    import concourse.bacc as _bacc
    from concourse import mybir as _mybir
    from concourse.bass_utils import run_bass_kernel_spmd as _run

    nc = _bacc.Bacc("TRN2", target_bir_lowering=False, num_devices=1)
    arrays, args = {}, []
    for name in _INS:
        a = _np.ascontiguousarray(inputs[name])
        arrays[f"in_{name}_dram"] = a
        args.append(nc.dram_tensor(f"in_{name}_dram", a.shape, _mybir.dt.from_np(a.dtype), kind="ExternalInput").ap())
    for i, (shape, dtype) in enumerate(_OUTS):
        dt = _mybir.dt.from_np(_np.dtype(dtype))
        args.append(nc.dram_tensor(f"out_{i}_dram", shape, dt, kind="ExternalOutput").ap())
    gated_recurrent_moe_kernel(nc, *args)
    r = _run(nc, [arrays], core_ids=[0])
    got = tuple(r.results[0][f"out_{i}_dram"] for i in range(len(_OUTS)))
    return got[0]
```

```python
from contextlib import ExitStack

import concourse.bass as bass
from concourse import mybir

F32 = mybir.dt.float32
F32R = mybir.dt.float32r
I32 = mybir.dt.int32
ALU = mybir.AluOpType
ACT = mybir.ActivationFunctionType
AX = mybir.AxisListType

P = 128


def gated_recurrent_moe_kernel(
    nc: bass.Bass,
    x: bass.AP,
    ln1_w: bass.AP,
    ln2_w: bass.AP,
    w_in: bass.AP,
    w_gate: bass.AP,
    a_param: bass.AP,
    w_a: bass.AP,
    w_out: bass.AP,
    w_mlp_gate: bass.AP,
    w_mlp_up: bass.AP,
    w_mlp_down: bass.AP,
    gate_w: bass.AP,
    Wg: bass.AP,
    Wu: bass.AP,
    Wd: bass.AP,
    Sg: bass.AP,
    Su: bass.AP,
    Sd: bass.AP,
    out: bass.AP,
):
    BATCH, T, H = x.shape
    REC = w_in.shape[0]
    INTER = w_mlp_gate.shape[0]
    E, _, I = Wg.shape
    IS = Sg.shape[1]
    TOK = BATCH * T
    NT = TOK // P
    BT = 4
    BLK = BT * P
    NB = TOK // BLK
    RC = REC // P
    IC = INTER // P
    EC = -(-I // P)
    SC = -(-IS // P)
    TILES = 2 * TOK // P + E - 1
    SLOTS = TILES * P
    QT = NT // 4
    HALF = NB // 2
    BIG = 3.0e38
    ZW = RC * BLK
    ROOM = 2 * NT * E + TILES * E + NT * (P + 6)
    assert H == P and T % BLK == 0 and T // BLK == 2 and IC == 4 and RC == 2 and SC == 2

    xt = x.rearrange("b (t p) d -> p (b t) d", p=P)
    ot = out.rearrange("b (t p) d -> p (b t) d", p=P)
    slots = nc.dram_tensor("slots", (SLOTS, P), F32, kind="Internal").ap()
    moved = nc.dram_tensor("moved", (SLOTS, P), F32, kind="Internal").ap()

    with ExitStack() as ctx:

        def sb(name, shape, dt=F32):
            return ctx.enter_context(nc.sbuf_tensor(name, shape, dt))

        def sem(name):
            return ctx.enter_context(nc.semaphore(name))

        pair = [ctx.enter_context(nc.psum_tensor(f"pair{i}", [P, 2, 512], F32)) for i in range(3)]
        turned = ctx.enter_context(nc.psum_tensor("turned", [P, 512], F32))
        bytok = ctx.enter_context(nc.psum_tensor("bytok", [P, 512], F32))

        xn = sb("xn", [P, NT, P])
        ident = sb("ident", [P, P])
        below = sb("below", [P, P])
        ones = sb("ones", [P, P])
        keep = sb("keep", [P, NB + 1])
        tiny = sb("tiny", [P, 3])

        raw_router = sb("raw_router", [P, E])
        ln1 = sb("ln1", [P, 1])
        ln2 = sb("ln2", [P, 1])
        ap_sb = sb("ap_sb", [P, RC])
        ap_half = sb("ap_half", [P, RC])
        NREC = 3 * RC
        w_hi = sb("w_hi", [P, NREC + 2 * IC, P], F32R)
        w_lo = sb("w_lo", [P, NREC + 2 * IC, P], F32R)
        wout_t = sb("wout_t", [P, RC, P])
        wdown_t = sb("wdown_t", [P, IC, P])
        sh_hi = sb("sh_hi", [P, 2, SC * P], F32R)
        sh_lo = sb("sh_lo", [P, 2, SC * P], F32R)
        sd_sb = sb("sd_sb", [P, SC, P])
        rt_w = sb("rt_w", [P, 2 * E], F32R)
        up_hi = sb("up_hi", [P, E, 2 * I], F32R)
        up_lo = sb("up_lo", [P, E, 2 * I], F32R)
        wd_sb = sb("wd_sb", [P, E, EC * P])

        mv = sb("mv", [P, NT, 2])
        std = sb("std", [P, NT])
        rstd = sb("rstd", [P, NT])
        msq = sb("msq", [P, NT])
        rms1 = sb("rms1", [P, NT])
        r1 = sb("r1", [P, NT])
        part_hi = sb("part_hi", [P, BLK], F32R)
        part_lo = sb("part_lo", [P, BLK], F32R)

        m1 = sb("m1", [P, NT])
        m2 = sb("m2", [P, NT])
        best = sb("best", [P, NT])
        gap = sb("gap", [P, NT])
        egap = sb("egap", [P, NT])
        esum = sb("esum", [P, NT])
        p1 = sb("p1", [P, NT])
        p2 = sb("p2", [P, NT])
        total = sb("total", [P, E])
        total_i = sb("total_i", [P, E], I32)
        tiles_i = sb("tiles_i", [P, E], I32)
        tiles = sb("tiles", [P, E])
        tiles_to = sb("tiles_to", [P, E])
        tiles_from = sb("tiles_from", [P, E])
        slot_f = sb("slot_f", [P, 2, NT])
        slot_i = sb("slot_i", [P, 2, NT], I32)
        expert_f = sb("expert_f", [P, TILES])
        expert_i = sb("expert_i", [P, TILES], I32)

        h_tok = sb("h_tok", [P, BT, P])
        hT_hi = sb("hT_hi", [P, BLK], F32R)
        hT_lo = sb("hT_lo", [P, BLK], F32R)
        rec_room = sb("rec_room", [P, 3 * RC * BLK])
        x_in, t_gate, t_decay = (
            rec_room[:, n * RC * BLK : (n + 1) * RC * BLK].rearrange("p (c t) -> p c t", c=RC) for n in range(3)
        )
        act_room = sb("act_room", [P, (2 + IC + SC) * BLK])
        silu_b, mlp_act, sh_act = (
            act_room[:, a * BLK : b * BLK].rearrange("p (c t) -> p c t", t=BLK)
            for a, b in ((0, 2), (2, 2 + IC), (2 + IC, 2 + IC + SC))
        )
        decay = sb("decay", [P, RC, BLK])
        state = sb("state", [P, RC, BLK])
        square = rest = root = t_decay
        feed = x_in
        y = t_gate
        zeros = state[:, :, :].rearrange("p a b -> p (a b)")
        carry = sb("carry", [P, RC])
        results = sb("results", [P, 2 * NT * P])
        s_tok = results[:, 0 : NT * P].rearrange("p (t d) -> p t d", d=P)
        shared = results[:, NT * P :].rearrange("p (t d) -> p t d", d=P)
        raw_up = results[:, 2 * NT * P - E * 2 * I :].rearrange("p (e i) -> p e i", e=E)
        ssq = sb("ssq", [P, BT])
        rms2 = sb("rms2", [P, BT])
        r2 = sb("r2", [P, BT])
        h2_tok = sb("h2_tok", [P, BT, P])
        squares = h2_tok
        h2_hi = sb("h2_hi", [P, BLK], F32R)
        h2_lo = sb("h2_lo", [P, BLK], F32R)

        x_tile = sh_act[:, :, :].rearrange("p a b -> p (a b)")[:, 0 : 4 * P].rearrange("p (k d) -> p k d", d=P)
        xe_hi = h2_hi[:, 0 : 2 * P].rearrange("p (k d) -> p k d", d=P)
        xe_lo = h2_lo[:, 0 : 2 * P].rearrange("p (k d) -> p k d", d=P)
        mlp_flat = mlp_act[:, :, :].rearrange("p a b -> p (a b)")
        silu_e = mlp_flat[:, 0 : 2 * I].rearrange("p (k d) -> p k d", k=2)
        actT = mlp_flat[:, 2 * I : 2 * I + 2 * EC * P].rearrange("p (k d) -> p k d", k=2)
        y_tile = mlp_flat[:, 2 * I + 2 * EC * P : 2 * I + (2 * EC + 4) * P].rearrange("p (k d) -> p k d", d=P)
        act_e = sb("act_e", [P, 2, EC * P])

        def carve(base, at, shape):
            size = 1
            for n in shape[1:]:
                size *= n
            flat = base[:, at[0] : at[0] + size]
            at[0] += size
            assert at[0] <= base.shape[1]
            if len(shape) == 2:
                return flat
            if len(shape) == 3:
                return flat.rearrange("p (a b) -> p a b", b=shape[2])
            assert len(shape) == 5
            return flat.rearrange("p (a b c d) -> p a b c d", b=shape[2], c=shape[3], d=shape[4])

        rec_raw = [0]
        raw_rec = carve(rec_room, rec_raw, [P, 2 * RC, P])
        raw_a = carve(rec_room, rec_raw, [P, RC, REC])
        raw_out = carve(rec_room, rec_raw, [P, REC])
        raw_down = carve(rec_room, rec_raw, [P, INTER])
        wa_t = carve(rec_room, rec_raw, [P, RC, REC])
        act_raw = [0]
        raw_mlp = carve(act_room, act_raw, [P, 2 * IC, P])
        raw_shared = carve(act_room, act_raw, [P, 2, SC * P])
        scaled = carve(act_room, act_raw, [P, NREC + 2 * IC, P])

        room = sb("room", [P, ROOM])
        early = [0]
        rank_of = carve(room, early, [P, NT, E])
        tile_no = carve(room, early, [P, TILES, E])
        restart = carve(room, early, [P, E, NT])
        st6 = carve(room, early, [P, NT, 6])
        routing = [early[0]]
        x_sb = carve(room, early, [P, NT, P])
        lg = carve(room, routing, [P, NT, 2 * E])
        logit = carve(room, routing, [P, NT, E])
        first = carve(room, routing, [P, NT, E])
        second = carve(room, routing, [P, NT, E])
        scratch = carve(room, routing, [P, NT, E])
        chosen = carve(room, routing, [P, E, NT])
        count = carve(room, routing, [P, E, NT])
        steps = carve(room, routing, [P, E, NT])
        offset = carve(room, routing, [P, E, NT])
        slot = carve(room, routing, [P, E, NT])
        passed = carve(room, routing, [P, TILES, E])
        late = [0]
        got = carve(room, late, [P, 2, 2, BT, P])
        half_sum = carve(room, late, [P, 2, BLK])
        fin = carve(room, late, [P, 2, BLK])
        x_back = carve(room, late, [P, 2, BLK])
        silu_f = fin
        gated = half_sum

        x_loaded = [sem(f"x_loaded{n}") for n in range(4)]
        rec_loaded = sem("rec_loaded")
        small_loaded = sem("small_loaded")
        mlp_loaded = sem("mlp_loaded")
        shared_loaded = sem("shared_loaded")
        up_loaded = sem("up_loaded")
        down_loaded = sem("down_loaded")
        zeroed = sem("zeroed")
        pads_ready = sem("pads_ready")
        zeros_ready = sem("zeros_ready")
        consts_ready = sem("consts_ready")
        const_step = sem("const_step")
        stats_done = sem("stats_done")
        std_done = sem("std_done")
        msq_done = sem("msq_done")
        rms1_done = sem("rms1_done")
        xn_done = sem("xn_done")
        normal_done = sem("normal_done")
        x_tok_done = sem("x_tok_done")
        rstd_done = sem("rstd_done")
        wT_done = sem("wT_done")
        wT_taken = sem("wT_taken")
        waT_done = sem("waT_done")
        scaled_done = sem("scaled_done")
        w_hi_done = sem("w_hi_done")
        w_lo_done = sem("w_lo_done")
        shared_split = sem("shared_split")
        router_split = sem("router_split")
        waT_taken = sem("waT_taken")
        tiny_ready = sem("tiny_ready")
        stats_step = sem("stats_step")
        feed_done = sem("feed_done")
        scan_done = sem("scan_done")
        carry_done = sem("carry_done")
        r2_done = sem("r2_done")
        half_done = sem("half_done")
        product_done = sem("product_done")
        up_hi_done = sem("up_hi_done")
        up_lo_done = sem("up_lo_done")
        xT_done = sem("xT_done")
        xT_hi_done = sem("xT_hi_done")
        xT_lo_done = sem("xT_lo_done")
        logits_done = sem("logits_done")
        route_step = sem("route_step")
        gap_done = sem("gap_done")
        egap_done = sem("egap_done")
        chosen_done = sem("chosen_done")
        ranks_done = sem("ranks_done")
        slots_known = sem("slots_known")
        experts_known = sem("experts_known")
        scattered = sem("scattered")

        h_done = sem("h_done")
        hT_done = sem("hT_done")
        hT_hi_done = sem("hT_hi_done")
        hT_lo_done = sem("hT_lo_done")
        pair_done = sem("pair_done")
        t_decay_done = sem("t_decay_done")
        decay_done = sem("decay_done")
        square_done = sem("square_done")
        rest_done = sem("rest_done")
        x_in_done = sem("x_in_done")
        t_gate_done = sem("t_gate_done")
        root_done = sem("root_done")
        y_done = sem("y_done")
        proj_done = sem("proj_done")
        mid_done = sem("mid_done")
        ssq_done = sem("ssq_done")
        rms2_done = sem("rms2_done")
        h2_done = sem("h2_done")
        h2T_done = sem("h2T_done")
        h2_hi_done = sem("h2_hi_done")
        h2_lo_done = sem("h2_lo_done")
        silu_done = sem("silu_done")
        sh_act_done = sem("sh_act_done")
        mlp_act_done = sem("mlp_act_done")
        sh_out_done = sem("sh_out_done")
        shared_done = sem("shared_done")
        mlp_out_done = sem("mlp_out_done")
        s_done = sem("s_done")

        tile_loaded = [sem(f"tile_loaded{i}") for i in range(4)]
        eT_done = sem("eT_done")
        e_hi_done = sem("e_hi_done")
        e_lo_done = sem("e_lo_done")
        e_up_done = sem("e_up_done")
        e_silu_done = sem("e_silu_done")
        e_act_done = sem("e_act_done")
        e_actT_done = sem("e_actT_done")
        e_copy_done = sem("e_copy_done")
        e_down_done = sem("e_down_done")
        e_out_done = sem("e_out_done")
        tile_stored = [sem(f"tile_stored{i}") for i in range(4)]
        gathered = [sem(f"gathered{i}") for i in range(2)]
        x_again = [sem(f"x_again{i}") for i in range(2)]
        summed = sem("summed")
        silu_f_done = sem("silu_f_done")
        gated_done = sem("gated_done")
        out_stored = [sem(f"out_stored{i}") for i in range(2)]

        GROUPS = [(0, 2 * RC), (2 * RC, NREC), (NREC, NREC + IC), (NREC + IC, NREC + 2 * IC)]
        ranks_ps = pair[2][:, 0, 0 : E * NT]
        counts_ps = pair[2][:, 1, 0 : E * NT]
        PAIRS = 3 + SC + IC
        assert PAIRS % 3 == 0

        block = ctx.enter_context(nc.Block())

        @block.sync
        def _(sp):
            for n in range(4):
                sp.dma_start(x_sb[:, n * QT : (n + 1) * QT, :], xt[:, n * QT : (n + 1) * QT, :]).then_inc(
                    x_loaded[n], 16
                )
            sp.dma_start(raw_rec[:, 0:RC, :], w_in.rearrange("(c p) h -> p c h", p=P)).then_inc(rec_loaded, 16)
            sp.dma_start(raw_rec[:, RC:, :], w_gate.rearrange("(c p) h -> p c h", p=P)).then_inc(rec_loaded, 16)
            sp.dma_start(raw_a[:, :, :], w_a.rearrange("(c p) h -> p c h", p=P)).then_inc(rec_loaded, 16)
            sp.dma_start(raw_out[:, :], w_out).then_inc(rec_loaded, 16)
            sp.dma_start(raw_down[:, :], w_mlp_down).then_inc(rec_loaded, 16)
            sp.dma_start(raw_mlp[:, 0:IC, :], w_mlp_gate.rearrange("(c p) h -> p c h", p=P)).then_inc(mlp_loaded, 16)
            sp.dma_start(raw_mlp[:, IC:, :], w_mlp_up.rearrange("(c p) h -> p c h", p=P)).then_inc(mlp_loaded, 16)
            sp.dma_start(raw_router[:, :], gate_w).then_inc(small_loaded, 16)
            sp.dma_start(ln1[:, :], ln1_w.rearrange("(p o) -> p o", o=1)).then_inc(small_loaded, 16)
            sp.dma_start(ln2[:, :], ln2_w.rearrange("(p o) -> p o", o=1)).then_inc(small_loaded, 16)
            for c in range(RC):
                sp.dma_start(ap_sb[:, c : c + 1], a_param[c * P : (c + 1) * P].rearrange("(p o) -> p o", o=1)).then_inc(
                    small_loaded, 16
                )
            sp.wait_ge(pads_ready, 4)
            sp.dma_start(raw_shared[:, 0, 0:IS], Sg).then_inc(shared_loaded, 16)
            sp.dma_start(raw_shared[:, 1, 0:IS], Su).then_inc(shared_loaded, 16)
            sp.dma_start(sd_sb[:, 0, :], Sd[0:P, :]).then_inc(shared_loaded, 16)
            sp.dma_start(sd_sb[0 : IS - P, 1, :], Sd[P:IS, :]).then_inc(shared_loaded, 16)
            sp.dma_start(raw_up[:, :, 0:I], Wg.rearrange("e h i -> h e i")).then_inc(up_loaded, 16)
            sp.dma_start(raw_up[:, :, I:], Wu.rearrange("e h i -> h e i")).then_inc(up_loaded, 16)
            for c in range(EC):
                n = min(P, I - c * P)
                sp.dma_start(
                    wd_sb[0:n, :, c * P : (c + 1) * P], Wd[:, c * P : c * P + n, :].rearrange("e i h -> i e h")
                ).then_inc(down_loaded, 16)
            sp.wait_ge(zeros_ready, 1)
            flat = slots.rearrange("(p n) d -> p (n d)", p=P)
            for c in range(0, SLOTS, ZW):
                n = min(ZW, SLOTS - c)
                sp.dma_start(flat[:, c : c + n], zeros[:, 0:n]).then_inc(zeroed, 16)

            def load_tile(i, j):
                sp.dma_start(x_tile[:, j % 4, :], slots[bass.ds((i * 4 + j) * P, P), :]).then_inc(
                    tile_loaded[j % 4], 16
                )

            def store_tile(i, j):
                sp.wait_ge(e_out_done, i * 4 + (j + 4))
                sp.dma_start(moved[bass.ds((i * 4 + j) * P, P), :], y_tile[:, j % 4, :]).then_inc(
                    tile_stored[j % 4], 16
                )

            sp.wait_ge(scattered, 16 * 2 * NT)
            sp.wait_ge(s_done, HALF + 1)
            for j in range(4):
                load_tile(0, j)
            for j in range(4):
                sp.wait_ge(eT_done, j + 1)
                load_tile(1, j)
            with sp.Fori(2, TILES // 4) as i:
                for j in range(4):
                    sp.wait_ge(eT_done, i * 4 + (j - 3))
                    load_tile(i, j)
                    store_tile(i - 2, j)
            for t in range(TILES - TILES % 4, TILES):
                sp.wait_ge(eT_done, t - 3)
                load_tile(0, t)
            for t in range(TILES - TILES % 4 - 8, TILES):
                store_tile(0, t)
            def load_x(i, k):
                sp.dma_start(x_back[:, k, :].rearrange("p (t d) -> p t d", d=P),
                             xt[:, bass.ds((i * 2 + k) * BT, BT), :]).then_inc(x_again[k], 16)

            def store(i, k):
                sp.wait_ge(gated_done, i * 2 + (k + 1))
                sp.dma_start(ot[:, bass.ds((i * 2 + k) * BT, BT), :],
                             gated[:, k, :].rearrange("p (t d) -> p t d", d=P)).then_inc(out_stored[k], 16)

            load_x(0, 0)
            load_x(0, 1)
            with sp.Fori(0, NB // 2 - 1) as i:
                for k in range(2):
                    store(i, k)
                    load_x(i + 1, k)
            for k in range(2):
                store(NB // 2 - 1, k)
            for k in range(2):
                sp.wait_ge(out_stored[k], 16 * (NB // 2))

        @block.gpsimd
        def _(pool):
            pool.memset(zeros[:, :], 0.0).then_inc(zeros_ready, 1)
            pool.memset(ident[:, :], 0.0).then_inc(const_step, 1)
            pool.memset(ones[:, :], 1.0).then_inc(const_step, 1)
            pool.memset(below[:, :], 1.0).then_inc(const_step, 1)
            pool.memset(rank_of[:, :, :], 0.0).then_inc(const_step, 1)
            pool.memset(raw_shared[:, :, IS:], 0.0).then_inc(pads_ready, 1)
            pool.memset(sd_sb[:, 1, :], 0.0).then_inc(pads_ready, 1)
            pool.memset(wd_sb[:, :, (EC - 1) * P :], 0.0).then_inc(pads_ready, 1)
            pool.memset(act_e[:, :, I:], 0.0).then_inc(pads_ready, 1)
            pool.wait_ge(const_step, 4)
            pool.affine_select(
                out=ident[:, :], in_=ident[:, :], compare_op=ALU.not_equal, fill=1.0, base=0,
                pattern=[[-1, P]], channel_multiplier=1,
            ).then_inc(consts_ready, 1)
            pool.affine_select(
                out=below[:, :], in_=below[:, :], compare_op=ALU.is_gt, fill=0.0, base=0,
                pattern=[[1, P]], channel_multiplier=-1,
            ).then_inc(consts_ready, 1)
            pool.iota(rank_of[:, :, :], pattern=[[0, NT], [-1, E]], base=E, channel_multiplier=0,
                      allow_small_or_imprecise_dtypes=True).then_inc(consts_ready, 1)
            pool.iota(tile_no[:, :, :], pattern=[[1, TILES], [0, E]], base=0, channel_multiplier=0,
                      allow_small_or_imprecise_dtypes=True).then_inc(consts_ready, 1)
            pool.memset(restart[:, :, :], 1.0).then_inc(const_step, 1)
            pool.memset(keep[:, :], 0.0).then_inc(const_step, 1)
            pool.wait_ge(const_step, 6)
            pool.memset(restart[:, :, 0:1], 0.0).then_inc(consts_ready, 1)
            pool.memset(keep[:, 1 : NB : 2], 1.0).then_inc(consts_ready, 1)
            for n, (c0, c1) in enumerate(GROUPS):
                pool.wait_ge(w_hi_done, n + 1)
                pool.tensor_tensor(w_lo[:, c0:c1, :], scaled[:, c0:c1, :], w_hi[:, c0:c1, :].bitcast(F32),
                                   ALU.subtract).then_inc(w_lo_done, 1)
            pool.wait_ge(shared_split, 1)
            pool.tensor_tensor(sh_lo[:, :, :], raw_shared[:, :, :], sh_hi[:, :, :].bitcast(F32),
                               ALU.subtract).then_inc(shared_split, 1)
            for e in range(E):
                pool.wait_ge(up_hi_done, e + 1)
                pool.tensor_tensor(up_lo[:, e, :], raw_up[:, e, :], up_hi[:, e, :].bitcast(F32),
                                   ALU.subtract).then_inc(up_lo_done, 1)
            pool.wait_ge(zeroed, 16 * -(-SLOTS // ZW))
            pool.wait_ge(slots_known, 1)
            pool.wait_ge(xn_done, NB)
            for t in range(NT):
                for c in range(2):
                    pool.indirect_dma_start(
                        slots, bass.IndirectOffsetOnAxis(ap=slot_i[:, c, t : t + 1], axis=0), xn[:, t, :], None
                    ).then_inc(scattered, 16)
            for k in range(4):
                pool.wait_ge(tile_stored[k], 16 * -(-(TILES - k) // 4))
            for f in range(NB):
                k = f % 2
                if f >= 2:
                    pool.wait_ge(summed, f - 1)
                for t in range(BT):
                    for c in range(2):
                        pool.indirect_dma_start(
                            got[:, k, c, t, :], None, moved,
                            bass.IndirectOffsetOnAxis(ap=slot_i[:, c, f * BT + t : f * BT + t + 1], axis=0),
                        ).then_inc(gathered[k], 16)

        @block.tensor
        def _(pe):
            def split_product(dst, c_hi, c_lo, m_hi, m_lo):
                pe.matmul(dst, c_hi, m_hi, start=True, stop=False)
                pe.matmul(dst, c_lo, m_hi, start=False, stop=False)
                return pe.matmul(dst, c_hi, m_lo, start=False, stop=True)

            pe.wait_ge(consts_ready, 1)
            pe.wait_ge(rec_loaded, 16 * 5)
            banks = [pair[0][:, 0, :], pair[0][:, 1, :], pair[1][:, 0, :], pair[1][:, 1, :]]
            for c in range(RC):
                for j in range(RC):
                    last = pe.transpose(pair[2][:, 0, (j * RC + c) * P : (j * RC + c + 1) * P],
                                        raw_a[:, c, j * P : (j + 1) * P], ident[:, :])
            last.then_inc(waT_done, 1)
            for c in range(2 * RC):
                last = pe.transpose(banks[0][:, c * P : (c + 1) * P], raw_rec[:, c, :], ident[:, :])
            last.then_inc(wT_done, 1)
            for c in range(RC):
                last = pe.transpose(banks[1][:, c * P : (c + 1) * P], raw_out[:, c * P : (c + 1) * P], ident[:, :])
            last.then_inc(wT_done, 1)
            for c in range(IC):
                last = pe.transpose(banks[2][:, c * P : (c + 1) * P], raw_down[:, c * P : (c + 1) * P], ident[:, :])
            last.then_inc(wT_done, 1)
            pe.wait_ge(waT_taken, 1)
            for j in range(RC):
                last = pe.matmul(banks[3][:, 0:REC], raw_rec[:, j, :], wa_t[:, j, :], start=(j == 0), stop=(j == RC - 1))
            last.then_inc(wT_done, 1)
            def turn_x(i, j):
                pe.wait_ge(normal_done, i * 2 + (j + 1))
                if not (isinstance(i, int) and i * 2 + j < 2):
                    pe.wait_ge(xT_lo_done, i * 2 + (j - 1))
                for k in range(BT):
                    last = pe.transpose((turned, bytok)[j % 2][:, k * P : (k + 1) * P],
                                        (h_tok, h2_tok)[j % 2][:, k, :], ident[:, :])
                last.then_inc(xT_done, 1)

            logits_ps = pair[2][:, 1, :].rearrange("p (t e) -> p t e", e=2 * E)

            def logits(i, j):
                pe.wait_ge(xT_lo_done, i * 2 + (j + 1))
                hi, lo = ((part_hi, part_lo), (hT_hi, hT_lo))[j % 2]
                for k in range(BT):
                    dst = logits_ps[:, (i * 2 + j) * BT + k, :]
                    pe.matmul(dst, hi[:, k * P : (k + 1) * P], rt_w[:, :], start=True, stop=False)
                    last = pe.matmul(dst, lo[:, k * P : (k + 1) * P], rt_w[:, :], start=False, stop=True)
                last.then_inc(logits_done, 1)

            pe.wait_ge(router_split, 2)
            turn_x(0, 0)
            turn_x(0, 1)
            with pe.Fori(0, NB // 2 - 1) as i:
                for j in range(2):
                    logits(i, j)
                    turn_x(i, j + 2)
            logits(0, NB - 2)
            logits(0, NB - 1)

            pe.wait_ge(mlp_loaded, 32)
            pe.wait_ge(wT_taken, 4)
            for half in range(2):
                for c in range(IC):
                    last = pe.transpose(banks[half][:, c * P : (c + 1) * P], raw_mlp[:, half * IC + c, :], ident[:, :])
                last.then_inc(wT_done, 1)

            def turn_h(b):
                pe.wait_ge(h_done, b + 1)
                for k in range(BT):
                    last = pe.transpose(turned[:, k * P : (k + 1) * P], h_tok[:, k, :], ident[:, :])
                last.then_inc(hT_done, 1)

            def rec_pair(n, b=None):
                first_chunk = (2 * RC, 0, RC)[n]
                if b is not None:
                    pe.wait_ge(mlp_act_done, b * IC + (n + 2 - IC))
                for c in range(RC):
                    w = first_chunk + c
                    last = split_product(pair[n][:, c, :], w_hi[:, w, :], w_lo[:, w, :], hT_hi[:, :], hT_lo[:, :])
                last.then_inc(pair_done, 1)

            def project(b):
                pe.wait_ge(y_done, b + 1)
                if not (isinstance(b, int) and b == 0):
                    pe.wait_ge(shared_done, b)
                for c in range(RC):
                    for k in range(BT):
                        last = pe.matmul(bytok[:, k * P : (k + 1) * P], y[:, c, k * P : (k + 1) * P], wout_t[:, c, :],
                                         start=(c == 0 and k == 0), stop=(c == RC - 1), skip_group_check=True)
                last.then_inc(proj_done, 1)

            def turn_block_x(b):
                pe.wait_ge(x_tok_done, b + 1)
                for k in range(BT):
                    last = pe.transpose(turned[:, k * P : (k + 1) * P], h_tok[:, k, :], ident[:, :])
                last.then_inc(xT_done, 1)

            def shared_up(b, ahead):
                pe.wait_ge(xT_lo_done, b + (NB + 1))
                for c in range(SC):
                    pe.wait_ge((t_decay_done, x_in_done)[c], b + 1 + ahead)
                    for g in range(2):
                        last = split_product(pair[c][:, g, :], sh_hi[:, g, c * P : (c + 1) * P],
                                             sh_lo[:, g, c * P : (c + 1) * P], part_hi[:, :], part_lo[:, :])
                    last.then_inc(pair_done, 1)

            def turn_h2(b):
                pe.wait_ge(h2_done, b + 1)
                for k in range(BT):
                    last = pe.transpose(turned[:, k * P : (k + 1) * P], h2_tok[:, k, :], ident[:, :])
                last.then_inc(h2T_done, 1)

            def shared_down(b):
                pe.wait_ge(sh_act_done, b * SC + SC)
                pe.wait_ge(s_done, b + 1)
                for c in range(SC):
                    for k in range(BT):
                        last = pe.matmul(bytok[:, k * P : (k + 1) * P], sh_act[:, c, k * P : (k + 1) * P],
                                         sd_sb[:, c, :], start=(c == 0 and k == 0), stop=(c == SC - 1),
                                         skip_group_check=True)
                last.then_inc(sh_out_done, 1)

            def mlp_up(b, ahead):
                pe.wait_ge(h2_lo_done, b + 1)
                for j in range(IC):
                    if j == 0:
                        pe.wait_ge(t_gate_done, b + 1 + ahead)
                    if j == IC - 1:
                        pe.wait_ge(mlp_act_done, b * IC + 1)
                    for g in range(2):
                        w = NREC + g * IC + j
                        last = split_product(pair[(SC + j) % 3][:, g, :], w_hi[:, w, :], w_lo[:, w, :],
                                             h2_hi[:, :], h2_lo[:, :])
                    last.then_inc(pair_done, 1)

            def mlp_down(b, alone=False):
                pe.wait_ge(mlp_act_done, b * IC + IC)
                if alone:
                    pe.wait_ge(shared_done, b + 1)
                else:
                    pe.wait_ge(mid_done, b + 2)
                for j in range(IC):
                    for k in range(BT):
                        last = pe.matmul(bytok[:, k * P : (k + 1) * P], mlp_act[:, j, k * P : (k + 1) * P],
                                         wdown_t[:, j, :], start=(j == 0 and k == 0), stop=(j == IC - 1),
                                         skip_group_check=True)
                last.then_inc(mlp_out_done, 1)

            def run_block(b, ahead=1, before=1):
                if ahead:
                    turn_h(b + 1)
                project(b)
                after = b if before else None
                if ahead:
                    pe.wait_ge(hT_lo_done, b + 2)
                    rec_pair(0, after)
                    rec_pair(1, after)
                turn_block_x(b)
                if ahead:
                    rec_pair(2, after)
                shared_up(b, ahead)
                if before:
                    mlp_down(b - 1)
                turn_h2(b)
                shared_down(b)
                mlp_up(b, ahead)

            pe.wait_ge(w_lo_done, 4)
            turn_h(0)
            pe.wait_ge(hT_lo_done, 1)
            rec_pair(0)
            rec_pair(1)
            every = chosen[:, :, :].rearrange("p e t -> p (e t)")
            pe.wait_ge(chosen_done, 1)
            pe.matmul(ranks_ps, below[:, :], every, start=True, stop=True)
            pe.matmul(counts_ps, ones[:, :], every, start=True, stop=True).then_inc(ranks_done, 1)
            pe.wait_ge(slots_known, 1)
            rec_pair(2)
            pe.wait_ge(shared_split, 2)
            run_block(0, before=0)
            with pe.Fori(1, HALF) as b:
                run_block(b)
            mlp_down(HALF - 1, alone=True)

            def e_turn(i, j):
                pe.wait_ge(tile_loaded[j % 4], i * 16 + (j // 4 + 1) * 16)
                pe.transpose(turned[:, 0:P], x_tile[:, j % 4, :], ident[:, :]).then_inc(eT_done, 1)

            expert_regs = [pe.alloc_register(f"expert{k}") for k in range(4)]

            hi_flat = up_hi[:, :, :].rearrange("p e i -> p (e i)")
            lo_flat = up_lo[:, :, :].rearrange("p e i -> p (e i)")
            wd_flat = wd_sb[:, :, :].rearrange("p e i -> p (e i)")

            def e_up(i, j, turn_next=True):
                pe.reg_load(expert_regs[j % 4], expert_i[0:1, bass.ds(i * 4 + j, 1)])
                e = pe.snap(expert_regs[j % 4], min_val=0, max_val=E - 1)
                pe.wait_ge(e_lo_done, i * 4 + (j + 1))
                if turn_next:
                    e_turn(i, j + 1)
                for g in range(2):
                    dst = pair[j % 2][:, g, 0:I]
                    hi = hi_flat[:, bass.ds(e * (2 * I) + g * I, I)]
                    lo = lo_flat[:, bass.ds(e * (2 * I) + g * I, I)]
                    pe.matmul(dst, xe_hi[:, j % 2, :], hi, start=True, stop=False)
                    pe.matmul(dst, xe_hi[:, j % 2, :], lo, start=False, stop=False)
                    last = pe.matmul(dst, xe_lo[:, j % 2, :], hi, start=False, stop=True)
                last.then_inc(e_up_done, 1)

            def e_turn_act(i, j):
                pe.wait_ge(e_act_done, i * 4 + (j + 2))
                for c in range(EC):
                    last = pe.transpose(pair[2][:, 0, c * P : (c + 1) * P], act_e[:, j % 2, c * P : (c + 1) * P],
                                        ident[:, :])
                last.then_inc(e_actT_done, 1)

            def e_down(i, j):
                e = pe.snap(expert_regs[j % 4], min_val=0, max_val=E - 1)
                pe.wait_ge(e_copy_done, i * 4 + (j + 3))
                pe.wait_ge(e_out_done, i * 4 + (j + 3))
                for c in range(EC):
                    last = pe.matmul(pair[2][:, 1, 0:P], actT[:, j % 2, c * P : (c + 1) * P],
                                     wd_flat[:, bass.ds(e * (EC * P) + c * P, P)], start=(c == 0), stop=(c == EC - 1))
                last.then_inc(e_down_done, 1)

            pe.wait_ge(s_done, HALF + 1)
            pe.wait_ge(experts_known, 1)
            pe.wait_ge(up_lo_done, E)
            pe.wait_ge(down_loaded, 16 * EC)
            e_turn(0, 0)
            e_up(0, 0)
            e_up(0, 1)
            e_turn_act(0, 0)

            def e_step(i, j):
                e_up(i, j + 1)
                e_down(i, j - 1)
                e_turn_act(i, j)

            for j in range(1, 4):
                e_step(0, j)
            with pe.Fori(1, (TILES - 3) // 4) as i:
                for j in range(4):
                    e_step(i, j)
            for t in range(TILES - 3, TILES):
                if t + 1 < TILES:
                    e_up(0, t + 1, turn_next=t + 2 < TILES)
                e_down(0, t - 1)
                e_turn_act(0, t)
            e_down(0, TILES - 1)

            pe.wait_ge(e_out_done, TILES + 3)
            run_block(HALF, before=0)
            with pe.Fori(HALF + 1, NB - 1) as b:
                run_block(b)
            run_block(NB - 1, ahead=0)
            mlp_down(NB - 1, alone=True)

        @block.scalar
        def _(act):
            act.wait_ge(tiny_ready, 3)
            for n in range(2):
                act.wait_ge(stats_done, n + 1)
                half = slice(n * NT // 2, (n + 1) * NT // 2)
                act.activation(std[:, half], mv[:, half, 1], ACT.Sqrt, bias=tiny[:, 0:1]).then_inc(std_done, 1)
            act.wait_ge(msq_done, 1)
            act.activation(rms1[:, :], msq[:, :], ACT.Sqrt, bias=tiny[:, 1:2]).then_inc(rms1_done, 1)

            act.wait_ge(waT_done, 1)
            act.activation(wa_t[:, :, :].rearrange("p a b -> p (a b)"), pair[2][:, 0, 0 : RC * REC],
                           ACT.Copy).then_inc(waT_taken, 1)
            act.wait_ge(wT_done, 1)
            act.wait_ge(small_loaded, 16 * (3 + RC))
            act.activation(scaled[:, 0 : 2 * RC, :].rearrange("p a b -> p (a b)"), pair[0][:, 0, :], ACT.Copy,
                           scale=ln1[:, 0:1]).then_inc(wT_taken, 1)

            def x_hi(i, j):
                act.wait_ge(xT_done, i * 2 + (j + 1))
                if not (isinstance(i, int) and i * 2 + j < 2):
                    act.wait_ge(logits_done, i * 2 + (j - 1))
                act.activation((part_hi, hT_hi)[j % 2][:, :], (turned, bytok)[j % 2][:, :], ACT.Copy).then_inc(
                    xT_hi_done, 1
                )
                act.activation(xn[:, bass.ds((i * 2 + j) * BT, BT), :], (h_tok, h2_tok)[j % 2][:, :, :],
                               ACT.Copy).then_inc(xn_done, 1)

            x_hi(0, 0)
            x_hi(0, 1)
            with act.Fori(0, NB // 2 - 1) as i:
                for j in range(2, 4):
                    x_hi(i, j)
            act.activation(w_hi[:, 0 : 2 * RC, :], scaled[:, 0 : 2 * RC, :], ACT.Copy).then_inc(w_hi_done, 1)
            act.wait_ge(wT_done, 4)
            act.activation(scaled[:, 2 * RC : NREC, :].rearrange("p a b -> p (a b)"), pair[1][:, 1, 0:REC], ACT.Copy,
                           scale=ln1[:, 0:1]).then_inc(wT_taken, 1)
            act.activation(wout_t[:, :, :].rearrange("p a b -> p (a b)"), pair[0][:, 1, 0:REC], ACT.Copy,
                           scale=0.5).then_inc(wT_taken, 1)
            act.activation(wdown_t[:, :, :].rearrange("p a b -> p (a b)"), pair[1][:, 0, :], ACT.Copy).then_inc(
                wT_taken, 1
            )
            act.wait_ge(wT_taken, 4)
            act.activation(w_hi[:, 2 * RC : NREC, :], scaled[:, 2 * RC : NREC, :], ACT.Copy).then_inc(w_hi_done, 1)
            act.wait_ge(gap_done, 1)
            act.activation(egap[:, :], gap[:, :], ACT.Exp).then_inc(egap_done, 1)
            for half in range(2):
                c0, c1 = GROUPS[2 + half]
                act.wait_ge(wT_done, 5 + half)
                act.activation(scaled[:, c0:c1, :].rearrange("p a b -> p (a b)"), pair[0][:, half, :], ACT.Copy,
                               scale=ln2[:, 0:1]).then_inc(scaled_done, 1)
                act.wait_ge(scaled_done, half + 1)
                act.activation(w_hi[:, c0:c1, :], scaled[:, c0:c1, :], ACT.Copy).then_inc(w_hi_done, 1)
            act.wait_ge(shared_loaded, 64)
            act.activation(sh_hi[:, :, :], raw_shared[:, :, :], ACT.Copy).then_inc(shared_split, 1)

            def h_hi(b):
                act.wait_ge(hT_done, b + 1)
                act.activation(hT_hi[:, :], turned[:, :], ACT.Copy).then_inc(hT_hi_done, 1)

            def rec_decay(b, q):
                act.wait_ge(pair_done, q + 1)
                for c in range(RC):
                    last = act.activation(t_decay[:, c, :], pair[0][:, c, :], ACT.Tanh, bias=ap_half[:, c : c + 1],
                                          scale=0.5)
                last.then_inc(t_decay_done, 1)

            def rec_square(b):
                act.wait_ge(decay_done, b + 1)
                act.activation(square[:, :, :], decay[:, :, :], ACT.Square).then_inc(square_done, 1)

            def rec_x_in(q):
                act.wait_ge(pair_done, q + 2)
                act.activation(x_in[:, :, :], pair[1][:, :, :], ACT.Copy).then_inc(x_in_done, 1)

            def rec_gate(q):
                act.wait_ge(pair_done, q + 3)
                act.activation(t_gate[:, :, :], pair[2][:, :, :], ACT.Tanh, scale=0.5).then_inc(t_gate_done, 1)

            def rec_root(b):
                act.wait_ge(rest_done, b + 1)
                act.activation(root[:, :, :], rest[:, :, :], ACT.Sqrt, bias=tiny[:, 2:3]).then_inc(root_done, 1)

            def mid_squares(b):
                act.wait_ge(mid_done, b + 1)
                for k in range(BT):
                    act.activation(squares[:, k, :], s_tok[:, b * BT + k, :], ACT.Square,
                                   accum_out=ssq[:, k : k + 1]).then_inc(ssq_done, 1)

            def mid_root(b):
                act.wait_ge(ssq_done, b * BT + BT)
                act.activation(rms2[:, :], ssq[:, :], ACT.Sqrt, bias=tiny[:, 1:2], scale=1.0 / H).then_inc(rms2_done, 1)

            def block_x_hi(b):
                act.wait_ge(xT_done, b + (NB + 1))
                act.activation(part_hi[:, :], turned[:, :], ACT.Copy).then_inc(xT_hi_done, 1)

            def take_silu(b, n, q):
                act.wait_ge(pair_done, q + 1)
                if n >= 2 + SC:
                    act.wait_ge(mlp_act_done, b * IC + (n - 2 - SC + 1))
                elif n >= 2:
                    act.wait_ge(sh_act_done, b * SC + (n - 2 + 1))
                act.activation(silu_b[:, n % 2, :], pair[n % 3][:, 0, :], ACT.Silu).then_inc(silu_done, 1)

            def run_block(b, ahead=1):
                q = b * PAIRS + 3
                if ahead:
                    h_hi(b + 1)
                mid_squares(b)
                if ahead:
                    rec_decay(b + 1, q)
                block_x_hi(b)
                if ahead:
                    rec_x_in(q)
                    rec_square(b + 1)
                    rec_gate(q)
                mid_root(b)
                if ahead:
                    rec_root(b + 1)
                for n in range(SC):
                    take_silu(b, n, q + 3 * ahead + n)
                act.wait_ge(h2T_done, b + 1)
                act.activation(h2_hi[:, :], turned[:, :], ACT.Copy).then_inc(h2_hi_done, 1)
                act.wait_ge(sh_out_done, b + 1)
                if isinstance(b, int) and b == 0:
                    act.wait_ge(up_lo_done, E)
                act.activation(shared[:, bass.ds(b * BT, BT), :].rearrange("p t d -> p (t d)"), bytok[:, :],
                               ACT.Copy).then_inc(shared_done, 1)
                for n in range(SC, SC + IC):
                    take_silu(b, n, q + 3 * ahead + n)

            def silu_final(f, k):
                act.wait_ge(summed, f + 1)
                act.activation(silu_f[:, k, :], fin[:, k, :], ACT.Silu).then_inc(silu_f_done, 1)

            h_hi(0)
            rec_decay(0, 0)
            rec_x_in(0)
            rec_square(0)
            act.wait_ge(up_loaded, 32)
            for e in range(E):
                act.activation(up_hi[:, e, :], raw_up[:, e, :], ACT.Copy).then_inc(up_hi_done, 1)
            rec_gate(0)
            rec_root(0)
            run_block(0)
            with act.Fori(1, HALF) as b:
                run_block(b)

            def e_hi(i, j):
                act.wait_ge(eT_done, i * 4 + (j + 1))
                act.activation(xe_hi[:, j % 2, :], turned[:, 0:P], ACT.Copy).then_inc(e_hi_done, 1)

            def e_silu(i, j):
                act.wait_ge(e_up_done, i * 4 + (j + 1))
                if not (isinstance(i, int) and i * 4 + j < 2):
                    act.wait_ge(e_act_done, i * 4 + j)
                act.activation(silu_e[:, j % 2, :], pair[j % 2][:, 0, 0:I], ACT.Silu).then_inc(e_silu_done, 1)

            def e_copy(i, j):
                act.wait_ge(e_actT_done, i * 4 + (j + 1))
                act.activation(actT[:, j % 2, :], pair[2][:, 0, 0 : EC * P], ACT.Copy).then_inc(e_copy_done, 1)

            e_hi(0, 0)
            e_hi(0, 1)
            e_silu(0, 0)
            e_hi(0, 2)
            e_silu(0, 1)
            e_copy(0, 0)

            def e_step(i, j):
                e_hi(i, j + 2)
                e_silu(i, j + 1)
                e_copy(i, j)

            for j in range(1, 4):
                e_step(0, j)
            with act.Fori(1, (TILES - 3) // 4) as i:
                for j in range(4):
                    e_step(i, j)
            for t in range(TILES - 3, TILES):
                if t + 2 < TILES:
                    e_hi(0, t + 2)
                if t + 1 < TILES:
                    e_silu(0, t + 1)
                e_copy(0, t)

            run_block(HALF)
            silu_final(0, 0)
            with act.Fori(HALF + 1, NB - 1) as b:
                run_block(b)
                for k in range(2):
                    silu_final(b * 2 + (k - 2 * HALF - 1), 1 - k)
            run_block(NB - 1, ahead=0)
            for f in range(NB - 3, NB):
                silu_final(f, f % 2)

        @block.vector
        def _(dve):
            def flat(ap):
                return ap.rearrange("p a b -> p (a b)")

            def each(ap):
                return ap.unsqueeze(2).to_broadcast([P, NT, E])

            dve.memset(tiny[:, 0:1], 1e-5).then_inc(tiny_ready, 1)
            dve.memset(tiny[:, 1:2], 1e-6).then_inc(tiny_ready, 1)
            dve.memset(tiny[:, 2:3], 1e-8).then_inc(tiny_ready, 1)
            for n in range(4):
                dve.wait_ge(x_loaded[n], 16)
                for t in range(n * QT, (n + 1) * QT):
                    dve.bn_stats(st6[:, t, :], x_sb[:, t, :]).then_inc(stats_step, 1)
                dve.wait_ge(stats_step, (n + 1) * QT)
                for t in range(n * QT, (n + 1) * QT):
                    last = dve.bn_aggr(mv[:, t, :], st6[:, t, :])
                if n % 2:
                    last.then_inc(stats_done, 1)
            dve.wait_ge(std_done, 2)
            dve.reciprocal(rstd[:, :], std[:, :]).then_inc(rstd_done, 1)
            dve.wait_ge(rstd_done, 1)
            dve.tensor_tensor(msq[:, :], mv[:, :, 1], rstd[:, :], ALU.mult).then_inc(rstd_done, 1)
            dve.wait_ge(rstd_done, 2)
            dve.tensor_tensor(msq[:, :], msq[:, :], rstd[:, :], ALU.mult).then_inc(msq_done, 1)
            dve.wait_ge(small_loaded, 16 * (3 + RC))
            dve.tensor_scalar(ap_half[:, :], ap_sb[:, :], 0.5, None, ALU.mult)
            dve.tensor_copy(rt_w[:, 0:E], raw_router[:, :]).then_inc(router_split, 1)
            dve.wait_ge(router_split, 1)
            dve.tensor_tensor(rt_w[:, E:], raw_router[:, :], rt_w[:, 0:E].bitcast(F32), ALU.subtract).then_inc(
                router_split, 1
            )

            def normalise(i, j):
                if not (isinstance(i, int) and i * 2 + j < 2):
                    dve.wait_ge(xn_done, i * 2 + (j - 1))
                for k in range(BT):
                    t = (i * 2 + j) * BT + k
                    last = dve.tensor_scalar((h_tok, h2_tok)[j % 2][:, k, :], x_sb[:, t, :], mv[:, t, 0:1],
                                             rstd[:, bass.ds(t, 1)], ALU.subtract, ALU.mult)
                last.then_inc(normal_done, 1)

            def x_lo(n, j=0):
                dve.wait_ge(xT_hi_done, n + 1)
                hi, lo = ((part_hi, part_lo), (hT_hi, hT_lo))[j % 2]
                dve.tensor_tensor(lo[:, :], (turned, bytok)[j % 2][:, :], hi[:, :].bitcast(F32),
                                  ALU.subtract).then_inc(xT_lo_done, 1)

            normalise(0, 0)
            normalise(0, 1)
            with dve.Fori(0, NB // 2 - 1) as i:
                for j in range(2):
                    x_lo(i * 2 + j, j)
                    normalise(i, j + 2)
            x_lo(NB - 2, 0)
            x_lo(NB - 1, 1)
            dve.wait_ge(rms1_done, 1)
            dve.reciprocal(r1[:, :], rms1[:, :]).then_inc(rstd_done, 1)

            step = [0]

            def done(ins):
                step[0] += 1
                ins.then_inc(route_step, 1)
                dve.wait_ge(route_step, step[0])

            dve.wait_ge(consts_ready, 6)
            dve.wait_ge(logits_done, NB)
            done(dve.tensor_copy(flat(lg[:, :, :]), pair[2][:, 1, :]))
            done(dve.tensor_tensor(logit[:, :, :], lg[:, :, 0:E], lg[:, :, E:], ALU.add))

            def best_of(values, top, one_hot):
                done(dve.tensor_reduce(top, values, AX.X, ALU.max))
                done(dve.tensor_tensor(scratch[:, :, :], values, each(top), ALU.is_equal))
                done(dve.tensor_tensor(scratch[:, :, :], scratch[:, :, :], rank_of[:, :, :], ALU.mult))
                done(dve.tensor_reduce(best[:, :], scratch[:, :, :], AX.X, ALU.max))
                done(dve.tensor_tensor(one_hot, scratch[:, :, :], each(best[:, :]), ALU.is_equal))

            best_of(logit[:, :, :], m1[:, :], first[:, :, :])
            done(dve.scalar_tensor_tensor(out=logit[:, :, :], in0=first[:, :, :], scalar=-BIG, in1=logit[:, :, :],
                                          op0=ALU.mult, op1=ALU.add))
            best_of(logit[:, :, :], m2[:, :], second[:, :, :])
            dve.tensor_tensor(gap[:, :], m2[:, :], m1[:, :], ALU.subtract).then_inc(gap_done, 1)
            dve.tensor_tensor(chosen[:, :, :].rearrange("p e t -> p t e"), first[:, :, :], second[:, :, :],
                              ALU.add).then_inc(chosen_done, 1)
            def make_h(b):
                for k in range(BT):
                    t = b * BT + k
                    last = dve.tensor_scalar(h_tok[:, k, :], xn[:, t, :], r1[:, bass.ds(t, 1)], None, ALU.mult)
                last.then_inc(h_done, 1)

            def h_lo(b):
                dve.wait_ge(hT_hi_done, b + 1)
                dve.tensor_tensor(hT_lo[:, :], turned[:, :], hT_hi[:, :].bitcast(F32), ALU.subtract).then_inc(
                    hT_lo_done, 1
                )

            def make_decay(b):
                dve.wait_ge(t_decay_done, b + 1)
                dve.tensor_scalar(decay[:, :, :], t_decay[:, :, :], 0.5, 0.5, ALU.mult, ALU.add).then_inc(decay_done, 1)

            def make_rest(b):
                dve.wait_ge(square_done, b + 1)
                dve.tensor_scalar(rest[:, :, :], square[:, :, :], -1.0, 1.0, ALU.mult, ALU.add).then_inc(rest_done, 1)

            def make_feed(b):
                dve.wait_ge(x_in_done, b + 1)
                dve.wait_ge(root_done, b + 1)
                dve.tensor_tensor(feed[:, :, :], root[:, :, :], x_in[:, :, :], ALU.mult).then_inc(feed_done, 1)

            def scan(b):
                dve.wait_ge(feed_done, b + 1)
                dve.wait_ge(carry_done, b + 1)
                for c in range(RC):
                    dve.tensor_tensor_scan(state[:, c, :], decay[:, c, :], feed[:, c, :], carry[:, c : c + 1],
                                           ALU.mult, ALU.add).then_inc(scan_done, 1)

            def make_y(b):
                dve.wait_ge(t_gate_done, b + 1)
                dve.wait_ge(scan_done, b * RC + RC)
                dve.tensor_scalar(carry[:, :], state[:, :, BLK - 1], keep[:, bass.ds(b + 1, 1)], None,
                                  ALU.mult).then_inc(carry_done, 1)
                dve.scalar_tensor_tensor(out=flat(y[:, :, :]), in0=flat(t_gate[:, :, :]), scalar=1.0,
                                         in1=flat(state[:, :, :]), op0=ALU.add, op1=ALU.mult).then_inc(y_done, 1)

            def tokens(ap, b):
                return ap[:, bass.ds(b * BT, BT), :].rearrange("p t d -> p (t d)")

            def middle(b):
                dve.wait_ge(proj_done, b + 1)
                dve.tensor_tensor(tokens(s_tok, b), bytok[:, :], tokens(xn, b), ALU.add).then_inc(mid_done, 1)

            def make_h2(b):
                dve.wait_ge(rms2_done, b + 1)
                dve.reciprocal(r2[:, :], rms2[:, :]).then_inc(r2_done, 1)
                dve.wait_ge(r2_done, b + 1)
                for k in range(BT):
                    last = dve.tensor_scalar(h2_tok[:, k, :], s_tok[:, b * BT + k, :], r2[:, k : k + 1], None, ALU.mult)
                last.then_inc(h2_done, 1)

            def make_h2_lo(b):
                dve.wait_ge(h2_hi_done, b + 1)
                dve.tensor_tensor(h2_lo[:, :], turned[:, :], h2_hi[:, :].bitcast(F32), ALU.subtract).then_inc(
                    h2_lo_done, 1
                )

            def shared_act(b, c):
                dve.wait_ge(silu_done, b * (SC + IC) + (c + 1))
                dve.tensor_tensor(sh_act[:, c, :], silu_b[:, c % 2, :], pair[c][:, 1, :], ALU.mult).then_inc(
                    sh_act_done, 1
                )

            def mlp_product(b, j):
                n = SC + j
                dve.wait_ge(silu_done, b * (SC + IC) + (n + 1))
                dve.tensor_tensor(mlp_act[:, j, :], silu_b[:, n % 2, :], pair[n % 3][:, 1, :], ALU.mult).then_inc(
                    mlp_act_done, 1
                )

            def make_s(b):
                dve.wait_ge(mlp_out_done, b + 1)
                dve.tensor_tensor(tokens(s_tok, b), bytok[:, :], tokens(s_tok, b), ALU.add).then_inc(s_done, 1)

            def run_block(b, ahead=2, before=1, sums=(), ends=()):
                if ahead:
                    h_lo(b + 1)
                dve.tensor_copy(h_tok[:, :, :], xn[:, bass.ds(b * BT, BT), :]).then_inc(x_tok_done, 1)
                middle(b)
                if ahead:
                    make_decay(b + 1)
                x_lo(b + NB)
                if ahead:
                    make_rest(b + 1)
                for args in sums[:1]:
                    add_experts(*args)
                make_h2(b)
                if ahead:
                    make_feed(b + 1)
                for c in range(SC):
                    shared_act(b, c)
                if before:
                    make_s(b - 1)
                if ahead:
                    scan(b + 1)
                make_h2_lo(b)
                mlp_product(b, 0)
                if ahead:
                    make_y(b + 1)
                if ahead > 1:
                    make_h(b + 2)
                for j in range(1, IC):
                    mlp_product(b, j)
                for args in sums[1:]:
                    add_experts(*args)
                for args in ends:
                    finish(*args)

            dve.memset(carry[:, :], 0.0).then_inc(carry_done, 1)
            dve.engine_nop().then_inc(s_done, 1)
            dve.engine_nop().then_inc(e_out_done, 3)
            dve.engine_nop().then_inc(e_act_done, 1)
            dve.engine_nop().then_inc(e_copy_done, 2)
            dve.wait_ge(rstd_done, 3)
            make_h(0)
            h_lo(0)

            dve.wait_ge(egap_done, 1)
            done(dve.tensor_scalar(esum[:, :], egap[:, :], 1.0, None, ALU.add))
            done(dve.reciprocal(p1[:, :], esum[:, :]))
            done(dve.tensor_tensor(p2[:, :], egap[:, :], p1[:, :], ALU.mult))

            dve.wait_ge(ranks_done, 1)
            done(dve.tensor_copy(flat(count[:, :, :]), counts_ps))
            done(dve.tensor_reduce(total[:, :], count[:, :, :], AX.X, ALU.add))
            done(dve.tensor_scalar(total_i[:, :], total[:, :], float(P - 1), None, ALU.add))
            done(dve.tensor_scalar(tiles_i[:, :], total_i[:, :], 7, None, ALU.logical_shift_right))
            done(dve.tensor_copy(tiles[:, :], tiles_i[:, :]))
            done(dve.tensor_tensor_scan(tiles_to[:, :], ones[:, 0:E], tiles[:, :], 0.0, ALU.mult, ALU.add))
            done(dve.tensor_tensor(tiles_from[:, :], tiles_to[:, :], tiles[:, :], ALU.subtract))
            done(dve.tensor_scalar(steps[:, :, 0], tiles_from[:, :], float(P), None, ALU.mult))
            done(dve.tensor_copy(steps[:, :, 1:], count[:, :, 0 : NT - 1]))
            done(dve.tensor_tensor_scan(flat(offset[:, :, :]), flat(restart[:, :, :]), flat(steps[:, :, :]), 0.0,
                                        ALU.mult, ALU.add))
            done(dve.tensor_tensor(flat(slot[:, :, :]), flat(offset[:, :, :]), ranks_ps, ALU.add))
            for c, one_hot in enumerate((first, second)):
                done(dve.tensor_tensor(scratch[:, :, :], one_hot[:, :, :], slot[:, :, :].rearrange("p e t -> p t e"),
                                       ALU.mult))
                done(dve.tensor_reduce(slot_f[:, c, :], scratch[:, :, :], AX.X, ALU.add))
            dve.tensor_copy(slot_i[:, :, :], slot_f[:, :, :]).then_inc(slots_known, 1)
            done(dve.tensor_tensor(passed[:, :, :], tile_no[:, :, :],
                                   tiles_to[:, :].unsqueeze(1).to_broadcast([P, TILES, E]), ALU.is_ge))
            done(dve.tensor_reduce(expert_f[:, :], passed[:, :, :], AX.X, ALU.add))
            dve.tensor_scalar(expert_i[:, :], expert_f[:, :], float(E - 1), None, ALU.min).then_inc(experts_known, 1)

            make_decay(0)
            make_rest(0)
            make_feed(0)
            dve.wait_ge(zeroed, 16 * -(-SLOTS // ZW))
            scan(0)
            make_y(0)
            make_h(1)
            run_block(0, before=0)
            with dve.Fori(1, HALF) as b:
                run_block(b)
            make_s(HALF - 1)

            def e_lo(i, j):
                dve.wait_ge(e_hi_done, i * 4 + (j + 1))
                dve.tensor_tensor(xe_lo[:, j % 2, :], turned[:, 0:P], xe_hi[:, j % 2, :].bitcast(F32),
                                  ALU.subtract).then_inc(e_lo_done, 1)

            def e_act(i, j):
                dve.wait_ge(e_silu_done, i * 4 + (j + 1))
                if not (isinstance(i, int) and i * 4 + j < 2):
                    dve.wait_ge(e_actT_done, i * 4 + (j - 1))
                dve.tensor_tensor(act_e[:, j % 2, 0:I], silu_e[:, j % 2, :], pair[j % 2][:, 1, 0:I],
                                  ALU.mult).then_inc(e_act_done, 1)

            def e_out(i, j):
                dve.wait_ge(e_down_done, i * 4 + (j + 1))
                if not (isinstance(i, int) and i * 4 + j < 4):
                    dve.wait_ge(tile_stored[j % 4], i * 16 + (j // 4) * 16)
                dve.tensor_copy(y_tile[:, j % 4, :], pair[2][:, 1, 0:P]).then_inc(e_out_done, 1)

            dve.wait_ge(pads_ready, 4)
            e_lo(0, 0)
            e_lo(0, 1)
            e_act(0, 0)
            e_lo(0, 2)
            e_act(0, 1)

            def e_step(i, j):
                e_lo(i, j + 2)
                e_act(i, j + 1)
                e_out(i, j - 1)

            for j in range(1, 4):
                e_step(0, j)
            for j in range(4):
                e_step(1, j)
            with dve.Fori(2, (TILES - 3) // 4) as i:
                for j in range(4):
                    e_step(i, j)
            for t in range(TILES - 3, TILES):
                if t + 2 < TILES:
                    e_lo(0, t + 2)
                if t + 1 < TILES:
                    e_act(0, t + 1)
                e_out(0, t - 1)
            e_out(0, TILES - 1)

            def add_experts(f, k, n):
                dve.wait_ge(gathered[k], n * (16 * 2 * BT))
                if not (isinstance(n, int) and n == 1):
                    dve.wait_ge(out_stored[k], n * 16 - 16)
                for t in range(BT):
                    cols = slice(t * P, (t + 1) * P)
                    dve.scalar_tensor_tensor(out=half_sum[:, k, cols], in0=got[:, k, 0, t, :],
                                             scalar=p1[:, bass.ds(f * BT + t, 1)], in1=shared[:, f * BT + t, :],
                                             op0=ALU.mult, op1=ALU.add).then_inc(half_done, 1)
                for t in range(BT):
                    cols = slice(t * P, (t + 1) * P)
                    dve.wait_ge(half_done, f * BT + (t + 1))
                    last = dve.scalar_tensor_tensor(out=fin[:, k, cols], in0=got[:, k, 1, t, :],
                                                    scalar=p2[:, bass.ds(f * BT + t, 1)], in1=half_sum[:, k, cols],
                                                    op0=ALU.mult, op1=ALU.add)
                last.then_inc(summed, 1)

            def finish(f, k, n):
                dve.wait_ge(silu_f_done, f + 1)
                dve.tensor_tensor(gated[:, k, :], silu_f[:, k, :], tokens(s_tok, f), ALU.mult).then_inc(product_done, 1)
                dve.wait_ge(product_done, f + 1)
                dve.wait_ge(x_again[k], n * 16)
                dve.tensor_tensor(gated[:, k, :], gated[:, k, :], x_back[:, k, :], ALU.add).then_inc(gated_done, 1)

            for k in range(4):
                dve.wait_ge(tile_stored[k], 16 * -(-(TILES - k) // 4))
            run_block(HALF, before=0, sums=[(0, 0, 1)], ends=[(0, 0, 1)])
            with dve.Fori(HALF + 1, NB - 2) as b:
                f = b * 2 - (2 * HALF + 1)
                two = [(f, 1, b - HALF), (f + 1, 0, b - (HALF - 1))]
                run_block(b, sums=two, ends=two)
            two = [(NB - 5, 1, NB - 2 - HALF), (NB - 4, 0, NB - 1 - HALF)]
            run_block(NB - 2, ahead=1, sums=two, ends=two)
            two = [(NB - 3, 1, NB - 1 - HALF), (NB - 2, 0, NB - HALF)]
            run_block(NB - 1, ahead=0, sums=two, ends=two)
            make_s(NB - 1)
            add_experts(NB - 1, 1, NB - HALF)
            finish(NB - 1, 1, NB - HALF)

    return nc


_INS = [
    "L0_attn_x", "L0_attn_ln1_w", "L0_attn_ln2_w", "L0_attn_w_in", "L0_attn_w_gate", "L0_attn_a_param", "L0_attn_w_a",
    "L0_attn_w_out", "L0_attn_w_mlp_gate", "L0_attn_w_mlp_up", "L0_attn_w_mlp_down", "L0_ffn_gate_w", "L0_ffn_Wg",
    "L0_ffn_Wu", "L0_ffn_Wd", "L0_ffn_Sg", "L0_ffn_Su", "L0_ffn_Sd",
]
_OUTS = [((4, 1024, 128), "float32")]


def kernel(**inputs):
    import numpy as _np
    import concourse.bacc as _bacc
    from concourse import mybir as _mybir
    from concourse.bass_utils import run_bass_kernel_spmd as _run

    nc = _bacc.Bacc("TRN2", target_bir_lowering=False, num_devices=1)
    arrays, args = {}, []
    for name in _INS:
        a = _np.ascontiguousarray(inputs[name])
        arrays[f"in_{name}_dram"] = a
        args.append(nc.dram_tensor(f"in_{name}_dram", a.shape, _mybir.dt.from_np(a.dtype), kind="ExternalInput").ap())
    for i, (shape, dtype) in enumerate(_OUTS):
        dt = _mybir.dt.from_np(_np.dtype(dtype))
        args.append(nc.dram_tensor(f"out_{i}_dram", shape, dt, kind="ExternalOutput").ap())
    gated_recurrent_moe_kernel(nc, *args)
    r = _run(nc, [arrays], core_ids=[0])
    got = tuple(r.results[0][f"out_{i}_dram"] for i in range(len(_OUTS)))
    return got[0]
```

```python
from contextlib import ExitStack

import concourse.bass as bass
from concourse import mybir

F32 = mybir.dt.float32
F32R = mybir.dt.float32r
I32 = mybir.dt.int32
ALU = mybir.AluOpType
ACT = mybir.ActivationFunctionType
AX = mybir.AxisListType

P = 128


def gated_recurrent_moe_kernel(
    nc: bass.Bass,
    x: bass.AP,
    ln1_w: bass.AP,
    ln2_w: bass.AP,
    w_in: bass.AP,
    w_gate: bass.AP,
    a_param: bass.AP,
    w_a: bass.AP,
    w_out: bass.AP,
    w_mlp_gate: bass.AP,
    w_mlp_up: bass.AP,
    w_mlp_down: bass.AP,
    gate_w: bass.AP,
    Wg: bass.AP,
    Wu: bass.AP,
    Wd: bass.AP,
    Sg: bass.AP,
    Su: bass.AP,
    Sd: bass.AP,
    out: bass.AP,
):
    BATCH, T, H = x.shape
    REC = w_in.shape[0]
    INTER = w_mlp_gate.shape[0]
    E, _, I = Wg.shape
    IS = Sg.shape[1]
    TOK = BATCH * T
    NT = TOK // P
    BT = 4
    BLK = BT * P
    NB = TOK // BLK
    RC = REC // P
    IC = INTER // P
    EC = -(-I // P)
    SC = -(-IS // P)
    IR = IS - P
    GATES = P // 2
    TILES = 2 * TOK // P + E - 1
    SLOTS = TILES * P
    QT = NT // 4
    HALF = NB // 2
    BIG = 3.0e38
    ZW = 2 * EC * P
    ROOM = 2 * NT * E + TILES * E + NT * (P + 6)
    assert NB == 8 and H == P and T % BLK == 0 and T // BLK == 2 and IC == 4 and RC == 2 and SC == 2 and IR <= GATES

    xt = x.rearrange("b (t p) d -> p (b t) d", p=P)
    ot = out.rearrange("b (t p) d -> p (b t) d", p=P)
    slots = nc.dram_tensor("slots", (SLOTS, P), F32, kind="Internal").ap()
    moved = nc.dram_tensor("moved", (SLOTS, P), F32, kind="Internal").ap()

    with ExitStack() as ctx:

        def sb(name, shape, dt=F32):
            return ctx.enter_context(nc.sbuf_tensor(name, shape, dt))

        def sem(name):
            return ctx.enter_context(nc.semaphore(name))

        pair = [ctx.enter_context(nc.psum_tensor(f"pair{i}", [P, 2, 512], F32)) for i in range(3)]
        turned = ctx.enter_context(nc.psum_tensor("turned", [P, 512], F32))
        bytok = ctx.enter_context(nc.psum_tensor("bytok", [P, 512], F32))

        xn = sb("xn", [P, NT, P])
        ident = sb("ident", [P, P])
        below = sb("below", [P, P])
        ones = sb("ones", [P, P])
        keep = sb("keep", [P, NB + 1])
        tiny = sb("tiny", [P, 3])

        raw_router = sb("raw_router", [P, E])
        ln1 = sb("ln1", [P, 1])
        ln2 = sb("ln2", [P, 1])
        ap_sb = sb("ap_sb", [P, RC])
        ap_half = sb("ap_half", [P, RC])
        NREC = 3 * RC
        w_hi = sb("w_hi", [P, NREC + 2 * IC, P], F32R)
        w_lo = sb("w_lo", [P, NREC + 2 * IC, P], F32R)
        wout_t = sb("wout_t", [P, RC, P])
        wdown_t = sb("wdown_t", [P, IC, P])
        sh_hi = sb("sh_hi", [P, 3 * P], F32R)
        sh_lo = sb("sh_lo", [P, 3 * P], F32R)
        sd_sb = sb("sd_sb", [P, SC, P])
        up_hi = sb("up_hi", [P, E, 2 * I], F32R)
        up_lo = sb("up_lo", [P, E, 2 * I], F32R)
        wd_sb = sb("wd_sb", [P, E, EC * P])

        mv = sb("mv", [P, NT, 2])
        std = sb("std", [P, NT])
        rstd = sb("rstd", [P, NT])
        msq = sb("msq", [P, NT])
        rms1 = sb("rms1", [P, NT])
        r1 = sb("r1", [P, NT])
        part_hi = sb("part_hi", [P, BLK], F32R)
        part_lo = sb("part_lo", [P, BLK], F32R)

        m1 = sb("m1", [P, NT])
        m2 = sb("m2", [P, NT])
        best = sb("best", [P, NT])
        gap = sb("gap", [P, NT])
        egap = sb("egap", [P, NT])
        esum = sb("esum", [P, NT])
        p1 = sb("p1", [P, NT])
        p2 = sb("p2", [P, NT])
        total = sb("total", [P, E])
        total_i = sb("total_i", [P, E], I32)
        tiles_i = sb("tiles_i", [P, E], I32)
        tiles = sb("tiles", [P, E])
        tiles_to = sb("tiles_to", [P, E])
        tiles_from = sb("tiles_from", [P, E])
        slot_f = sb("slot_f", [P, 2, NT])
        slot_i = sb("slot_i", [P, 2, NT], I32)
        expert_f = sb("expert_f", [P, TILES])
        expert_i = sb("expert_i", [P, TILES], I32)

        h_tok = sb("h_tok", [P, BT, P])
        hT_hi = sb("hT_hi", [P, BLK], F32R)
        hT_lo = sb("hT_lo", [P, BLK], F32R)
        rec_room = sb("rec_room", [P, 3 * RC * BLK])
        x_in, t_gate, t_decay = (
            rec_room[:, n * RC * BLK : (n + 1) * RC * BLK].rearrange("p (c t) -> p c t", c=RC) for n in range(3)
        )
        act_room = sb("act_room", [P, (2 + IC + SC) * BLK])
        silu_b, mlp_act, sh_act = (
            act_room[:, a * BLK : b * BLK].rearrange("p (c t) -> p c t", t=BLK)
            for a, b in ((0, 2), (2, 2 + IC), (2 + IC, 2 + IC + SC))
        )
        decay = sb("decay", [P, RC, BLK])
        state = sb("state", [P, RC, BLK])
        square = rest = root = t_decay
        feed = x_in
        y = t_gate
        carry = sb("carry", [P, RC])
        results = sb("results", [P, 2 * NT * P])
        s_tok = results[:, 0 : NT * P].rearrange("p (t d) -> p t d", d=P)
        shared = results[:, NT * P :].rearrange("p (t d) -> p t d", d=P)
        raw_up = results[:, 2 * NT * P - E * 2 * I :].rearrange("p (e i) -> p e i", e=E)
        ssq = sb("ssq", [P, BT])
        rms2 = sb("rms2", [P, BT])
        r2 = sb("r2", [P, BT])
        h2_tok = sb("h2_tok", [P, BT, P])
        squares = h2_tok
        h2_hi = sb("h2_hi", [P, BLK], F32R)
        h2_lo = sb("h2_lo", [P, BLK], F32R)
        xT = (results[:, 3 * BLK : 4 * BLK], results[:, 4 * BLK : 5 * BLK])

        xe_hi = part_hi[:, 0 : 2 * P].rearrange("p (k d) -> p k d", d=P)
        xe_lo = part_lo[:, 0 : 2 * P].rearrange("p (k d) -> p k d", d=P)
        actT = rec_room[:, 0 : 2 * EC * P].rearrange("p (k d) -> p k d", k=2)
        silu_e = rec_room[:, 2 * RC * BLK : 2 * RC * BLK + 2 * I].rearrange("p (k d) -> p k d", k=2)
        y_tile = state[:, :, :].rearrange("p a b -> p (a b)")[:, 0 : 4 * P].rearrange("p (k d) -> p k d", d=P)
        act_e = sb("act_e", [P, 2, EC * P])
        zeros = act_e[:, :, :].rearrange("p a b -> p (a b)")
        got = [
            room_e[:, :, :].rearrange("p e i -> p (e i)")[:, 0 : NT * P].bitcast(F32).rearrange("p (t d) -> p t d", d=P)
            for room_e in (up_hi, up_lo)
        ]

        def carve(base, at, shape):
            size = 1
            for n in shape[1:]:
                size *= n
            flat = base[:, at[0] : at[0] + size]
            at[0] += size
            assert at[0] <= base.shape[1]
            if len(shape) == 2:
                return flat
            if len(shape) == 3:
                return flat.rearrange("p (a b) -> p a b", b=shape[2])
            assert len(shape) == 5
            return flat.rearrange("p (a b c d) -> p a b c d", b=shape[2], c=shape[3], d=shape[4])

        rec_raw = [0]
        raw_rec = carve(rec_room, rec_raw, [P, 2 * RC, P])
        raw_a = carve(rec_room, rec_raw, [P, RC, REC])
        raw_out = carve(rec_room, rec_raw, [P, REC])
        raw_down = carve(rec_room, rec_raw, [P, INTER])
        wa_t = carve(rec_room, rec_raw, [P, RC, REC])
        act_raw = [0]
        raw_mlp = carve(act_room, act_raw, [P, 2 * IC, P])
        raw_shared = carve(act_room, act_raw, [P, 3 * P])
        scaled = carve(act_room, act_raw, [P, NREC + 2 * IC, P])

        room = sb("room", [P, ROOM])
        early = [0]
        rank_of = carve(room, early, [P, NT, E])
        tile_no = carve(room, early, [P, TILES, E])
        restart = carve(room, early, [P, E, NT])
        st6 = carve(room, early, [P, NT, 6])
        routing = [early[0]]
        x_sb = carve(room, early, [P, NT, P])
        logit = carve(room, routing, [P, NT, E])
        first = carve(room, routing, [P, NT, E])
        second = carve(room, routing, [P, NT, E])
        scratch = carve(room, routing, [P, NT, E])
        chosen = carve(room, routing, [P, E, NT])
        ranked = carve(room, routing, [P, 2, E * NT])
        ranks = ranked[:, 0, :].rearrange("p (e t) -> p e t", t=NT)
        count = ranked[:, 1, :].rearrange("p (e t) -> p e t", t=NT)
        steps = carve(room, routing, [P, E, NT])
        offset = carve(room, routing, [P, E, NT])
        slot = carve(room, routing, [P, E, NT])
        passed = carve(room, routing, [P, TILES, E])
        x_back = room[:, 0 : NT * P].rearrange("p (t d) -> p t d", d=P)
        x_tile = room[:, NT * P : NT * P + 4 * P].rearrange("p (k d) -> p k d", d=P)

        x_loaded = [sem(f"x_loaded{n}") for n in range(4)]
        rec_loaded = sem("rec_loaded")
        out_loaded = sem("out_loaded")
        small_loaded = sem("small_loaded")
        mlp_loaded = sem("mlp_loaded")
        shared_loaded = sem("shared_loaded")
        up_loaded = sem("up_loaded")
        down_loaded = sem("down_loaded")
        zeroed = sem("zeroed")
        pads_ready = sem("pads_ready")
        zeros_ready = sem("zeros_ready")
        consts_ready = sem("consts_ready")
        const_step = sem("const_step")
        stats_done = sem("stats_done")
        std_done = sem("std_done")
        msq_done = sem("msq_done")
        rms1_done = sem("rms1_done")
        ranks_taken = sem("ranks_taken")
        xn_done = sem("xn_done")
        ap_half_done = sem("ap_half_done")
        r1_done = sem("r1_done")
        x_tok_done = sem("x_tok_done")
        rstd_done = sem("rstd_done")
        wT_done = sem("wT_done")
        wT_taken = sem("wT_taken")
        waT_done = sem("waT_done")
        scaled_done = sem("scaled_done")
        w_hi_done = sem("w_hi_done")
        w_lo_done = sem("w_lo_done")
        shared_split = sem("shared_split")
        waT_taken = sem("waT_taken")
        tiny_ready = sem("tiny_ready")
        stats_step = sem("stats_step")
        feed_done = sem("feed_done")
        scan_done = sem("scan_done")
        carry_done = sem("carry_done")
        r2_done = sem("r2_done")
        half_done = sem("half_done")
        product_done = sem("product_done")
        last_product_done = sem("last_product_done")
        last_gated_done = sem("last_gated_done")
        up_hi_done = sem("up_hi_done")
        up_lo_done = sem("up_lo_done")
        xT_done = sem("xT_done")
        router_xT_done = sem("router_xT_done")
        router_xT_taken = sem("router_xT_taken")
        xT_hi_done = sem("xT_hi_done")
        xT_lo_done = sem("xT_lo_done")
        logits_done = sem("logits_done")
        logits_taken = sem("logits_taken")
        route_step = sem("route_step")
        gap_done = sem("gap_done")
        egap_done = sem("egap_done")
        chosen_done = sem("chosen_done")
        ranks_done = sem("ranks_done")
        slots_known = sem("slots_known")
        experts_known = sem("experts_known")
        scattered = sem("scattered")

        h_done = sem("h_done")
        hT_done = sem("hT_done")
        hT_hi_done = sem("hT_hi_done")
        hT_lo_done = sem("hT_lo_done")
        pair_done = sem("pair_done")
        t_decay_done = sem("t_decay_done")
        decay_done = sem("decay_done")
        square_done = sem("square_done")
        rest_done = sem("rest_done")
        x_in_done = sem("x_in_done")
        t_gate_done = sem("t_gate_done")
        root_done = sem("root_done")
        y_done = sem("y_done")
        proj_done = sem("proj_done")
        mid_done = sem("mid_done")
        ssq_done = sem("ssq_done")
        rms2_done = sem("rms2_done")
        h2_done = sem("h2_done")
        h2T_done = sem("h2T_done")
        h2_hi_done = sem("h2_hi_done")
        h2_lo_done = sem("h2_lo_done")
        silu_done = sem("silu_done")
        sh_act_done = sem("sh_act_done")
        mlp_act_done = sem("mlp_act_done")
        sh_out_done = sem("sh_out_done")
        shared_done = sem("shared_done")
        mlp_out_done = sem("mlp_out_done")
        s_done = sem("s_done")

        tile_loaded = [sem(f"tile_loaded{i}") for i in range(4)]
        eT_done = sem("eT_done")
        e_hi_done = sem("e_hi_done")
        e_lo_done = sem("e_lo_done")
        e_up_done = sem("e_up_done")
        e_silu_done = sem("e_silu_done")
        e_act_done = sem("e_act_done")
        e_actT_done = sem("e_actT_done")
        e_copy_done = sem("e_copy_done")
        e_down_done = sem("e_down_done")
        e_out_done = sem("e_out_done")
        tile_stored = [sem(f"tile_stored{i}") for i in range(4)]
        gathered = [sem(f"gathered{f}") for f in range(NB)]
        x_again = sem("x_again")
        summed = sem("summed")
        silu_f_done = sem("silu_f_done")
        gated_done = sem("gated_done")
        out_stored = sem("out_stored")

        GROUPS = [(0, 2 * RC), (2 * RC, NREC), (NREC, NREC + IC), (NREC + IC, NREC + 2 * IC)]
        PAIRS = 3 + SC + IC
        assert PAIRS % 3 == 0

        block = ctx.enter_context(nc.Block())

        @block.sync
        def _(sp):
            def load_quarter(n):
                sp.dma_start(x_sb[:, n * QT : (n + 1) * QT, :], xt[:, n * QT : (n + 1) * QT, :]).then_inc(
                    x_loaded[n], 16
                )

            load_quarter(0)
            load_quarter(1)
            sp.dma_start(raw_a[:, :, :], w_a.rearrange("(c p) h -> p c h", p=P)).then_inc(rec_loaded, 16)
            sp.dma_start(raw_rec[:, 0:RC, :], w_in.rearrange("(c p) h -> p c h", p=P)).then_inc(rec_loaded, 16)
            sp.dma_start(raw_rec[:, RC:, :], w_gate.rearrange("(c p) h -> p c h", p=P)).then_inc(rec_loaded, 16)
            sp.dma_start(ln1[:, :], ln1_w.rearrange("(p o) -> p o", o=1)).then_inc(small_loaded, 16)
            sp.dma_start(ln2[:, :], ln2_w.rearrange("(p o) -> p o", o=1)).then_inc(small_loaded, 16)
            for c in range(RC):
                sp.dma_start(ap_sb[:, c : c + 1], a_param[c * P : (c + 1) * P].rearrange("(p o) -> p o", o=1)).then_inc(
                    small_loaded, 16
                )
            sp.dma_start(raw_router[:, :], gate_w).then_inc(small_loaded, 16)
            load_quarter(2)
            load_quarter(3)
            sp.dma_start(raw_out[:, :], w_out).then_inc(out_loaded, 16)
            sp.dma_start(raw_down[:, :], w_mlp_down).then_inc(out_loaded, 16)
            sp.dma_start(raw_mlp[:, 0:IC, :], w_mlp_gate.rearrange("(c p) h -> p c h", p=P)).then_inc(mlp_loaded, 16)
            sp.dma_start(raw_mlp[:, IC:, :], w_mlp_up.rearrange("(c p) h -> p c h", p=P)).then_inc(mlp_loaded, 16)
            sp.wait_ge(pads_ready, 2)
            for src, at in ((Sg[:, 0:P], 0), (Su[:, 0:P], P), (Su[:, P:], 2 * P), (Sg[:, P:], 2 * P + GATES)):
                sp.dma_start(raw_shared[:, at : at + src.shape[1]], src).then_inc(shared_loaded, 16)
            sp.dma_start(sd_sb[:, 0, :], Sd[0:P, :]).then_inc(shared_loaded, 16)
            sp.dma_start(sd_sb[0:IR, 1, :], Sd[P:IS, :]).then_inc(shared_loaded, 16)
            sp.dma_start(raw_up[:, :, 0:I], Wg.rearrange("e h i -> h e i")).then_inc(up_loaded, 16)
            sp.dma_start(raw_up[:, :, I:], Wu.rearrange("e h i -> h e i")).then_inc(up_loaded, 16)
            for c in range(EC):
                n = min(P, I - c * P)
                sp.dma_start(
                    wd_sb[0:n, :, c * P : (c + 1) * P], Wd[:, c * P : c * P + n, :].rearrange("e i h -> i e h")
                ).then_inc(down_loaded, 16)
            sp.wait_ge(zeros_ready, 1)
            flat = slots.rearrange("(p n) d -> p (n d)", p=P)
            for c in range(0, SLOTS, ZW):
                n = min(ZW, SLOTS - c)
                sp.dma_start(flat[:, c : c + n], zeros[:, 0:n]).then_inc(zeroed, 16)

            sp.wait_ge(experts_known, 1)
            sp.dma_start(x_back[:, :, :], xt).then_inc(x_again, 16)

            def load_tile(i, j):
                sp.dma_start(x_tile[:, j % 4, :], slots[bass.ds((i * 4 + j) * P, P), :]).then_inc(
                    tile_loaded[j % 4], 16
                )

            def store_tile(i, j):
                sp.wait_ge(e_out_done, i * 4 + (j + 4))
                sp.dma_start(moved[bass.ds((i * 4 + j) * P, P), :], y_tile[:, j % 4, :]).then_inc(
                    tile_stored[j % 4], 16
                )

            sp.wait_ge(scattered, 16 * 2 * NT)
            for j in range(4):
                load_tile(0, j)
            for j in range(4):
                sp.wait_ge(eT_done, j + 1)
                load_tile(1, j)
            with sp.Fori(2, TILES // 4) as i:
                for j in range(4):
                    sp.wait_ge(eT_done, i * 4 + (j - 3))
                    load_tile(i, j)
                    store_tile(i - 2, j)
            for t in range(TILES - TILES % 4, TILES):
                sp.wait_ge(eT_done, t - 3)
                load_tile(0, t)
            for t in range(TILES - TILES % 4 - 8, TILES):
                store_tile(0, t)
            def store(f):
                sp.dma_start(ot[:, bass.ds(f * BT, BT), :], got[0][:, bass.ds(f * BT, BT), :]).then_inc(out_stored, 16)

            with sp.Fori(0, NB - 2) as f:
                sp.wait_ge(gated_done, f + 1)
                store(f)
            for f in range(NB - 2, NB):
                sp.wait_ge(last_gated_done, f - (NB - 3))
                store(f)
            sp.wait_ge(out_stored, 16 * NB)

        @block.gpsimd
        def _(pool):
            pool.memset(zeros[:, :], 0.0).then_inc(zeros_ready, 1)
            pool.memset(ident[:, :], 0.0).then_inc(const_step, 1)
            pool.memset(ones[:, :], 1.0).then_inc(const_step, 1)
            pool.memset(below[:, :], 1.0).then_inc(const_step, 1)
            pool.memset(rank_of[:, :, :], 0.0).then_inc(const_step, 1)
            pool.memset(raw_shared[:, 2 * P :], 0.0).then_inc(pads_ready, 1)
            pool.memset(wd_sb[:, :, (EC - 1) * P :], 0.0).then_inc(pads_ready, 1)
            pool.wait_ge(const_step, 4)
            pool.affine_select(
                out=ident[:, :], in_=ident[:, :], compare_op=ALU.not_equal, fill=1.0, base=0,
                pattern=[[-1, P]], channel_multiplier=1,
            ).then_inc(consts_ready, 1)
            pool.affine_select(
                out=below[:, :], in_=below[:, :], compare_op=ALU.is_gt, fill=0.0, base=0,
                pattern=[[1, P]], channel_multiplier=-1,
            ).then_inc(consts_ready, 1)
            pool.iota(rank_of[:, :, :], pattern=[[0, NT], [-1, E]], base=E, channel_multiplier=0,
                      allow_small_or_imprecise_dtypes=True).then_inc(consts_ready, 1)
            pool.iota(tile_no[:, :, :], pattern=[[1, TILES], [0, E]], base=0, channel_multiplier=0,
                      allow_small_or_imprecise_dtypes=True).then_inc(consts_ready, 1)
            pool.memset(restart[:, :, :], 1.0).then_inc(const_step, 1)
            pool.memset(keep[:, :], 0.0).then_inc(const_step, 1)
            pool.wait_ge(const_step, 6)
            pool.memset(restart[:, :, 0:1], 0.0).then_inc(consts_ready, 1)
            pool.memset(keep[:, 1 : NB : 2], 1.0).then_inc(consts_ready, 1)

            def weight_lo(n):
                c0, c1 = GROUPS[n]
                pool.wait_ge(w_hi_done, n + 1)
                pool.tensor_tensor(w_lo[:, c0:c1, :], scaled[:, c0:c1, :], w_hi[:, c0:c1, :].bitcast(F32),
                                   ALU.subtract).then_inc(w_lo_done, 1)

            def up_weight_lo(e):
                pool.wait_ge(up_hi_done, e + 1)
                pool.tensor_tensor(up_lo[:, e, :], raw_up[:, e, :], up_hi[:, e, :].bitcast(F32), ALU.subtract).then_inc(up_lo_done, 1)

            weight_lo(0)
            weight_lo(1)
            for e in range(4):
                up_weight_lo(e)
            pool.wait_ge(shared_split, 1)
            pool.tensor_tensor(sh_lo[:, :], raw_shared[:, :], sh_hi[:, :].bitcast(F32),
                               ALU.subtract).then_inc(shared_split, 1)
            weight_lo(2)
            weight_lo(3)
            for e in range(4, E):
                up_weight_lo(e)
            pool.wait_ge(zeroed, 16 * -(-SLOTS // ZW))
            pool.wait_ge(slots_known, 1)
            pool.wait_ge(xn_done, NB)
            for t in range(NT):
                for c in range(2):
                    pool.indirect_dma_start(
                        slots, bass.IndirectOffsetOnAxis(ap=slot_i[:, c, t : t + 1], axis=0), xn[:, t, :], None
                    ).then_inc(scattered, 16)
            for k in range(4):
                pool.wait_ge(tile_stored[k], 16 * -(-(TILES - k) // 4))

            def gather(f):
                for t in range(f * BT, (f + 1) * BT):
                    for c in range(2):
                        pool.indirect_dma_start(
                            got[c][:, t, :], None, moved, bass.IndirectOffsetOnAxis(ap=slot_i[:, c, t : t + 1], axis=0)
                        ).then_inc(gathered[f], 16)

            def finish(f):
                rows = slice(f * BT, (f + 1) * BT)
                pool.wait_ge(silu_f_done, f + 1)
                pool.wait_ge(s_done, f + 2)
                pool.tensor_tensor(got[0][:, rows, :], got[1][:, rows, :], s_tok[:, rows, :], ALU.mult).then_inc(
                    product_done, 1
                )
                pool.wait_ge(product_done, f + 1)
                pool.tensor_tensor(got[0][:, rows, :], got[0][:, rows, :], x_back[:, rows, :], ALU.add).then_inc(
                    gated_done, 1
                )

            for f in range(NB):
                gather(f)
            pool.wait_ge(x_again, 16)
            for f in range(NB - 2):
                finish(f)

        @block.tensor
        def _(pe):
            def split_product(dst, c_hi, c_lo, m_hi, m_lo):
                pe.matmul(dst, c_hi, m_hi, start=True, stop=False)
                pe.matmul(dst, c_lo, m_hi, start=False, stop=False)
                return pe.matmul(dst, c_hi, m_lo, start=False, stop=True)

            banks = [pair[0][:, 0, :], pair[0][:, 1, :], pair[1][:, 0, :], pair[1][:, 1, :]]

            def turn_weights(bank, tiles):
                for c, tile in enumerate(tiles):
                    last = pe.transpose(bank[:, c * P : (c + 1) * P], tile, ident[:, :])
                return last

            def columns(ap, count):
                return [ap[:, c * P : (c + 1) * P] for c in range(count)]

            pe.wait_ge(consts_ready, 1)
            pe.wait_ge(rec_loaded, 16 * 3)
            turn_weights(turned, [raw_a[:, c, j * P : (j + 1) * P] for j in range(RC) for c in range(RC)]).then_inc(
                waT_done, 1
            )
            turn_weights(banks[0], [raw_rec[:, c, :] for c in range(2 * RC)]).then_inc(wT_done, 1)
            pe.wait_ge(waT_taken, 1)
            for j in range(RC):
                last = pe.matmul(banks[3][:, 0:REC], raw_rec[:, j, :], wa_t[:, j, :], start=(j == 0), stop=(j == RC - 1))
            last.then_inc(wT_done, 1)
            router_banks = (bytok, pair[2][:, 0, :])
            logits_ps = pair[2][:, 1, 0 : NT * E].rearrange("p (t e) -> p t e", e=E)

            def turn_x(b):
                pe.wait_ge(xn_done, b + 1)
                if b >= 2:
                    pe.wait_ge(router_xT_taken, b - 1)
                for k in range(BT):
                    last = pe.transpose(router_banks[b % 2][:, k * P : (k + 1) * P], xn[:, b * BT + k, :], ident[:, :])
                last.then_inc(router_xT_done, 1)

            def logits(b):
                pe.wait_ge(router_xT_taken, b + 1)
                for k in range(BT):
                    last = pe.matmul(logits_ps[:, b * BT + k, :], xT[b % 2][:, k * P : (k + 1) * P],
                                     raw_router[:, :], start=True, stop=True)
                last.then_inc(logits_done, 1)

            def turn_h(b):
                pe.wait_ge(h_done, b + 1)
                for k in range(BT):
                    last = pe.transpose(turned[:, k * P : (k + 1) * P], h_tok[:, k, :], ident[:, :])
                last.then_inc(hT_done, 1)

            def rec_chunk(n, c):
                w = (2 * RC, 0, RC)[n] + c
                return split_product(pair[n][:, c, :], w_hi[:, w, :], w_lo[:, w, :], hT_hi[:, :], hT_lo[:, :])

            def rec_pair(n, b=None):
                if b is not None:
                    pe.wait_ge(mlp_act_done, b * IC + (n + 2 - IC))
                for c in range(RC):
                    last = rec_chunk(n, c)
                last.then_inc(pair_done, 1)

            def project(b):
                pe.wait_ge(y_done, b + 1)
                if not (isinstance(b, int) and b == 0):
                    pe.wait_ge(shared_done, b)
                for c in range(RC):
                    for k in range(BT):
                        last = pe.matmul(bytok[:, k * P : (k + 1) * P], y[:, c, k * P : (k + 1) * P], wout_t[:, c, :],
                                         start=(c == 0 and k == 0), stop=(c == RC - 1), skip_group_check=True)
                last.then_inc(proj_done, 1)

            def turn_block_x(b):
                pe.wait_ge(x_tok_done, b + 1)
                for k in range(BT):
                    last = pe.transpose(turned[:, k * P : (k + 1) * P], h_tok[:, k, :], ident[:, :])
                last.then_inc(xT_done, 1)

            def shared_up(b, ahead):
                pe.wait_ge(xT_lo_done, b + 1)
                for c in range(SC):
                    pe.wait_ge((t_decay_done, x_in_done)[c], b + 1 + min(ahead, 1))
                    for g in range(2 - c):
                        cols = slice((2 * c + g) * P, (2 * c + g + 1) * P)
                        last = split_product(pair[c][:, g, :], sh_hi[:, cols], sh_lo[:, cols], part_hi[:, :],
                                             part_lo[:, :])
                    last.then_inc(pair_done, 1)

            def turn_h2(b):
                pe.wait_ge(h2_done, b + 1)
                for k in range(BT):
                    last = pe.transpose(turned[:, k * P : (k + 1) * P], h2_tok[:, k, :], ident[:, :])
                last.then_inc(h2T_done, 1)

            def shared_down(b):
                pe.wait_ge(sh_act_done, b * SC + SC)
                pe.wait_ge(s_done, b + 1)
                for c in range(SC):
                    rows = (P, IR)[c]
                    for k in range(BT):
                        last = pe.matmul(bytok[:, k * P : (k + 1) * P], sh_act[0:rows, c, k * P : (k + 1) * P],
                                         sd_sb[0:rows, c, :], start=(c == 0 and k == 0), stop=(c == SC - 1),
                                         skip_group_check=True)
                last.then_inc(sh_out_done, 1)

            def mlp_up(b, ahead, shared_end):
                pe.wait_ge(h2_lo_done, b + 1)
                for j in range(IC):
                    if j == 0:
                        pe.wait_ge(t_gate_done, b + 1 + min(ahead, 1))
                    if j == 2:
                        if shared_end:
                            shared_down(b)
                        if ahead > 1:
                            turn_h(b + 2)
                    if j == IC - 1:
                        pe.wait_ge(mlp_act_done, b * IC + 1)
                    for g in range(2):
                        w = NREC + g * IC + j
                        last = split_product(pair[(SC + j) % 3][:, g, :], w_hi[:, w, :], w_lo[:, w, :],
                                             h2_hi[:, :], h2_lo[:, :])
                    last.then_inc(pair_done, 1)

            def mlp_down(b, alone=False, middle=None):
                if alone:
                    pe.wait_ge(shared_done, b + 1)
                else:
                    pe.wait_ge(mid_done, b + 2)
                    pe.wait_ge(mlp_act_done, b * IC + IC)
                for j in range(IC):
                    if j == 1 and middle:
                        middle()
                    if alone:
                        pe.wait_ge(mlp_act_done, b * IC + j + 1)
                    for k in range(BT):
                        last = pe.matmul(bytok[:, k * P : (k + 1) * P], mlp_act[:, j, k * P : (k + 1) * P],
                                         wdown_t[:, j, :], start=(j == 0 and k == 0), stop=(j == IC - 1),
                                         skip_group_check=True)
                last.then_inc(mlp_out_done, 1)

            def rank_tokens():
                every = chosen[:, :, :].rearrange("p e t -> p (e t)")
                pe.wait_ge(chosen_done, 1)
                pe.wait_ge(hT_lo_done, 2)
                pe.matmul(turned[:, 0 : E * NT], below[:, :], every, start=True, stop=True)
                pe.matmul(turned[:, E * NT :], ones[:, :], every, start=True, stop=True).then_inc(ranks_done, 1)

            def run_block(b, ahead=2, before=1, projected=0):
                if not projected:
                    project(b)
                after = b if before else None
                if not before:
                    rank_tokens()
                    pe.wait_ge(wT_taken, 4)
                    pe.wait_ge(scaled_done, 2)
                if ahead:
                    pe.wait_ge(hT_lo_done, b + 2)
                    rec_pair(0, after)
                if not before:
                    pe.wait_ge(ranks_taken, 1)
                turn_block_x(b)
                if ahead:
                    rec_pair(1, after)
                    rec_pair(2, after)
                if not before:
                    pe.wait_ge(shared_split, 2)
                    pe.wait_ge(w_lo_done, 4)
                if before and not ahead:
                    mlp_down(b - 1)
                shared_up(b, ahead)
                if before and ahead:
                    mlp_down(b - 1, middle=lambda: turn_h2(b))
                else:
                    turn_h2(b)
                if not ahead:
                    shared_down(b)
                mlp_up(b, ahead, shared_end=ahead)

            turn_h(0)
            turn_x(0)
            turn_x(1)
            for b in range(NB):
                logits(b)
                if b + 2 < NB:
                    turn_x(b + 2)
                if b == 0:
                    pe.wait_ge(w_lo_done, 2)
                    pe.wait_ge(hT_lo_done, 1)
                    rec_pair(0)
                if b == 1:
                    rec_pair(1)
                if b == 3:
                    pe.wait_ge(out_loaded, 32)
                    pe.wait_ge(t_decay_done, 1)
                    turn_weights(banks[0], columns(raw_out, RC)).then_inc(wT_done, 1)
                    turn_weights(banks[1], columns(raw_down, IC)).then_inc(wT_done, 1)
                if b == 5:
                    pe.wait_ge(mlp_loaded, 32)
                    pe.wait_ge(x_in_done, 1)
                    turn_weights(banks[2], [raw_mlp[:, c, :] for c in range(IC)]).then_inc(wT_done, 1)
                    turn_weights(banks[3], [raw_mlp[:, IC + c, :] for c in range(IC)]).then_inc(wT_done, 1)
            pe.wait_ge(router_xT_taken, NB)
            rec_chunk(2, 0)
            pe.wait_ge(logits_taken, 1)
            rec_chunk(2, 1).then_inc(pair_done, 1)
            turn_h(1)
            pe.wait_ge(wT_taken, 3)
            run_block(0, before=0)
            with pe.Fori(1, HALF) as b:
                run_block(b)

            def e_turn(i, j):
                pe.wait_ge(tile_loaded[j % 4], i * 16 + (j // 4 + 1) * 16)
                pe.transpose(turned[:, 0:P], x_tile[:, j % 4, :], ident[:, :]).then_inc(eT_done, 1)

            expert_regs = [pe.alloc_register(f"expert{k}") for k in range(4)]

            hi_flat = up_hi[:, :, :].rearrange("p e i -> p (e i)")
            lo_flat = up_lo[:, :, :].rearrange("p e i -> p (e i)")
            wd_flat = wd_sb[:, :, :].rearrange("p e i -> p (e i)")

            def e_up(i, j, turn_next=True):
                pe.reg_load(expert_regs[j % 4], expert_i[0:1, bass.ds(i * 4 + j, 1)])
                e = pe.snap(expert_regs[j % 4], min_val=0, max_val=E - 1)
                pe.wait_ge(e_lo_done, i * 4 + (j + 1))
                if turn_next:
                    e_turn(i, j + 1)
                for g in range(2):
                    dst = pair[j % 2][:, g, 0:I]
                    hi = hi_flat[:, bass.ds(e * (2 * I) + g * I, I)]
                    lo = lo_flat[:, bass.ds(e * (2 * I) + g * I, I)]
                    pe.matmul(dst, xe_hi[:, j % 2, :], hi, start=True, stop=False)
                    pe.matmul(dst, xe_hi[:, j % 2, :], lo, start=False, stop=False)
                    last = pe.matmul(dst, xe_lo[:, j % 2, :], hi, start=False, stop=True)
                last.then_inc(e_up_done, 1)

            def e_turn_act(i, j):
                pe.wait_ge(e_act_done, i * 4 + (j + 2))
                for c in range(EC):
                    last = pe.transpose(pair[2][:, 0, c * P : (c + 1) * P], act_e[:, j % 2, c * P : (c + 1) * P],
                                        ident[:, :])
                last.then_inc(e_actT_done, 1)

            def e_down(i, j):
                e = pe.snap(expert_regs[j % 4], min_val=0, max_val=E - 1)
                pe.wait_ge(e_copy_done, i * 4 + (j + 3))
                pe.wait_ge(e_out_done, i * 4 + (j + 3))
                for c in range(EC):
                    last = pe.matmul(pair[2][:, 1, 0:P], actT[:, j % 2, c * P : (c + 1) * P],
                                     wd_flat[:, bass.ds(e * (EC * P) + c * P, P)], start=(c == 0), stop=(c == EC - 1))
                last.then_inc(e_down_done, 1)

            pe.wait_ge(hT_lo_done, HALF + 2)
            pe.wait_ge(experts_known, 1)
            pe.wait_ge(up_lo_done, E)
            pe.wait_ge(down_loaded, 16 * EC)
            e_turn(0, 0)
            e_up(0, 0)
            e_up(0, 1)
            e_turn_act(0, 0)

            def e_step(i, j):
                e_up(i, j + 1)
                e_down(i, j - 1)
                e_turn_act(i, j)

            for j in range(1, 4):
                e_step(0, j)
            with pe.Fori(1, (TILES - 3) // 4) as i:
                for j in range(4):
                    e_step(i, j)
            for t in range(TILES - 3, TILES):
                if t + 1 < TILES:
                    e_up(0, t + 1, turn_next=t + 2 < TILES)
                e_down(0, t - 1)
                e_turn_act(0, t)
            project(HALF)
            e_down(0, TILES - 1)

            pe.wait_ge(e_out_done, TILES + 3)
            run_block(HALF, projected=1)
            for b in range(HALF + 1, NB - 2):
                run_block(b)
            run_block(NB - 2, ahead=1)
            run_block(NB - 1, ahead=0)
            mlp_down(NB - 1, alone=True)

        @block.scalar
        def _(act):
            def root_of_variance(n):
                act.wait_ge(stats_done, n + 1)
                some = slice(n * QT, (n + 1) * QT)
                act.activation(std[:, some], mv[:, some, 1], ACT.Sqrt, bias=tiny[:, 0:1]).then_inc(std_done, 1)

            def root_of_mean_square(n):
                act.wait_ge(msq_done, n + 1)
                some = slice(n * QT, (n + 1) * QT)
                act.activation(rms1[:, some], msq[:, some], ACT.Sqrt, bias=tiny[:, 1:2]).then_inc(rms1_done, 1)

            def take(dst, src, scale=1.0):
                return act.activation(dst.rearrange("p a b -> p (a b)"), src, ACT.Copy, scale=scale)

            def take_x(b):
                act.wait_ge(router_xT_done, b + 1)
                if b >= 2:
                    act.wait_ge(logits_done, b - 1)
                act.activation(xT[b % 2], (bytok[:, :], pair[2][:, 0, :])[b % 2], ACT.Copy).then_inc(router_xT_taken, 1)

            def h_hi(b):
                act.wait_ge(hT_done, b + 1)
                act.activation(hT_hi[:, :], turned[:, :], ACT.Copy).then_inc(hT_hi_done, 1)

            def weight_hi(n):
                c0, c1 = GROUPS[n]
                act.activation(w_hi[:, c0:c1, :], scaled[:, c0:c1, :], ACT.Copy).then_inc(w_hi_done, 1)

            def up_weight_hi(e):
                act.activation(up_hi[:, e, :], raw_up[:, e, :], ACT.Copy).then_inc(up_hi_done, 1)

            act.wait_ge(tiny_ready, 3)
            root_of_variance(0)
            act.wait_ge(waT_done, 1)
            take(wa_t[:, :, :], turned[:, :]).then_inc(waT_taken, 1)
            act.wait_ge(wT_done, 1)
            act.wait_ge(small_loaded, 16 * (3 + RC))
            take(scaled[:, 0 : 2 * RC, :], pair[0][:, 0, :], ln1[:, 0:1]).then_inc(wT_taken, 1)
            root_of_mean_square(0)
            act.wait_ge(wT_taken, 1)
            weight_hi(0)
            act.wait_ge(wT_done, 2)
            take(scaled[:, 2 * RC : NREC, :], pair[1][:, 1, 0:REC], ln1[:, 0:1]).then_inc(wT_taken, 1)
            act.wait_ge(wT_taken, 2)
            weight_hi(1)
            root_of_variance(1)
            h_hi(0)
            take_x(0)
            take_x(1)
            root_of_mean_square(1)
            root_of_variance(2)
            take_x(2)
            root_of_mean_square(2)
            root_of_variance(3)
            take_x(3)
            root_of_mean_square(3)

            def rec_decay(b, q):
                act.wait_ge(pair_done, q + 1)
                for c in range(RC):
                    last = act.activation(t_decay[:, c, :], pair[0][:, c, :], ACT.Tanh, bias=ap_half[:, c : c + 1],
                                          scale=0.5)
                last.then_inc(t_decay_done, 1)

            def rec_x_in(q):
                act.wait_ge(pair_done, q + 2)
                act.activation(x_in[:, :, :], pair[1][:, :, :], ACT.Copy).then_inc(x_in_done, 1)

            def rec_gate(q):
                act.wait_ge(pair_done, q + 3)
                act.activation(t_gate[:, :, :], pair[2][:, :, :], ACT.Tanh, scale=0.5).then_inc(t_gate_done, 1)

            def rec_root(b):
                act.wait_ge(rest_done, b + 1)
                act.activation(root[:, :, :], rest[:, :, :], ACT.Sqrt, bias=tiny[:, 2:3]).then_inc(root_done, 1)

            def mid_squares(b):
                act.wait_ge(mid_done, b + 1)
                for k in range(BT):
                    act.activation(squares[:, k, :], s_tok[:, b * BT + k, :], ACT.Square,
                                   accum_out=ssq[:, k : k + 1]).then_inc(ssq_done, 1)

            def mid_root(b):
                act.wait_ge(ssq_done, b * BT + BT)
                act.activation(rms2[:, :], ssq[:, :], ACT.Sqrt, bias=tiny[:, 1:2], scale=1.0 / H).then_inc(rms2_done, 1)

            def block_x_hi(b):
                act.wait_ge(xT_done, b + 1)
                act.activation(part_hi[:, :], turned[:, :], ACT.Copy).then_inc(xT_hi_done, 1)

            def take_silu(b, n, q):
                act.wait_ge(pair_done, q + 1)
                if n >= 2 + SC:
                    act.wait_ge(mlp_act_done, b * IC + (n - 2 - SC + 1))
                elif n >= 2:
                    act.wait_ge(sh_act_done, b * SC + (n - 2 + 1))
                src, dst = pair[n % 3][:, 0, :], silu_b[:, n % 2, :]
                if n == 1:
                    src, dst = pair[1][GATES : GATES + IR, 0, :], silu_b[0:IR, 1, :]
                act.activation(dst, src, ACT.Silu).then_inc(silu_done, 1)

            def silu_final(f):
                act.wait_ge(summed, f + 1)
                rows = got[1][:, bass.ds(f * BT, BT), :]
                act.activation(rows, rows, ACT.Silu).then_inc(silu_f_done, 1)

            def take_shared(b):
                act.wait_ge(sh_out_done, b + 1)
                if isinstance(b, int) and b == 0:
                    act.wait_ge(up_lo_done, E)
                act.activation(shared[:, bass.ds(b * BT, BT), :].rearrange("p t d -> p (t d)"), bytok[:, :],
                               ACT.Copy).then_inc(shared_done, 1)

            def run_block(b, ahead=2, first=0):
                q = b * PAIRS + 3
                mid_squares(b)
                block_x_hi(b)
                if ahead:
                    rec_decay(b + 1, q)
                if ahead:
                    rec_x_in(q)
                if first:
                    experts_gap()
                mid_root(b)
                if ahead:
                    rec_root(b + 1)
                for n in range(SC):
                    take_silu(b, n, q + 3 * min(ahead, 1) + n)
                    if n == 0:
                        act.wait_ge(h2T_done, b + 1)
                        act.activation(h2_hi[:, :], turned[:, :], ACT.Copy).then_inc(h2_hi_done, 1)
                        if ahead:
                            rec_gate(q)
                if not ahead:
                    take_shared(b)
                    silu_final(NB - 3)
                    silu_final(NB - 2)
                for n in range(SC, SC + IC):
                    take_silu(b, n, q + 3 * min(ahead, 1) + n)
                    if n == SC + 1:
                        if ahead:
                            take_shared(b)
                        if ahead > 1:
                            h_hi(b + 2)

            act.wait_ge(ap_half_done, 1)
            rec_decay(0, 0)
            act.wait_ge(up_loaded, 32)
            for b in range(2, NB):
                if b > 3:
                    take_x(b)
                if b == 3:
                    rec_x_in(0)
                if b < 6:
                    up_weight_hi(b - 2)
                if b == 6:
                    rec_root(0)
            act.wait_ge(wT_done, 4)
            take(wout_t[:, :, :], pair[0][:, 0, 0:REC], 0.5).then_inc(wT_taken, 1)
            for e in range(4, E):
                up_weight_hi(e)
            rec_gate(0)
            h_hi(1)
            take(wdown_t[:, :, :], pair[0][:, 1, :]).then_inc(wT_taken, 1)
            act.wait_ge(wT_done, 6)
            take(scaled[:, NREC : NREC + IC, :], pair[1][:, 0, :], ln2[:, 0:1]).then_inc(scaled_done, 1)
            take(scaled[:, NREC + IC :, :], pair[1][:, 1, :], ln2[:, 0:1]).then_inc(scaled_done, 1)
            act.wait_ge(shared_loaded, 16 * 6)
            act.activation(sh_hi[:, :], raw_shared[:, :], ACT.Copy).then_inc(shared_split, 1)

            act.wait_ge(scaled_done, 2)
            weight_hi(2)
            weight_hi(3)

            def experts_gap():
                act.wait_ge(gap_done, 1)
                act.activation(egap[:, :], gap[:, :], ACT.Exp).then_inc(egap_done, 1)

            run_block(0, first=1)
            with act.Fori(1, HALF) as b:
                run_block(b)

            def e_hi(i, j):
                act.wait_ge(eT_done, i * 4 + (j + 1))
                act.activation(xe_hi[:, j % 2, :], turned[:, 0:P], ACT.Copy).then_inc(e_hi_done, 1)

            def e_silu(i, j):
                act.wait_ge(e_up_done, i * 4 + (j + 1))
                if not (isinstance(i, int) and i * 4 + j < 2):
                    act.wait_ge(e_act_done, i * 4 + j)
                act.activation(silu_e[:, j % 2, :], pair[j % 2][:, 0, 0:I], ACT.Silu).then_inc(e_silu_done, 1)

            def e_copy(i, j):
                act.wait_ge(e_actT_done, i * 4 + (j + 1))
                act.activation(actT[:, j % 2, :], pair[2][:, 0, 0 : EC * P], ACT.Copy).then_inc(e_copy_done, 1)

            e_hi(0, 0)
            e_hi(0, 1)
            act.wait_ge(y_done, HALF + 1)
            e_silu(0, 0)
            e_hi(0, 2)
            e_silu(0, 1)
            e_copy(0, 0)

            def e_step(i, j):
                e_hi(i, j + 2)
                e_silu(i, j + 1)
                e_copy(i, j)

            for j in range(1, 4):
                e_step(0, j)
            with act.Fori(1, (TILES - 3) // 4) as i:
                for j in range(4):
                    e_step(i, j)
            for t in range(TILES - 3, TILES):
                if t + 2 < TILES:
                    e_hi(0, t + 2)
                if t + 1 < TILES:
                    e_silu(0, t + 1)
                e_copy(0, t)

            run_block(HALF)
            silu_final(0)
            run_block(HALF + 1)
            silu_final(1)
            silu_final(2)
            run_block(NB - 2, ahead=1)
            silu_final(3)
            silu_final(4)
            run_block(NB - 1, ahead=0)
            silu_final(NB - 1)

        @block.vector
        def _(dve):
            def flat(ap):
                return ap.rearrange("p a b -> p (a b)")

            def each(ap):
                return ap.unsqueeze(2).to_broadcast([P, NT, E])

            dve.memset(tiny[:, 0:1], 1e-5).then_inc(tiny_ready, 1)
            dve.memset(tiny[:, 1:2], 1e-6).then_inc(tiny_ready, 1)
            dve.memset(tiny[:, 2:3], 1e-8).then_inc(tiny_ready, 1)
            def statistics(n):
                dve.wait_ge(x_loaded[n], 16)
                for t in range(n * QT, (n + 1) * QT):
                    dve.bn_stats(st6[:, t, :], x_sb[:, t, :]).then_inc(stats_step, 1)
                dve.wait_ge(stats_step, (n + 1) * QT)
                for t in range(n * QT, (n + 1) * QT):
                    last = dve.bn_aggr(mv[:, t, :], st6[:, t, :])
                last.then_inc(stats_done, 1)

            def scales(n):
                some = slice(n * QT, (n + 1) * QT)
                dve.wait_ge(std_done, n + 1)
                dve.reciprocal(rstd[:, some], std[:, some]).then_inc(rstd_done, 1)
                dve.wait_ge(rstd_done, 2 * n + 1)
                dve.tensor_tensor(msq[:, some], mv[:, some, 1], rstd[:, some], ALU.mult).then_inc(rstd_done, 1)
                dve.wait_ge(rstd_done, 2 * n + 2)
                dve.tensor_tensor(msq[:, some], msq[:, some], rstd[:, some], ALU.mult).then_inc(msq_done, 1)

            def h_scales(n):
                some = slice(n * QT, (n + 1) * QT)
                dve.wait_ge(rms1_done, n + 1)
                dve.reciprocal(r1[:, some], rms1[:, some]).then_inc(r1_done, 1)

            def normalise(b):
                for t in range(b * BT, (b + 1) * BT):
                    last = dve.tensor_scalar(xn[:, t, :], x_sb[:, t, :], mv[:, t, 0:1], rstd[:, t : t + 1],
                                             ALU.subtract, ALU.mult)
                last.then_inc(xn_done, 1)

            def x_lo(b):
                dve.wait_ge(xT_hi_done, b + 1)
                dve.tensor_tensor(part_lo[:, :], turned[:, :], part_hi[:, :].bitcast(F32), ALU.subtract).then_inc(
                    xT_lo_done, 1
                )

            def make_h(b):
                for k in range(BT):
                    t = b * BT + k
                    last = dve.tensor_scalar(h_tok[:, k, :], xn[:, t, :], r1[:, bass.ds(t, 1)], None, ALU.mult)
                last.then_inc(h_done, 1)

            def h_lo(b):
                dve.wait_ge(hT_hi_done, b + 1)
                dve.tensor_tensor(hT_lo[:, :], turned[:, :], hT_hi[:, :].bitcast(F32), ALU.subtract).then_inc(
                    hT_lo_done, 1
                )

            def make_decay(b):
                dve.wait_ge(t_decay_done, b + 1)
                dve.tensor_scalar(decay[:, :, :], t_decay[:, :, :], 0.5, 0.5, ALU.mult, ALU.add).then_inc(decay_done, 1)

            def make_square(b):
                dve.wait_ge(decay_done, b + 1)
                dve.tensor_tensor(square[:, :, :], decay[:, :, :], decay[:, :, :], ALU.mult).then_inc(square_done, 1)

            def make_rest(b):
                dve.wait_ge(square_done, b + 1)
                dve.tensor_scalar(rest[:, :, :], square[:, :, :], -1.0, 1.0, ALU.mult, ALU.add).then_inc(rest_done, 1)

            def make_feed(b):
                dve.wait_ge(x_in_done, b + 1)
                dve.wait_ge(root_done, b + 1)
                dve.tensor_tensor(feed[:, :, :], root[:, :, :], x_in[:, :, :], ALU.mult).then_inc(feed_done, 1)

            def scan(b):
                dve.wait_ge(feed_done, b + 1)
                dve.wait_ge(carry_done, b + 1)
                for c in range(RC):
                    dve.tensor_tensor_scan(state[:, c, :], decay[:, c, :], feed[:, c, :], carry[:, c : c + 1],
                                           ALU.mult, ALU.add).then_inc(scan_done, 1)

            def make_y(b):
                dve.wait_ge(t_gate_done, b + 1)
                dve.wait_ge(scan_done, b * RC + RC)
                dve.tensor_scalar(carry[:, :], state[:, :, BLK - 1], keep[:, bass.ds(b + 1, 1)], None,
                                  ALU.mult).then_inc(carry_done, 1)
                dve.scalar_tensor_tensor(out=flat(y[:, :, :]), in0=flat(t_gate[:, :, :]), scalar=1.0,
                                         in1=flat(state[:, :, :]), op0=ALU.add, op1=ALU.mult).then_inc(y_done, 1)

            def tokens(ap, b):
                return ap[:, bass.ds(b * BT, BT), :].rearrange("p t d -> p (t d)")

            def middle(b):
                dve.wait_ge(proj_done, b + 1)
                dve.tensor_tensor(tokens(s_tok, b), bytok[:, :], tokens(xn, b), ALU.add).then_inc(mid_done, 1)

            def make_h2(b):
                dve.wait_ge(rms2_done, b + 1)
                dve.reciprocal(r2[:, :], rms2[:, :]).then_inc(r2_done, 1)
                dve.wait_ge(r2_done, b + 1)
                for k in range(BT):
                    last = dve.tensor_scalar(h2_tok[:, k, :], s_tok[:, b * BT + k, :], r2[:, k : k + 1], None, ALU.mult)
                last.then_inc(h2_done, 1)

            def make_h2_lo(b):
                dve.wait_ge(h2_hi_done, b + 1)
                dve.tensor_tensor(h2_lo[:, :], turned[:, :], h2_hi[:, :].bitcast(F32), ALU.subtract).then_inc(
                    h2_lo_done, 1
                )

            def shared_act(b, c):
                dve.wait_ge(silu_done, b * (SC + IC) + (c + 1))
                rows = (P, IR)[c]
                dve.tensor_tensor(sh_act[0:rows, c, :], silu_b[0:rows, c, :], pair[c][0:rows, 1 - c, :],
                                  ALU.mult).then_inc(sh_act_done, 1)

            def mlp_product(b, j):
                n = SC + j
                dve.wait_ge(silu_done, b * (SC + IC) + (n + 1))
                dve.tensor_tensor(mlp_act[:, j, :], silu_b[:, n % 2, :], pair[n % 3][:, 1, :], ALU.mult).then_inc(
                    mlp_act_done, 1
                )

            def make_s(b):
                dve.wait_ge(mlp_out_done, b + 1)
                dve.tensor_tensor(tokens(s_tok, b), bytok[:, :], tokens(s_tok, b), ALU.add).then_inc(s_done, 1)

            step = [0]

            def done(ins):
                step[0] += 1
                ins.then_inc(route_step, 1)
                dve.wait_ge(route_step, step[0])

            def best_of(values, top, one_hot):
                done(dve.tensor_reduce(top, values, AX.X, ALU.max))
                done(dve.tensor_tensor(scratch[:, :, :], values, each(top), ALU.is_equal))
                done(dve.tensor_tensor(scratch[:, :, :], scratch[:, :, :], rank_of[:, :, :], ALU.mult))
                done(dve.tensor_reduce(best[:, :], scratch[:, :, :], AX.X, ALU.max))
                done(dve.tensor_tensor(one_hot, scratch[:, :, :], each(best[:, :]), ALU.is_equal))

            def take_logits():
                dve.wait_ge(logits_done, NB)
                dve.tensor_copy(flat(logit[:, :, :]), pair[2][:, 1, 0 : NT * E]).then_inc(logits_taken, 1)

            def choose_first():
                dve.wait_ge(consts_ready, 6)
                dve.wait_ge(logits_taken, 1)
                best_of(logit[:, :, :], m1[:, :], first[:, :, :])
                done(dve.scalar_tensor_tensor(out=logit[:, :, :], in0=first[:, :, :], scalar=-BIG, in1=logit[:, :, :],
                                              op0=ALU.mult, op1=ALU.add))

            def choose_second():
                best_of(logit[:, :, :], m2[:, :], second[:, :, :])
                dve.tensor_tensor(chosen[:, :, :].rearrange("p e t -> p t e"), first[:, :, :], second[:, :, :],
                                  ALU.add).then_inc(chosen_done, 1)
                dve.tensor_tensor(gap[:, :], m2[:, :], m1[:, :], ALU.subtract).then_inc(gap_done, 1)

            def shares():
                dve.wait_ge(egap_done, 1)
                done(dve.tensor_scalar(esum[:, :], egap[:, :], 1.0, None, ALU.add))
                done(dve.reciprocal(p1[:, :], esum[:, :]))
                done(dve.tensor_tensor(p2[:, :], egap[:, :], p1[:, :], ALU.mult))

            def place():
                dve.wait_ge(ranks_done, 1)
                done(dve.tensor_copy(flat(ranked[:, :, :]), turned[:, :]))
                dve.engine_nop().then_inc(ranks_taken, 1)
                done(dve.tensor_reduce(total[:, :], count[:, :, :], AX.X, ALU.add))
                done(dve.tensor_scalar(total_i[:, :], total[:, :], float(P - 1), None, ALU.add))
                done(dve.tensor_scalar(tiles_i[:, :], total_i[:, :], 7, None, ALU.logical_shift_right))
                done(dve.tensor_copy(tiles[:, :], tiles_i[:, :]))
                done(dve.tensor_tensor_scan(tiles_to[:, :], ones[:, 0:E], tiles[:, :], 0.0, ALU.mult, ALU.add))
                done(dve.tensor_tensor(tiles_from[:, :], tiles_to[:, :], tiles[:, :], ALU.subtract))
                done(dve.tensor_scalar(steps[:, :, 0], tiles_from[:, :], float(P), None, ALU.mult))
                done(dve.tensor_copy(steps[:, :, 1:], count[:, :, 0 : NT - 1]))
                done(dve.tensor_tensor_scan(flat(offset[:, :, :]), flat(restart[:, :, :]), flat(steps[:, :, :]), 0.0,
                                            ALU.mult, ALU.add))

            def find_slots():
                done(dve.tensor_tensor(slot[:, :, :], offset[:, :, :], ranks[:, :, :], ALU.add))
                for c, one_hot in enumerate((first, second)):
                    done(dve.tensor_tensor(scratch[:, :, :], one_hot[:, :, :],
                                           slot[:, :, :].rearrange("p e t -> p t e"), ALU.mult))
                    done(dve.tensor_reduce(slot_f[:, c, :], scratch[:, :, :], AX.X, ALU.add))
                dve.tensor_copy(slot_i[:, :, :], slot_f[:, :, :]).then_inc(slots_known, 1)

            def find_experts():
                done(dve.tensor_tensor(passed[:, :, :], tile_no[:, :, :],
                                       tiles_to[:, :].unsqueeze(1).to_broadcast([P, TILES, E]), ALU.is_ge))
                done(dve.tensor_reduce(expert_f[:, :], passed[:, :, :], AX.X, ALU.add))
                dve.tensor_scalar(expert_i[:, :], expert_f[:, :], float(E - 1), None, ALU.min).then_inc(
                    experts_known, 1
                )
                shares()

            def add_experts(f):
                dve.wait_ge(gathered[f], 16 * 2 * BT)
                dve.wait_ge(shared_done, f + 1)
                for t in range(BT):
                    at = bass.ds(f * BT + t, 1)
                    dve.scalar_tensor_tensor(out=got[0][:, at, :], in0=got[0][:, at, :], scalar=p1[:, at],
                                             in1=shared[:, at, :], op0=ALU.mult, op1=ALU.add).then_inc(half_done, 1)
                for t in range(BT):
                    at = bass.ds(f * BT + t, 1)
                    dve.wait_ge(half_done, f * BT + (t + 1))
                    last = dve.scalar_tensor_tensor(out=got[1][:, at, :], in0=got[1][:, at, :], scalar=p2[:, at],
                                                    in1=got[0][:, at, :], op0=ALU.mult, op1=ALU.add)
                last.then_inc(summed, 1)

            def run_block(b, ahead=2, before=1, steps=None, early_sums=(), late_sums=(), state_free=None):
                dve.tensor_copy(h_tok[:, :, :], xn[:, bass.ds(b * BT, BT), :]).then_inc(x_tok_done, 1)
                if steps:
                    steps[0]()
                middle(b)
                if steps:
                    steps[1]()
                for f in early_sums:
                    add_experts(f)
                x_lo(b)
                if ahead:
                    make_decay(b + 1)
                    make_square(b + 1)
                if ahead:
                    make_rest(b + 1)
                make_h2(b)
                if steps:
                    steps[2]()
                if ahead:
                    make_feed(b + 1)
                shared_act(b, 0)
                make_h2_lo(b)
                if state_free:
                    state_free()
                if ahead:
                    scan(b + 1)
                shared_act(b, 1)
                if before:
                    make_s(b - 1)
                if ahead > 1:
                    make_h(b + 2)
                for f in late_sums:
                    add_experts(f)
                if steps:
                    steps[3]()
                mlp_product(b, 0)
                if ahead:
                    make_y(b + 1)
                mlp_product(b, 1)
                if ahead > 1:
                    h_lo(b + 2)
                for j in range(2, IC):
                    mlp_product(b, j)

            dve.memset(carry[:, :], 0.0).then_inc(carry_done, 1)
            dve.engine_nop().then_inc(s_done, 1)
            dve.engine_nop().then_inc(e_out_done, 3)
            dve.engine_nop().then_inc(e_act_done, 1)
            dve.engine_nop().then_inc(e_copy_done, 2)
            statistics(0)
            statistics(1)
            scales(0)
            normalise(0)
            h_scales(0)
            dve.wait_ge(r1_done, 1)
            dve.wait_ge(xn_done, 1)
            make_h(0)
            normalise(1)
            statistics(2)
            h_lo(0)
            scales(1)
            normalise(2)
            normalise(3)
            statistics(3)
            scales(2)
            normalise(4)
            normalise(5)
            scales(3)
            dve.wait_ge(small_loaded, 16 * (3 + RC))
            dve.tensor_scalar(ap_half[:, :], ap_sb[:, :], 0.5, None, ALU.mult).then_inc(ap_half_done, 1)
            for n in range(1, 4):
                h_scales(n)
            normalise(6)
            make_decay(0)
            make_square(0)
            normalise(7)
            make_h(1)
            make_rest(0)
            make_feed(0)
            scan(0)
            take_logits()
            choose_first()
            make_y(0)
            h_lo(1)
            run_block(0, before=0, steps=[choose_second, place, find_slots, find_experts])
            with dve.Fori(1, HALF) as b:
                run_block(b)

            def e_lo(i, j):
                dve.wait_ge(e_hi_done, i * 4 + (j + 1))
                dve.tensor_tensor(xe_lo[:, j % 2, :], turned[:, 0:P], xe_hi[:, j % 2, :].bitcast(F32),
                                  ALU.subtract).then_inc(e_lo_done, 1)

            def e_act(i, j):
                dve.wait_ge(e_silu_done, i * 4 + (j + 1))
                if not (isinstance(i, int) and i * 4 + j < 2):
                    dve.wait_ge(e_actT_done, i * 4 + (j - 1))
                dve.tensor_tensor(act_e[:, j % 2, 0:I], silu_e[:, j % 2, :], pair[j % 2][:, 1, 0:I],
                                  ALU.mult).then_inc(e_act_done, 1)

            def e_out(i, j):
                dve.wait_ge(e_down_done, i * 4 + (j + 1))
                if not (isinstance(i, int) and i * 4 + j < 4):
                    dve.wait_ge(tile_stored[j % 4], i * 16 + (j // 4) * 16)
                dve.tensor_copy(y_tile[:, j % 4, :], pair[2][:, 1, 0:P]).then_inc(e_out_done, 1)

            e_lo(0, 0)
            e_lo(0, 1)
            e_act(0, 0)
            e_lo(0, 2)
            e_act(0, 1)

            def e_step(i, j):
                e_lo(i, j + 2)
                e_act(i, j + 1)
                e_out(i, j - 1)

            for j in range(1, 4):
                e_step(0, j)
            for j in range(4):
                e_step(1, j)
            with dve.Fori(2, (TILES - 3) // 4) as i:
                for j in range(4):
                    e_step(i, j)
            for t in range(TILES - 3, TILES):
                if t + 2 < TILES:
                    e_lo(0, t + 2)
                if t + 1 < TILES:
                    e_act(0, t + 1)
                e_out(0, t - 1)
            e_out(0, TILES - 1)

            def finish_last(f):
                rows = slice(f * BT, (f + 1) * BT)
                dve.wait_ge(silu_f_done, f + 1)
                dve.wait_ge(s_done, f + 2)
                dve.tensor_tensor(got[0][:, rows, :], got[1][:, rows, :], s_tok[:, rows, :], ALU.mult).then_inc(
                    last_product_done, 1
                )
                dve.wait_ge(last_product_done, f - (NB - 3))
                dve.wait_ge(x_again, 16)
                dve.tensor_tensor(got[0][:, rows, :], got[0][:, rows, :], x_back[:, rows, :], ALU.add).then_inc(
                    last_gated_done, 1
                )

            def tiles_stored():
                for k in range(4):
                    dve.wait_ge(tile_stored[k], 16 * -(-(TILES - k) // 4))

            run_block(HALF, late_sums=[0], state_free=tiles_stored)
            run_block(HALF + 1, early_sums=[1], late_sums=[2])
            run_block(NB - 2, ahead=1, early_sums=[3], late_sums=[4])
            run_block(NB - 1, ahead=0, early_sums=[5], late_sums=[6, 7])
            finish_last(NB - 2)
            make_s(NB - 1)
            finish_last(NB - 1)

    return nc


_INS = [
    "L0_attn_x", "L0_attn_ln1_w", "L0_attn_ln2_w", "L0_attn_w_in", "L0_attn_w_gate", "L0_attn_a_param", "L0_attn_w_a",
    "L0_attn_w_out", "L0_attn_w_mlp_gate", "L0_attn_w_mlp_up", "L0_attn_w_mlp_down", "L0_ffn_gate_w", "L0_ffn_Wg",
    "L0_ffn_Wu", "L0_ffn_Wd", "L0_ffn_Sg", "L0_ffn_Su", "L0_ffn_Sd",
]
_OUTS = [((4, 1024, 128), "float32")]


def kernel(**inputs):
    import numpy as _np
    import concourse.bacc as _bacc
    from concourse import mybir as _mybir
    from concourse.bass_utils import run_bass_kernel_spmd as _run

    nc = _bacc.Bacc("TRN2", target_bir_lowering=False, num_devices=1)
    arrays, args = {}, []
    for name in _INS:
        a = _np.ascontiguousarray(inputs[name])
        arrays[f"in_{name}_dram"] = a
        args.append(nc.dram_tensor(f"in_{name}_dram", a.shape, _mybir.dt.from_np(a.dtype), kind="ExternalInput").ap())
    for i, (shape, dtype) in enumerate(_OUTS):
        dt = _mybir.dt.from_np(_np.dtype(dtype))
        args.append(nc.dram_tensor(f"out_{i}_dram", shape, dt, kind="ExternalOutput").ap())
    gated_recurrent_moe_kernel(nc, *args)
    r = _run(nc, [arrays], core_ids=[0])
    got = tuple(r.results[0][f"out_{i}_dram"] for i in range(len(_OUTS)))
    return got[0]
```
